# Optimizing a Trainium2 kernel written in Bass

```python
import numpy as np
import jax
import jax.numpy as jnp

def _softmax(x, axis=-1):
    return jax.nn.softmax(x, axis=axis)

def _gelu(x):
    return jax.nn.gelu(x, approximate=True)

def _silu(x):
    return jax.nn.silu(x)

def _sigmoid(x):
    return jax.nn.sigmoid(x)

def _layernorm(x, axis=-1, eps=1e-05):
    m = jnp.mean(x, axis=axis, keepdims=True)
    v = jnp.var(x, axis=axis, keepdims=True)
    return (x - m) / jnp.sqrt(v + eps)

def _scatter_add(tgt, idx, src, axis=0):
    return tgt.at[idx].add(src)

def _segment_sum(src, seg, n):
    return jax.ops.segment_sum(src, seg, n)
kernel_name = 'mk_gnn_preln_d2_gnn_r64_61bb0b'

def setup_inputs(seed: int=0):
    np.random.seed(seed)
    _w = jnp.asarray

    def _rec_inputs():
        import jax
        import jax.numpy as jnp
        _gk = jax.random.key(seed)
        x = -7.329e-05 + 0.9999 * jax.random.normal(jax.random.fold_in(_gk, 1), (10000, 512), jnp.float32)
        _s = jax.random.randint(jax.random.fold_in(_gk, 2), (2500,), 0, 10000, jnp.int32)
        _d = jax.random.randint(jax.random.fold_in(_gk, 3), (2500,), 0, 10000, jnp.int32)
        _loop = jnp.arange(10000, dtype=jnp.int32)
        src = jnp.concatenate([_s, _d, _loop])
        dst = jnp.concatenate([_d, _s, _loop])
        _o = jnp.argsort(dst, stable=True)
        src = src[_o]
        dst = dst[_o]
        return (x, src, dst)
    x, src, dst = _rec_inputs()

    def _L0_gnn_setup():
        import jax, jax.numpy as jnp
        import numpy as np
        N_NODES = 100000
        N_EDGES = 12800
        D = 512
        L = 3
        LN_EPS = 1e-05
        key = jax.random.key(seed)
        ks = jax.random.split(key, 8)
        x = jax.random.normal(ks[0], (N_NODES, D), dtype=jnp.float32)
        edge_index = jax.random.randint(ks[1], (2, N_EDGES), 0, N_NODES, dtype=jnp.int32)
        scale = 1.0 / np.sqrt(D)
        W_l = jax.random.normal(ks[2], (L, D, D), dtype=jnp.float32) * scale
        W_r = jax.random.normal(ks[3], (L, D, D), dtype=jnp.float32) * scale
        b = jax.random.normal(ks[4], (L, D), dtype=jnp.float32) * 0.01
        ln_g = jnp.ones((L, D), dtype=jnp.float32)
        ln_b = jnp.zeros((L, D), dtype=jnp.float32)
        return {'x': x, 'edge_index': edge_index, 'W_l': W_l, 'W_r': W_r, 'b': b, 'ln_g': ln_g, 'ln_b': ln_b}
    _L0_gnn_all = _L0_gnn_setup()
    _L0_gnn_in = {k: v for k, v in _L0_gnn_all.items() if k in ('W_l', 'W_r', 'b', 'ln_g', 'ln_b')}
    del _L0_gnn_all

    def _L1_gnn_setup():
        import jax, jax.numpy as jnp
        import numpy as np
        N_NODES = 20000
        N_EDGES = 5000
        D = 512
        L = 3
        key = jax.random.key(seed)
        ks = jax.random.split(key, 6)
        x = jax.random.normal(ks[0], (N_NODES, D), dtype=jnp.float32)
        Ws_self = jax.random.normal(ks[1], (L, D, D), dtype=jnp.float32) * 0.05
        Ws_neigh = jax.random.normal(ks[2], (L, D, D), dtype=jnp.float32) * 0.05
        bs = jax.random.normal(ks[3], (L, D), dtype=jnp.float32) * 0.05
        src = jax.random.randint(ks[4], (N_EDGES,), 0, N_NODES, dtype=jnp.int64)
        dst = jax.random.randint(ks[5], (N_EDGES,), 0, N_NODES, dtype=jnp.int64)
        return {'x': x, 'Ws_self': Ws_self, 'Ws_neigh': Ws_neigh, 'bs': bs, 'src': src, 'dst': dst}
    _L1_gnn_all = _L1_gnn_setup()
    _L1_gnn_in = {k: v for k, v in _L1_gnn_all.items() if k in ('Ws_self', 'Ws_neigh', 'bs')}
    del _L1_gnn_all
    return {'x': x, 'src': src, 'dst': dst, 'L0_gnn_W_l': _L0_gnn_in['W_l'], 'L0_gnn_W_r': _L0_gnn_in['W_r'], 'L0_gnn_b': _L0_gnn_in['b'], 'L0_gnn_ln_g': _L0_gnn_in['ln_g'], 'L0_gnn_ln_b': _L0_gnn_in['ln_b'], 'L1_gnn_Ws_self': _L1_gnn_in['Ws_self'], 'L1_gnn_Ws_neigh': _L1_gnn_in['Ws_neigh'], 'L1_gnn_bs': _L1_gnn_in['bs']}

def reference(x, src, dst, L0_gnn_W_l, L0_gnn_W_r, L0_gnn_b, L0_gnn_ln_g, L0_gnn_ln_b, L1_gnn_Ws_self, L1_gnn_Ws_neigh, L1_gnn_bs):
    import jax
    import jax.numpy as jnp

    def _L0_gnn_ref(x, edge_index, W_l, W_r, b, ln_g, ln_b):
        import jax, jax.numpy as jnp
        import numpy as np
        N_NODES = 100000
        N_EDGES = 12800
        D = 512
        L = 3
        LN_EPS = 1e-05
        src = edge_index[0]
        tgt = edge_index[1]
        n = x.shape[0]
        cnt = jax.ops.segment_sum(jnp.ones((src.shape[0],), x.dtype), tgt, num_segments=n)
        inv_cnt = (1.0 / jnp.maximum(cnt, 1.0))[:, None]
        for i in range(W_l.shape[0]):
            x_in = x
            agg = jax.ops.segment_sum(x[src], tgt, num_segments=n) * inv_cnt
            h = agg @ W_l[i].T + x @ W_r[i].T + b[i]
            mu = jnp.mean(h, axis=-1, keepdims=True)
            var = jnp.mean(jnp.square(h - mu), axis=-1, keepdims=True)
            h = (h - mu) * jax.lax.rsqrt(var + LN_EPS) * ln_g[i] + ln_b[i]
            h = jax.nn.relu(h)
            x = h + x_in
        return x

    def _L1_gnn_ref(x, Ws_self, Ws_neigh, bs, src, dst):
        import jax, jax.numpy as jnp
        import numpy as np
        N_NODES = 20000
        N_EDGES = 5000
        D = 512
        L = 3
        n = x.shape[0]
        deg = jax.ops.segment_sum(jnp.ones_like(dst, dtype=x.dtype), dst, num_segments=n)
        inv_deg = (1.0 / jnp.clip(deg, 1.0))[:, None]
        h = x
        n_layers = Ws_self.shape[0]
        for l in range(n_layers):
            neigh = jax.ops.segment_sum(h[src], dst, num_segments=n) * inv_deg
            h = h @ Ws_self[l] + neigh @ Ws_neigh[l] + bs[l]
            if l != n_layers - 1:
                h = jax.nn.relu(h)
        return h
    edge_index = jnp.stack([src, dst])
    h = jnp.maximum(_layernorm(x, axis=-1), 0.0)
    x = x + _L0_gnn_ref(h, edge_index, L0_gnn_W_l, L0_gnn_W_r, L0_gnn_b, L0_gnn_ln_g, L0_gnn_ln_b)
    h = jnp.maximum(_layernorm(x, axis=-1), 0.0)
    x = x + _L1_gnn_ref(h, L1_gnn_Ws_self, L1_gnn_Ws_neigh, L1_gnn_bs, src, dst)
    return x

_drawn_inputs = setup_inputs


def setup_inputs(seed=0):
    import zlib

    import numpy as np

    out = dict(_drawn_inputs(seed))
    spreads = {'L0_gnn_ln_g': (1.0, 0.2), 'L0_gnn_ln_b': (0.0, 0.1)}
    factors = {'L0_gnn_b': 8.0}
    for name, (base, spread) in spreads.items():
        noise = np.random.default_rng([zlib.crc32(name.encode()), seed]).standard_normal(out[name].shape)
        drawn = base * np.exp(spread * noise) if base else spread * noise
        out[name] = jnp.asarray(drawn.astype(out[name].dtype))
    for name, factor in factors.items():
        out[name] = (out[name] * factor).astype(out[name].dtype)
    return out
```

```python
import concourse.bass as bass
from concourse import mybir
from contextlib import ExitStack

F32 = mybir.dt.float32
F32R = mybir.dt.float32r
BF16 = mybir.dt.bfloat16
I32 = mybir.dt.int32
ALU = mybir.AluOpType
ACT = mybir.ActivationFunctionType
AX = mybir.AxisListType
ds = bass.ds

P = 128
LN_EPS = 1e-5


def build_gnn(nc, x, src, dst, W_l, W_r, b0, ln_g, ln_b, Ws_self, Ws_neigh, b1, out):
    N, D = x.shape
    E = src.shape[0]
    KC = D // P
    LA, LB = W_l.shape[0], Ws_self.shape[0]
    L = LA + LB
    QUAD = 4
    NQ = -(-N // (QUAD * P))
    NT = NQ * QUAD
    NP = NT * P
    EP = max(p for p in range(1, P + 1) if E % p == 0)
    EC = E // EP
    CB = max(b for b in range(1, 13) if EC % b == 0)
    CC = max(b for b in range(1, 5) if EC % b == 0)
    LG = 4
    EK = -(-E // (P * LG)) * LG
    UNIT = 2 * P
    CH = 2 * (NT + E // UNIT + 1)

    node_tab = nc.dram_tensor("node_tab", (NP, 2), F32, kind="Internal").ap()
    H = [nc.dram_tensor(f"h{l}", (NP, D), F32, kind="Internal").ap() for l in range(L)]
    h_first_net = nc.dram_tensor("h_first_net", (NP, D), F32, kind="Internal").ap()
    x1_dram = nc.dram_tensor("x1", (NP, D), F32, kind="Internal").ap()
    wp = [nc.dram_tensor(f"wp{l}", (P, 4, KC * D), F32, kind="Internal").ap() for l in range(L)]

    ctx = ExitStack()
    with ctx:
        def sb(name, shape, dt):
            return ctx.enter_context(nc.sbuf_tensor(name, shape, dt))

        def sem(name):
            return ctx.enter_context(nc.semaphore(name))

        banks = [ctx.enter_context(nc.psum_tensor(f"bank{i}", [P, 512], F32)) for i in range(8)]

        diff_i = sb("diff_i", [P, P], I32)
        iota_i = sb("iota_i", [P, CH], I32)
        slot_i = sb("slot_i", [P, P], I32)
        nid_i = sb("nid_i", [P, P], I32)
        diff = sb("diff", [P, P], F32)
        iota = sb("iota", [P, CH], F32)
        slot = sb("slot", [P, P], F32)
        nid = sb("nid", [P, P], F32)
        iota_b = sb("iota_b", [P, P], BF16)
        ident = sb("ident", [P, P], F32)
        below = sb("below", [P, P], F32)
        ones = sb("ones", [P, P], F32)
        zeros = sb("zeros", [P, CH], F32)
        eps = sb("eps", [P, 1], F32)

        bias = sb("bias", [P, L, D], F32)
        gain = sb("gain", [P, LA, D], F32)
        shift = sb("shift", [P, LA, D], F32)
        bsum = sb("bsum", [P, LA], F32)

        G = sb("G", [P, QUAD, 2, KC, P], F32)
        wraw = G[:, :, :, :, :].rearrange("p (a b) c d k -> p a (b c d k)", a=2) \
            .rearrange("p a (c n) -> p a c n", c=KC)
        wtmp = sb("wtmp", [P, 2, D], F32)
        wsum = sb("wsum", [P, 2], F32)
        wneg = sb("wneg", [P, 2], F32)
        wcen = sb("wcen", [P, 2, D], F32)
        W = sb("W", [P, 4, KC, D], F32R)

        src_i = sb("src_i", [EP, EC], I32)
        dst_i = sb("dst_i", [EP, EC], I32)
        dhi_i = sb("dhi_i", [EP, EC], I32)
        dlo_i = sb("dlo_i", [EP, EC], I32)
        e_f = sb("e_f", [EP, 8, EC], F32)
        dhi_b = sb("dhi_b", [EP, EC], BF16)
        dlo_b = sb("dlo_b", [EP, EC], BF16)
        self_b = sb("self_b", [EP, EC], BF16)
        oh_hi = sb("oh_hi", [EP, CB, NT], BF16)
        oh_lo = sb("oh_lo", [EP, CB, 2, P], BF16)
        nd = sb("nd", [NT, 12, P], F32)
        ntab = sb("ntab", [NT, P, 2], F32)
        nsm = sb("nsm", [P, 16], F32)
        qa_t = sb("qa_t", [P, 2, NT], F32)
        qt_i = sb("qt_i", [P, 3, NT], I32)
        qt_f = sb("qt_f", [P, 2, NT], F32)
        perm_oh = sb("perm_oh", [P, QUAD, P + 2 * NT], F32)
        pos_node_i = sb("pos_node_i", [P, NT], I32)
        pos_read_i = sb("pos_read_i", [P, NT], I32)
        pos_f = sb("pos_f", [P, 2, NT], F32)
        own = sb("own", [P, NT], F32)
        comp_oh = sb("comp_oh", [EP, CC, P + 2 * EK], F32)
        ce_i = sb("ce_i", [P, 2, EK], I32)
        ctab = sb("ctab", [P, EK, 4], F32)
        c_i = sb("c_i", [P, 4, EK], I32)
        c_f = sb("c_f", [P, 8, EK], F32)
        cnt_pb = sb("cnt_pb", [P, NT], F32)
        ub = sb("ub", [P, 6, NT], F32)
        ub_i = sb("ub_i", [P, 2, NT], I32)
        buck_oh = sb("buck_oh", [P, P + 3 * CH], F32)
        buck_eq = sb("buck_eq", [P, CH], F32)
        edge_row = sb("edge_row", [P, CH], I32)
        edge_dw = sb("edge_dw", [P, CH, 2], F32)
        scal_i = sb("scal_i", [1, 8], I32)
        unit_i = sb("unit_i", [1, 3, NT], I32)
        small_i = sb("small_i", [P, 2], I32)
        stage_c = sb("stage_c", [P, 2, LG], I32)
        looked = sb("looked", [P, LG, 2, 2], F32)

        X = sb("X", [P, QUAD, KC, P], F32)
        XR = sb("XR", [P, QUAD, D], F32)
        OUT = sb("OUT", [P, QUAD, D], F32)
        xhi = sb("xhi", [P, 2, KC, P], F32R)
        xlo = sb("xlo", [P, 2, KC, P], F32R)
        vhi = sb("vhi", [P, 2, KC, P], F32R)
        vlo = sb("vlo", [P, 2, KC, P], F32R)
        HB = sb("HB", [P, 2, D], F32)
        T1 = sb("T1", [P, D], F32)
        T2 = sb("T2", [P, D], F32)
        SQ = sb("SQ", [P, D], F32)
        stat = sb("stat", [P, 2, 4], F32)
        mvb = sb("mvb", [P, QUAD, 6], F32)
        mv = sb("mv", [P, QUAD, 2], F32)
        ms = sb("ms", [P, 3, QUAD], F32)
        S = sb("S", [P, QUAD, 3, P], F32)
        XG = sb("XG", [P, 2, KC, P], F32)
        XS = sb("XS", [P, 2, P], F32)
        stage_i = sb("stage_i", [P, QUAD, 2], I32)
        stage_f = sb("stage_f", [P, QUAD, 5], F32)
        xstage_i = sb("xstage_i", [P, 2], I32)
        xstage_f = sb("xstage_f", [P, 4], F32)
        astage = sb("astage", [P, QUAD], I32)

        edges_loaded = sem("edges_loaded")
        consts_made = sem("consts_made")
        consts_cast = sem("consts_cast")
        dve_chain = sem("dve_chain")
        cnt_built = sem("cnt_built")
        cnt_used = sem("cnt_used")
        cnt_done = sem("cnt_done")
        cnt_link = sem("cnt_link")
        heavy_counted = sem("heavy_counted")
        heavy_based = sem("heavy_based")
        tab_built = sem("tab_built")
        tab_stored = sem("tab_stored")
        qa_turned = sem("qa_turned")
        qa_split = sem("qa_split")
        perm_link = sem("perm_link")
        perm_built = sem("perm_built")
        perm_used = sem("perm_used")
        perm_done = sem("perm_done")
        pos_ready = sem("pos_ready")
        comp_link = sem("comp_link")
        comp_built = sem("comp_built")
        comp_used = sem("comp_used")
        comp_done = sem("comp_done")
        comp_ready = sem("comp_ready")
        look_staged = sem("look_staged")
        look_loaded = sem("look_loaded")
        look_done = sem("look_done")
        buck_link = sem("buck_link")
        buck_counted = sem("buck_counted")
        buck_based = sem("buck_based")
        buck2_link = sem("buck2_link")
        place_link = sem("place_link")
        place_built = sem("place_built")
        place_used = sem("place_used")
        place_done = sem("place_done")
        tables_ready = sem("tables_ready")
        vecs_loaded = sem("vecs_loaded")
        vec_link = sem("vec_link")
        wraw_loaded = sem("wraw_loaded")
        wp_stored = sem("wp_stored")
        w_summed = sem("w_summed")
        w_turned = sem("w_turned")
        w_copied = sem("w_copied")
        w_link = sem("w_link")
        w_centred = sem("w_centred")
        w_high = sem("w_high")
        w_low = sem("w_low")
        W_loaded = [sem(f"W_loaded{i}") for i in range(2)]
        a_staged = sem("a_staged")
        a_loaded = [sem(f"a_loaded{j}") for j in range(QUAD)]
        a_h_loaded = [sem(f"a_h_loaded{j}") for j in range(QUAD)]
        a_stats = sem("a_stats")
        a_link = sem("a_link")
        a_std = sem("a_std")
        a_norm = sem("a_norm")
        a_out = sem("a_out")
        a_stored = [sem(f"a_stored{j}") for j in range(QUAD)]
        a_x1_added = sem("a_x1_added")
        a_x1_stored = [sem(f"a_x1_stored{j}") for j in range(QUAD)]
        x_loaded = [sem(f"x_loaded{j}") for j in range(QUAD)]
        x1_loaded = [sem(f"x1_loaded{j}") for j in range(QUAD)]
        out_stored = [sem(f"out_stored{j}") for j in range(QUAD)]
        xt_ready = sem("xt_ready")
        xhi_ready = sem("xhi_ready")
        xlo_ready = sem("xlo_ready")
        xr_ready = sem("xr_ready")
        h_ready = sem("h_ready")
        hb_ready = sem("hb_ready")
        sq_ready = sem("sq_ready")
        std_ready = sem("std_ready")
        ln_chain = sem("ln_chain")
        out_ready = sem("out_ready")
        g_staged = sem("g_staged")
        g_loaded = [sem(f"g_loaded{j}") for j in range(QUAD)]
        s_built = sem("s_built")
        v_ready = sem("v_ready")
        vhi_ready = sem("vhi_ready")
        vlo_ready = sem("vlo_ready")
        xg_staged = sem("xg_staged")
        xg_loaded = sem("xg_loaded")
        xs_built = sem("xs_built")
        xg_used = sem("xg_used")
        fin_staged = sem("fin_staged")
        fin_stored = [sem(f"fin_stored{j}") for j in range(QUAD)]

        waits_passed = {e: sem(f"waits_passed_{e}") for e in ("SP", "Pool", "DVE")}

        H_CREDIT = QUAD
        OUT_CREDIT = QUAD
        HB_CREDIT = 2
        V_CREDIT = QUAD

        psT = [banks[0], banks[1]]
        psH = [banks[2], banks[3]]
        psV = banks[4]

        block = ctx.enter_context(nc.Block())

        def wait_alone(eng, name, value):
            eng.wait_ge(name, value)
            eng.sem_inc(waits_passed[eng.engine.name], 1)

        def within(value, low, high):
            return nc.s_assert_within(value, low, high,
                                      skip_runtime_bounds_check_because="the tables and loops keep it there")

        def heavy_quads(eng, qh, nh):
            with eng.Fori(0, nh) as h:
                yield within(qh + h, 0, NQ - 1), h

        def quad_before(q):
            return within(q - 1, 0, NQ - 2)

        def first_heavy(eng):
            return (eng.value_load(scal_i[0:1, 0:1], min_val=0, max_val=NQ - 1),
                    eng.value_load(scal_i[0:1, 5:6], min_val=1, max_val=NQ))

        @block.sync
        def _(sp):
            sp.dma_start(src_i[:, :], src.rearrange("(p c) -> p c", p=EP)).then_inc(edges_loaded, 16)
            sp.dma_start(dst_i[:, :], dst.rearrange("(p c) -> p c", p=EP)).then_inc(edges_loaded, 16)
            for l in range(LA):
                sp.dma_start(bias[:, l, :], b0[l, :].partition_broadcast(P)).then_inc(vecs_loaded, 16)
                sp.dma_start(gain[:, l, :], ln_g[l, :].partition_broadcast(P)).then_inc(vecs_loaded, 16)
                sp.dma_start(shift[:, l, :], ln_b[l, :].partition_broadcast(P)).then_inc(vecs_loaded, 16)
            for l in range(LB):
                sp.dma_start(bias[:, LA + l, :], b1[l, :].partition_broadcast(P)).then_inc(vecs_loaded, 16)
            sp.wait_ge(tab_built, 1)
            sp.dma_start(node_tab.rearrange("(p c) t -> p (c t)", p=NT),
                         ntab[:, :, :].rearrange("p c t -> p (c t)")).then_inc(tab_stored, 16)
            for l in range(L):
                wa, wb = (W_l[l], W_r[l]) if l < LA else (Ws_neigh[l - LA], Ws_self[l - LA])
                if l:
                    sp.wait_ge(w_low, 8 * l)
                sp.dma_start(wraw[:, 0, :, :], wa.rearrange("(c p) n -> p c n", p=P)).then_inc(wraw_loaded, 16)
                sp.dma_start(wraw[:, 1, :, :], wb.rearrange("(c p) n -> p c n", p=P)).then_inc(wraw_loaded, 16)
                sp.wait_ge(w_low, 8 * (l + 1))
                sp.dma_start(wp[l], W[:, :, :, :].bitcast(F32).rearrange("p m c n -> p m (c n)")).then_inc(wp_stored, 16)
                sp.wait_ge(wp_stored, 16 * (l + 1))

            def a_stores(q, j, target):
                wait_alone(sp, a_out, QUAD * q + j + 1)
                sp.dma_start(target[ds((QUAD * q + j) * P, P), :], OUT[:, j, :]).then_inc(a_stored[j], 16)

            with sp.Fori(0, NQ) as q:
                for j in range(QUAD):
                    a_stores(q, j, H[0])
            for j in range(QUAD):
                sp.wait_ge(a_stored[j], 16 * NQ)

            def load_tile(l, q, j):
                n = (l * NQ + q) * QUAD + j
                wait_alone(sp, h_ready, n + 1)
                if l < LA:
                    if not (l == 0 and isinstance(q, int) and q == 0):
                        wait_alone(sp, xr_ready, n + 1 - QUAD)
                sp.dma_start(X[:, j, :, :], H[l][ds((QUAD * q + j) * P, P), :]
                             .rearrange("p (c k) -> p c k", c=KC)).then_inc(x_loaded[j], 16)

            def load_x1(q, j):
                wait_alone(sp, out_ready, ((L - 1) * NQ + q) * QUAD + j + 1)
                sp.dma_start(XR[:, j, :], x1_dram[ds((QUAD * q + j) * P, P), :]).then_inc(x1_loaded[j], 16)

            def store_tile(l, q, j):
                n = (l * NQ + q) * QUAD + j
                wait_alone(sp, out_ready, n + 1 + OUT_CREDIT)
                target = h_first_net if l == LA - 1 else H[l + 1]
                sp.dma_start(target[ds((QUAD * q + j) * P, P), :], OUT[:, j, :]).then_inc(out_stored[j], 16)

            for l in range(L):
                if l == LA:
                    def m_loads(q, j):
                        if not isinstance(q, int):
                            wait_alone(sp, a_out, QUAD * (NQ + q - 1) + j + 1)
                            wait_alone(sp, a_x1_stored[j], 16 * q)
                        sp.dma_start(XR[:, j, :], h_first_net[ds((QUAD * q + j) * P, P), :]).then_inc(a_h_loaded[j], 16)

                    for j in range(QUAD):
                        sp.wait_ge(out_stored[j], 16 * (LA * NQ + 1))
                    for j in range(QUAD):
                        m_loads(0, j)
                    with sp.Fori(0, NQ - 1) as q:
                        for j in range(QUAD):
                            wait_alone(sp, a_x1_added, QUAD * q + j + 1)
                            sp.dma_start(x1_dram[ds((QUAD * q + j) * P, P), :], XR[:, j, :]).then_inc(a_x1_stored[j], 16)
                        for j in range(QUAD):
                            wait_alone(sp, a_out, QUAD * (NQ + q) + j + 1)
                            sp.dma_start(H[LA][ds((QUAD * q + j) * P, P), :], OUT[:, j, :]).then_inc(a_stored[j], 16)
                        for j in range(QUAD):
                            wait_alone(sp, a_x1_stored[j], 16 * q + 16)
                            sp.dma_start(XR[:, j, :], h_first_net[ds((QUAD * q + QUAD + j) * P, P), :]).then_inc(a_h_loaded[j], 16)
                    for j in range(QUAD):
                        sp.wait_ge(a_x1_added, QUAD * (NQ - 1) + j + 1)
                        sp.dma_start(x1_dram[(QUAD * (NQ - 1) + j) * P:(QUAD * (NQ - 1) + j + 1) * P, :],
                                     XR[:, j, :]).then_inc(a_x1_stored[j], 16)
                        sp.wait_ge(a_out, QUAD * (2 * NQ - 1) + j + 1)
                        sp.dma_start(H[LA][(QUAD * (NQ - 1) + j) * P:(QUAD * (NQ - 1) + j + 1) * P, :],
                                     OUT[:, j, :]).then_inc(a_stored[j], 16)
                    for j in range(QUAD):
                        sp.wait_ge(a_x1_stored[j], 16 * NQ)
                        sp.wait_ge(a_stored[j], 32 * NQ)
                if l:
                    sp.wait_ge(h_ready, l * NT + H_CREDIT)
                sp.dma_start(W[:, 0:2, :, :].bitcast(F32).rearrange("p m c n -> p m (c n)"), wp[l][:, 0:2, :]).then_inc(W_loaded[0], 16)
                sp.dma_start(W[:, 2:4, :, :].bitcast(F32).rearrange("p m c n -> p m (c n)"), wp[l][:, 2:4, :]).then_inc(W_loaded[1], 16)
                for j in range(QUAD):
                    if l and l != LA:
                        sp.wait_ge(out_stored[j], 16 * (l * NQ + 1))
                for j in range(QUAD):
                    load_tile(l, 0, j)
                    if l == L - 1:
                        load_x1(0, j)
                with sp.Fori(0, NQ - 1) as q:
                    for j in range(QUAD):
                        load_tile(l, q + 1, j)
                        if l == L - 1:
                            load_x1(q + 1, j)
                        if l < L - 1:
                            store_tile(l, q, j)
                if l < L - 1:
                    for j in range(QUAD):
                        store_tile(l, NQ - 1, j)

        @block.gpsimd
        def _(pool):
            nc.gpsimd.iota(diff_i[:, :], [[1, P]], 0, -1).then_inc(consts_made, 1)
            nc.gpsimd.iota(iota_i[:, :], [[1, CH]], 0, 0).then_inc(consts_made, 1)
            nc.gpsimd.iota(slot_i[:, :], [[P, P]], 0, 1).then_inc(consts_made, 1)
            nc.gpsimd.iota(nid_i[:, :], [[1, P]], 0, P).then_inc(consts_made, 1)
            nc.gpsimd.memset(ones[:, :], 1.0).then_inc(consts_made, 1)
            nc.gpsimd.memset(zeros[:, :], 0.0).then_inc(consts_made, 1)
            nc.gpsimd.memset(eps[:, :], LN_EPS).then_inc(consts_made, 1)
            nc.gpsimd.memset(ctab[:, :, :], 0.0).then_inc(consts_made, 1)
            nc.gpsimd.memset(cnt_pb[:, :], 0.0).then_inc(consts_made, 1)

            pool.wait_ge(comp_ready, 1)
            pool.wait_ge(tab_stored, 16)
            chunk_groups = pool.value_load(scal_i[0:1, 4:5], min_val=1, max_val=EK // LG)
            with pool.Fori(0, chunk_groups) as g:
                nc.gpsimd.tensor_copy(stage_c[:, :, :], ce_i[:, :, ds(LG * g, LG)]).then_inc(look_staged, 1)
                wait_alone(pool, look_staged, g + 1)
                for c in range(LG):
                    for e in range(2):
                        pool.indirect_dma_start(
                            out=looked[:, c, e, :], out_offset=None, in_=node_tab,
                            in_offset=bass.IndirectOffsetOnAxis(ap=stage_c[:, e, c:c + 1], axis=0)).then_inc(look_loaded, 16)
                wait_alone(pool, look_loaded, 32 * LG * (g + 1))
                nc.gpsimd.tensor_copy(ctab[:, ds(LG * g, LG), :].rearrange("p a t -> p (a t)"),
                                      looked[:, :, :, :].rearrange("p c e t -> p (c e t)")).then_inc(look_done, 1)
                wait_alone(pool, look_done, g + 1)

            def gather_x(n, j):
                nc.gpsimd.tensor_copy(astage[:, j:j + 1], pos_read_i[:, ds(n[1], 1)]).then_inc(a_staged, 1)
                wait_alone(pool, a_staged, n[0] + 1)
                pool.indirect_dma_start(
                    out=X[:, j, :, :].rearrange("p c k -> p (c k)"), out_offset=None, in_=x,
                    in_offset=bass.IndirectOffsetOnAxis(ap=astage[:, j:j + 1], axis=0)).then_inc(a_loaded[j], 16)

            pool.wait_ge(pos_ready, 1)
            for j in range(QUAD):
                gather_x((j, j), j)
            with pool.Fori(1, NQ) as q:
                for j in range(QUAD):
                    wait_alone(pool, a_out, QUAD * q + j - QUAD + 1)
                    gather_x((QUAD * q + j, QUAD * q + j), j)

            pool.wait_ge(tables_ready, 1)
            qh, nh = first_heavy(pool)
            extra_all = pool.value_load(scal_i[0:1, 2:3], min_val=0, max_val=E // UNIT + 1)

            def gather_neighbours(l, q, h, j):
                t = QUAD * q + j
                hn = QUAD * (l * nh + h) + j
                unit = pool.value_load(unit_i[0:1, 0, ds(t, 1)], min_val=0, max_val=CH // 2 - 1)
                more = pool.value_load(unit_i[0:1, 1, ds(t, 1)], min_val=0, max_val=E // UNIT)
                extra = pool.value_load(unit_i[0:1, 2, ds(t, 1)], min_val=0, max_val=CH // 2)
                wait_alone(pool, v_ready, hn + 1)
                nc.gpsimd.tensor_copy(stage_i[:, j, :], edge_row[:, ds(2 * unit, 2)]).then_inc(g_staged, 1)
                nc.gpsimd.tensor_copy(stage_f[:, j, 0:4], edge_dw[:, ds(2 * unit, 2), :]
                                      .rearrange("p a t -> p (a t)")).then_inc(g_staged, 1)
                nc.gpsimd.tensor_copy(stage_f[:, j, 4:5], own[:, ds(QUAD * q + j, 1)]).then_inc(g_staged, 1)
                wait_alone(pool, g_staged, 3 * hn + 3)
                for c in range(2):
                    pool.indirect_dma_start(
                        out=G[:, j, c, :, :].rearrange("p c k -> p (c k)"), out_offset=None, in_=H[l],
                        in_offset=bass.IndirectOffsetOnAxis(ap=stage_i[:, j, c:c + 1], axis=0)).then_inc(g_loaded[j], 16)
                for c in range(2):
                    nc.gpsimd.tensor_scalar(S[:, j, c, :], iota[:, 0:P], stage_f[:, j, 2 * c:2 * c + 1],
                                            stage_f[:, j, 2 * c + 1:2 * c + 2], ALU.is_equal, ALU.mult)
                nc.gpsimd.tensor_scalar(S[:, j, 2, :], ident[:, :], stage_f[:, j, 4:5], None,
                                        ALU.mult).then_inc(s_built, 1)
                with pool.If(more > 0):
                    with pool.Fori(0, more) as k:
                        e = l * extra_all + extra + k
                        u = within(unit + k + 1, 1, CH // 2 - 1)
                        wait_alone(pool, xg_used, e + 1)
                        nc.gpsimd.tensor_copy(xstage_i[:, :], edge_row[:, ds(2 * u, 2)]).then_inc(xg_staged, 1)
                        nc.gpsimd.tensor_copy(xstage_f[:, :], edge_dw[:, ds(2 * u, 2), :]
                                              .rearrange("p a t -> p (a t)")).then_inc(xg_staged, 1)
                        wait_alone(pool, xg_staged, 2 * e + 2)
                        for c in range(2):
                            pool.indirect_dma_start(
                                out=XG[:, c, :, :].rearrange("p c k -> p (c k)"), out_offset=None, in_=H[l],
                                in_offset=bass.IndirectOffsetOnAxis(ap=xstage_i[:, c:c + 1], axis=0)).then_inc(xg_loaded, 16)
                        nc.gpsimd.tensor_scalar(XS[:, 0, :], iota[:, 0:P], xstage_f[:, 0:1],
                                                xstage_f[:, 1:2], ALU.is_equal, ALU.mult)
                        nc.gpsimd.tensor_scalar(XS[:, 1, :], iota[:, 0:P], xstage_f[:, 2:3],
                                                xstage_f[:, 3:4], ALU.is_equal, ALU.mult).then_inc(xs_built, 1)

            pool.sem_inc(fin_staged, QUAD)

            def scatter_out(q, j):
                n = QUAD * q + j
                if not isinstance(q, int):
                    n = within(n, 0, NT - 1)
                wait_alone(pool, out_ready, (L - 1) * NT + n + 1 + OUT_CREDIT)
                nc.gpsimd.tensor_copy(astage[:, j:j + 1], pos_node_i[:, ds(n, 1)]).then_inc(fin_staged, 1)
                wait_alone(pool, fin_staged, n + 1 + QUAD)
                pool.indirect_dma_start(
                    out=out, out_offset=bass.IndirectOffsetOnAxis(ap=astage[:, j:j + 1], axis=0),
                    in_=OUT[:, j, :], in_offset=None, bounds_check=N - 1, oob_is_err=False).then_inc(fin_stored[j], 16)

            for l in range(L):
                if l == LA:
                    pool.wait_ge(h_ready, LA * NT + H_CREDIT)
                    pool.wait_ge(xr_ready, LA * NT)
                    for j in range(QUAD):
                        gather_x((NT + j, j), j)
                    with pool.Fori(1, NQ) as q:
                        for j in range(QUAD):
                            wait_alone(pool, a_x1_added, QUAD * q + j - QUAD + 1)
                            gather_x((NT + QUAD * q + j, QUAD * q + j), j)
                for j in range(QUAD):
                    if l == 0:
                        pool.wait_ge(a_stored[j], 16 * NQ)
                    elif l == LA:
                        pool.wait_ge(a_stored[j], 32 * NQ)
                    else:
                        pool.wait_ge(out_stored[j], 16 * (l * NQ + 1))
                if l < L - 1:
                    for q, h in heavy_quads(pool, qh, nh):
                        for j in range(QUAD):
                            gather_neighbours(l, q, h, j)
                else:
                    with pool.If(qh > 1):
                        with pool.Fori(1, qh) as q:
                            for j in range(QUAD):
                                scatter_out(quad_before(q), j)
                    for q, h in heavy_quads(pool, qh, nh):
                        for j in range(QUAD):
                            gather_neighbours(l, q, h, j)
                        with pool.If(q > 0):
                            for j in range(QUAD):
                                scatter_out(quad_before(q), j)
                    for j in range(QUAD):
                        scatter_out(NQ - 1, j)
            for j in range(QUAD):
                pool.wait_ge(fin_stored[j], 16 * NQ)

        @block.tensor
        def _(pe):
            mm = nc.tensor.matmul
            pe.wait_ge(consts_cast, 1)

            cnt = banks[5][0:NT, 0:2 * P]
            mm(cnt, zeros[:, 0:NT], zeros[:, 0:2 * P], start=True, stop=False, skip_group_check=True)
            with pe.Fori(0, EC // CB) as i:
                pe.wait_ge(cnt_built, i + 1)
                for c in range(CB):
                    last = mm(cnt, oh_hi[:, c, :], oh_lo[:, c, :, :].rearrange("p a k -> p (a k)"),
                              start=False, stop=False, skip_group_check=True)
                last.then_inc(cnt_used, 1)
            mm(cnt, zeros[:, 0:NT], zeros[:, 0:2 * P], start=False, stop=True, skip_group_check=True).then_inc(cnt_done, 1)

            pe.wait_ge(heavy_counted, 1)
            mm(banks[6][0:NT, 0:1], below[0:NT, 0:NT], nd[:, 6, P - 1:P], start=True, stop=True)
            mm(banks[6][:, 2:3], ones[0:NT, :], nd[:, 6, P - 1:P], start=True, stop=True).then_inc(heavy_based, 1)

            pe.wait_ge(heavy_counted, 2)
            mm(banks[7][0:EP, 0:1], below[0:EP, 0:EP], e_f[:, 5, EC - 1:EC], start=True, stop=True)
            mm(banks[7][:, 2:3], ones[0:EP, :], e_f[:, 5, EC - 1:EC], start=True, stop=True).then_inc(heavy_based, 1)

            pe.wait_ge(tab_built, 1)
            mm(banks[0][:, 0:NT], nd[:, 8, :], ident[0:NT, 0:NT], start=True, stop=True)
            mm(banks[0][:, P:P + NT], nd[:, 3, :], ident[0:NT, 0:NT], start=True, stop=True).then_inc(qa_turned, 1)

            perm = banks[1][:, 0:2 * NT]
            mm(perm, zeros[:, 0:P], zeros[:, 0:2 * NT], start=True, stop=False, skip_group_check=True)
            with pe.Fori(0, NQ) as i:
                pe.wait_ge(perm_built, i + 1)
                for c in range(QUAD):
                    last = mm(perm, perm_oh[:, c, 0:P], perm_oh[:, c, P:], start=False, stop=False, skip_group_check=True)
                last.then_inc(perm_used, 1)
            mm(perm, zeros[:, 0:P], zeros[:, 0:2 * NT], start=False, stop=True, skip_group_check=True).then_inc(perm_done, 1)

            comp = banks[2][:, 0:2 * EK]
            mm(comp, zeros[:, 0:P], zeros[:, 0:2 * EK], start=True, stop=False, skip_group_check=True)
            with pe.Fori(0, EC // CC) as i:
                pe.wait_ge(comp_built, i + 1)
                for c in range(CC):
                    last = mm(comp, comp_oh[:, c, 0:P], comp_oh[:, c, P:], start=False, stop=False, skip_group_check=True)
                last.then_inc(comp_used, 1)
            mm(comp, zeros[:, 0:P], zeros[:, 0:2 * EK], start=False, stop=True, skip_group_check=True).then_inc(comp_done, 1)

            for l in range(L):
                for k in range(8):
                    m, c = k // KC, k % KC
                    if l < LA:
                        if k == 0:
                            pe.wait_ge(w_summed, l + 1)
                        if 8 * l + k >= 2:
                            pe.wait_ge(w_copied, 8 * l + k - 1)
                        for nb in range(KC):
                            last = nc.tensor.transpose(banks[6 + k % 2][:, nb * P:(nb + 1) * P],
                                                       wraw[:, 1 - m, nb, c * P:(c + 1) * P], ident[:, :])
                        last.then_inc(w_turned, 1)

            pe.wait_ge(buck_counted, 1)
            mm(banks[4][:, 0:NT], below[:, :], cnt_pb[:, :], start=True, stop=True)
            mm(banks[4][:, P:P + NT], ones[:, :], cnt_pb[:, :], start=True, stop=True).then_inc(buck_based, 1)

            for f in range(3):
                mm(banks[5 + f][:, 0:CH], zeros[:, 0:P], zeros[:, 0:CH], start=True, stop=False, skip_group_check=True)
            chunks = pe.value_load(scal_i[0:1, 1:2], min_val=1, max_val=EK)
            with pe.Fori(0, chunks) as i:
                pe.wait_ge(place_built, i + 1)
                for f in range(3):
                    last = mm(banks[5 + f][:, 0:CH], buck_oh[:, 0:P], buck_oh[:, P + f * CH:P + (f + 1) * CH],
                              start=False, stop=False, skip_group_check=True)
                last.then_inc(place_used, 1)
            for f in range(3):
                last = mm(banks[5 + f][:, 0:CH], zeros[:, 0:P], zeros[:, 0:CH], start=False, stop=True, skip_group_check=True)
            last.then_inc(place_done, 1)

            pe.wait_ge(tables_ready, 1)
            qh, nh = first_heavy(pe)
            extra_all = pe.value_load(scal_i[0:1, 2:3], min_val=0, max_val=E // UNIT + 1)
            pe.sem_inc(h_ready, H_CREDIT)
            pe.sem_inc(v_ready, V_CREDIT)
            pe.sem_inc(xg_used, 1)

            def turn(l, q, j):
                n = (l * NQ + q) * QUAD + j
                pe.wait_ge(x_loaded[j], 16 * (l * NQ + q) + 16)
                pe.wait_ge(xlo_ready, n + 1)
                for c in range(KC):
                    last = nc.tensor.transpose(psT[j % 2][:, c * P:(c + 1) * P], X[:, j, c, :], ident[:, :])
                last.then_inc(xt_ready, 1)

            def products(h, hi, lo, w, first, final):
                last = None
                for c in range(KC):
                    mm(h, hi[:, c, :], W[:, w, c, :], start=first and c == 0, stop=False, skip_group_check=True)
                    mm(h, hi[:, c, :], W[:, w + 1, c, :], start=False, stop=False, skip_group_check=True)
                    last = mm(h, lo[:, c, :], W[:, w, c, :], start=False, stop=final and c == KC - 1,
                              skip_group_check=True)
                return last

            def tile(l, q, j, h=None):
                n = (l * NQ + q) * QUAD + j
                if j < QUAD - 1:
                    turn(l, q, j + 1)
                else:
                    with pe.If(q < NQ - 1):
                        turn(l, within(q + 1, 1, NQ - 1), 0)
                if h is not None:
                    t = QUAD * q + j
                    hq = l * nh + h
                    hn = QUAD * hq + j
                    more = pe.value_load(unit_i[0:1, 1, ds(t, 1)], min_val=0, max_val=E // UNIT)
                    extra = pe.value_load(unit_i[0:1, 2, ds(t, 1)], min_val=0, max_val=CH // 2)
                    pe.wait_ge(g_loaded[j], 32 * hq + 32)
                    pe.wait_ge(s_built, hn + 1)
                    for c in range(2):
                        for f in range(KC):
                            mm(psV[:, f * P:(f + 1) * P], G[:, j, c, f, :], S[:, j, c, :],
                               start=c == 0 and f == 0, stop=False, skip_group_check=True)
                    with pe.If(more > 0):
                        with pe.Fori(0, more) as k:
                            e = l * extra_all + extra + k
                            pe.wait_ge(xg_loaded, 32 * e + 32)
                            pe.wait_ge(xs_built, e + 1)
                            for c in range(2):
                                for f in range(KC):
                                    last = mm(psV[:, f * P:(f + 1) * P], XG[:, c, f, :], XS[:, c, :],
                                              start=False, stop=False, skip_group_check=True)
                            last.then_inc(xg_used, 1)
                    for f in range(KC):
                        last = mm(psV[:, f * P:(f + 1) * P], X[:, j, f, :], S[:, j, 2, :],
                                  start=False, stop=True, skip_group_check=True)
                    last.then_inc(v_ready, 1)
                pe.wait_ge(xlo_ready, n + 1 + 2)
                pe.wait_ge(hb_ready, n + 1)
                last = products(psH[j % 2][:, :], xhi[:, j % 2], xlo[:, j % 2], 0, True, h is None)
                if h is not None:
                    pe.wait_ge(W_loaded[1], 16 * (l + 1))
                    pe.wait_ge(vlo_ready, hn + 1)
                    last = products(psH[j % 2][:, :], vhi[:, j % 2], vlo[:, j % 2], 2, False, True)
                last.then_inc(h_ready, 1)

            for l in range(L):
                turn(l, 0, 0)
                pe.wait_ge(W_loaded[0], 16 * (l + 1))
                with pe.If(qh > 0):
                    with pe.Fori(0, qh) as q:
                        for j in range(QUAD):
                            tile(l, q, j)
                for q, h in heavy_quads(pe, qh, nh):
                    for j in range(QUAD):
                        tile(l, q, j, h)

        @block.scalar
        def _(act):
            for l in range(L):
                for k in range(8):
                    m, c = k // KC, k % KC
                    i = 8 * l + k
                    if l < LA:
                        act.wait_ge(w_turned, i + 1)
                        if i >= 2:
                            act.wait_ge(w_low, i - 1)
                        nc.scalar.activation(wtmp[:, k % 2, :], banks[6 + k % 2][:, :], ACT.Copy,
                                             accum_out=wsum[:, k % 2:k % 2 + 1]).then_inc(w_copied, 1)
                        act.wait_ge(w_centred, i + 1)
                        if l and k == 0:
                            act.wait_ge(wp_stored, 16 * l)
                        nc.scalar.copy(W[:, 2 * m, c, :], wcen[:, k % 2, :]).then_inc(w_high, 1)
                    else:
                        if k == 0:
                            act.wait_ge(w_summed, l + 1)
                            act.wait_ge(wp_stored, 16 * l)
                        nc.scalar.copy(W[:, 2 * m, c, :], wraw[:, 1 - m, c, :]).then_inc(w_high, 1)

            def normalise(n0, q):
                act.wait_ge(a_stats, n0 + q + 1)
                nc.scalar.activation(ms[:, 0, :], mv[:, :, 1], ACT.Sqrt, bias=eps[:, 0:1]).then_inc(a_std, 1)
                act.wait_ge(a_norm, n0 + q + 1)
                for j in range(QUAD):
                    act.wait_ge(a_stored[j], 16 * (n0 + q)) if not isinstance(q, int) else None
                    src_t = X[:, j, :, :].rearrange("p c k -> p (c k)") if n0 == 0 else XR[:, j, :]
                    nc.scalar.activation(OUT[:, j, :], src_t, ACT.Relu, bias=ms[:, 2, j:j + 1],
                                         scale=ms[:, 1, j:j + 1]).then_inc(a_out, 1)

            normalise(0, 0)
            with act.Fori(1, NQ) as q:
                normalise(0, q)

            act.wait_ge(tables_ready, 1)
            qh, nh = first_heavy(act)
            act.sem_inc(out_ready, OUT_CREDIT)
            for j in range(QUAD):
                act.sem_inc(out_stored[j], 16)

            def split(l, q, j):
                n = (l * NQ + q) * QUAD + j
                act.wait_ge(xt_ready, n + 1)
                act.wait_ge(h_ready, n + 1 + H_CREDIT - 2)
                nc.scalar.copy(xhi[:, j % 2, :, :].rearrange("p c k -> p (c k)"), psT[j % 2][:, :]).then_inc(xhi_ready, 1)
                if l < LA:
                    act.wait_ge(out_ready, n + 1)
                    nc.scalar.copy(XR[:, j, :], X[:, j, :, :].rearrange("p c k -> p (c k)")).then_inc(xr_ready, 1)

            def back(l, q, j, n):
                act.wait_ge(hb_ready, n + 1 + HB_CREDIT)
                if l < LA:
                    nc.scalar.activation(SQ[:, :], HB[:, j % 2, :], ACT.Square,
                                         accum_out=stat[:, j % 2, 0:1]).then_inc(sq_ready, 1)
                    act.wait_ge(sq_ready, n + 1)
                    nc.scalar.activation(stat[:, j % 2, 1:2], stat[:, j % 2, 0:1], ACT.Sqrt,
                                         bias=eps[:, 0:1], scale=1.0 / D).then_inc(std_ready, 1)
                elif l < L - 1:
                    act.wait_ge(out_stored[j], 16 * (l * NQ + q) + 16)
                    nc.scalar.activation(OUT[:, j, :], HB[:, j % 2, :], ACT.Relu).then_inc(out_ready, 1)

            def tile(l, q, j, h=None):
                if h is not None:
                    hn = QUAD * (l * nh + h) + j
                    n = (l * NQ + q) * QUAD + j
                    act.wait_ge(v_ready, hn + 1 + V_CREDIT)
                    act.wait_ge(h_ready, n + 1 + H_CREDIT - 2)
                    nc.scalar.copy(vhi[:, j % 2, :, :].rearrange("p c k -> p (c k)"), psV[:, :]).then_inc(vhi_ready, 1)
                if j < QUAD - 1:
                    split(l, q, j + 1)
                else:
                    with act.If(q < NQ - 1):
                        split(l, within(q + 1, 1, NQ - 1), 0)
                if l < L - 1:
                    if j:
                        back(l, q, j - 1, (l * NQ + q) * QUAD + j - 1)
                    else:
                        with act.If(q > 0):
                            back(l, quad_before(q), QUAD - 1, (l * NQ + q) * QUAD - 1)

            for l in range(L):
                if l == LA:
                    with act.Fori(0, NQ) as q:
                        normalise(NQ, q)
                split(l, 0, 0)
                with act.If(qh > 0):
                    with act.Fori(0, qh) as q:
                        for j in range(QUAD):
                            tile(l, q, j)
                for q, h in heavy_quads(act, qh, nh):
                    for j in range(QUAD):
                        tile(l, q, j, h)
                if l < L - 1:
                    back(l, NQ - 1, QUAD - 1, (l + 1) * NT - 1)

        @block.vector
        def _(dve):
            v = nc.vector
            chain = [0]

            def link(ins):
                chain[0] += 1
                ins.then_inc(dve_chain, 1)
                dve.wait_ge(dve_chain, chain[0])

            def bc_in(ap, n):
                return ap.unsqueeze(2).broadcast_to([ap.shape[0], ap.shape[1], n])

            def bc_out(ap, n):
                return ap.unsqueeze(1).broadcast_to([ap.shape[0], n, ap.shape[1]])

            dve.wait_ge(consts_made, 9)
            v.tensor_copy(iota[:, :], iota_i[:, :])
            v.tensor_copy(slot[:, :], slot_i[:, :])
            v.tensor_copy(nid[:, :], nid_i[:, :])
            v.tensor_copy(iota_b[:, :], iota_i[:, 0:P])
            link(v.tensor_copy(diff[:, :], diff_i[:, :]))
            v.tensor_scalar(ident[:, :], diff[:, :], 0.0, None, ALU.is_equal)
            v.tensor_scalar(below[:, :], diff[:, :], 0.0, None, ALU.is_gt).then_inc(consts_cast, 1)

            sf, df, dhif, dlof, ns, cum, cp, tmp = (e_f[:, k, :] for k in range(8))
            dve.wait_ge(edges_loaded, 32)
            v.tensor_copy(sf, src_i[:, :])
            v.tensor_copy(df, dst_i[:, :])
            v.tensor_scalar(dhi_i[:, :], dst_i[:, :], 7, None, ALU.arith_shift_right)
            link(v.tensor_scalar(dlo_i[:, :], dst_i[:, :], P - 1, None, ALU.bitwise_and))
            v.tensor_copy(dhi_b[:, :], dhi_i[:, :])
            v.tensor_copy(dlo_b[:, :], dlo_i[:, :])
            v.tensor_tensor(self_b[:, :], sf, df, ALU.is_equal)
            link(v.tensor_tensor(ns, sf, df, ALU.not_equal))

            def count_step(i, static):
                if not static:
                    dve.wait_ge(cnt_used, i)
                v.tensor_tensor(oh_hi[:, :, :], bc_out(iota_b[0:EP, 0:NT], CB), bc_in(dhi_b[:, ds(i * CB, CB)], NT), ALU.is_equal)
                v.tensor_tensor(oh_lo[:, :, 0, :], bc_out(iota_b[0:EP, :], CB), bc_in(dlo_b[:, ds(i * CB, CB)], P),
                                ALU.is_equal).then_inc(cnt_link, 1)
                dve.wait_ge(cnt_link, i + 1)
                v.tensor_tensor(oh_lo[:, :, 1, :], oh_lo[:, :, 0, :], bc_in(self_b[:, ds(i * CB, CB)], P),
                                ALU.mult).then_inc(cnt_built, 1)

            count_step(0, True)
            with dve.Fori(1, EC // CB) as i:
                count_step(i, False)

            cntf, loops, inv, owna, heavy, other, hcum, hexc, pos, none, okn, t0 = (nd[:, k, :] for k in range(12))
            dve.wait_ge(cnt_done, 1)
            v.tensor_copy(loops, banks[5][0:NT, P:2 * P])
            link(v.tensor_copy(cntf, banks[5][0:NT, 0:P]))
            link(v.tensor_scalar(t0, cntf, 1.0, None, ALU.max))
            v.tensor_scalar(none, cntf, 0.5, None, ALU.is_lt)
            v.tensor_tensor(other, cntf, loops, ALU.not_equal)
            v.tensor_scalar(okn, nid[0:NT, :], float(N), None, ALU.is_lt)
            link(v.reciprocal(inv, t0))
            link(v.tensor_tensor(heavy, none, other, ALU.max))
            link(v.tensor_tensor(heavy, heavy, okn, ALU.mult))
            link(v.tensor_tensor(t0, loops, inv, ALU.mult))
            link(v.tensor_scalar(t0, t0, -1.0, None, ALU.add))
            link(v.tensor_tensor(owna, t0, heavy, ALU.mult))
            v.tensor_tensor_scan(hcum, ones[0:NT, :], heavy, 0.0, ALU.mult, ALU.add).then_inc(heavy_counted, 1)
            v.tensor_tensor_scan(cum, ones[0:EP, 0:EC], ns, 0.0, ALU.mult, ALU.add).then_inc(heavy_counted, 1)
            dve.wait_ge(heavy_based, 1)
            link(v.tensor_copy(nsm[0:NT, 0:1], banks[6][0:NT, 0:1]))
            link(v.tensor_copy(nsm[:, 1:2], banks[6][:, 2:3]))
            link(v.tensor_tensor(hexc, hcum, heavy, ALU.subtract))
            link(v.tensor_scalar(hexc, hexc, nsm[0:NT, 0:1], None, ALU.add))
            link(v.tensor_scalar(nsm[:, 2:3], nsm[:, 1:2], -1.0, float(NP), ALU.mult, ALU.add))
            link(v.tensor_tensor(pos, nid[0:NT, :], hexc, ALU.subtract))
            link(v.tensor_scalar(t0, hexc, nsm[0:NT, 2:3], None, ALU.add))
            link(v.tensor_tensor(t0, t0, pos, ALU.subtract))
            link(v.tensor_tensor(t0, t0, heavy, ALU.mult))
            link(v.tensor_tensor(pos, pos, t0, ALU.add))
            v.tensor_copy(ntab[:, :, 0], pos)
            v.tensor_copy(ntab[:, :, 1], inv).then_inc(tab_built, 1)
            link(v.tensor_copy(small_i[:, 0:1], nsm[:, 2:3]))
            link(v.tensor_scalar(small_i[:, 1:2], small_i[:, 0:1], 9, None, ALU.arith_shift_right))
            link(v.tensor_scalar(nsm[:, 3:4], small_i[:, 1:2], float(NQ - 1), None, ALU.min))
            link(v.tensor_scalar(nsm[:, 9:10], nsm[:, 3:4], float(QUAD), None, ALU.mult))
            link(v.tensor_copy(scal_i[0:1, 0:1], nsm[0:1, 3:4]))
            link(v.tensor_scalar(nsm[:, 11:12], nsm[:, 3:4], -1.0, float(NQ), ALU.mult, ALU.add))
            link(v.tensor_copy(scal_i[0:1, 5:6], nsm[0:1, 11:12]))

            dve.wait_ge(qa_turned, 1)
            v.tensor_copy(qa_t[:, 1, :], banks[0][:, P:P + NT])
            v.tensor_copy(qt_i[:, 0, :], banks[0][:, 0:NT])
            link(v.tensor_copy(qa_t[:, 0, :], banks[0][:, 0:NT]))
            v.tensor_scalar(qt_i[:, 1, :], qt_i[:, 0, :], 7, None, ALU.arith_shift_right)
            link(v.tensor_scalar(qt_i[:, 2, :], qt_i[:, 0, :], P - 1, None, ALU.bitwise_and))
            v.tensor_copy(qt_f[:, 0, :], qt_i[:, 1, :])
            link(v.tensor_copy(qt_f[:, 1, :], qt_i[:, 2, :]))

            def perm_step(i, static):
                if not static:
                    dve.wait_ge(perm_used, i)
                cols = ds(i * QUAD, QUAD)
                v.tensor_tensor(perm_oh[:, :, 0:P], bc_out(iota[:, 0:P], QUAD), bc_in(qt_f[:, 1, cols], P), ALU.is_equal)
                v.tensor_tensor(perm_oh[:, :, P:P + NT], bc_out(iota[:, 0:NT], QUAD), bc_in(qt_f[:, 0, cols], NT),
                                ALU.is_equal).then_inc(perm_link, 1)
                dve.wait_ge(perm_link, 2 * i + 1)
                v.tensor_tensor(perm_oh[:, :, P + NT:], perm_oh[:, :, P:P + NT], bc_in(qa_t[:, 1, cols], NT),
                                ALU.mult).then_inc(perm_link, 1)
                dve.wait_ge(perm_link, 2 * i + 2)
                v.tensor_tensor(perm_oh[:, :, P:P + NT], perm_oh[:, :, P:P + NT], bc_in(slot[:, cols], NT),
                                ALU.mult).then_inc(perm_built, 1)

            perm_step(0, True)
            with dve.Fori(1, NQ) as i:
                perm_step(i, False)
            dve.wait_ge(perm_done, 1)
            v.tensor_copy(own[:, :], banks[1][:, NT:2 * NT])
            v.tensor_copy(pos_node_i[:, :], banks[1][:, 0:NT])
            link(v.tensor_copy(pos_f[:, 0, :], banks[1][:, 0:NT]))
            v.tensor_scalar(pos_read_i[:, :], pos_f[:, 0, :], float(N - 1), None, ALU.min).then_inc(pos_ready, 1)

            dve.wait_ge(heavy_based, 2)
            link(v.tensor_copy(nsm[0:EP, 4:5], banks[7][0:EP, 0:1]))
            link(v.tensor_copy(nsm[:, 5:6], banks[7][:, 2:3]))
            link(v.tensor_scalar(cp, cum, nsm[0:EP, 4:5], -1.0, ALU.add, ALU.add))
            link(v.tensor_tensor(cp, cp, ns, ALU.mult))
            link(v.tensor_copy(dhi_i[:, :], cp))
            link(v.tensor_scalar(dlo_i[:, :], dhi_i[:, :], P - 1, None, ALU.bitwise_and))
            link(v.tensor_scalar(dhi_i[:, :], dhi_i[:, :], 7, None, ALU.arith_shift_right))
            link(v.tensor_copy(dlof, dlo_i[:, :]))
            link(v.tensor_copy(dhif, dhi_i[:, :]))
            link(v.tensor_scalar(dhif, dhif, 1.0, None, ALU.add))
            link(v.tensor_tensor(dhif, dhif, ns, ALU.mult))
            link(v.tensor_scalar(dhif, dhif, -1.0, None, ALU.add))

            def comp_step(i, static):
                if not static:
                    dve.wait_ge(comp_used, i)
                cols = ds(i * CC, CC)
                v.tensor_tensor(comp_oh[:, :, 0:P], bc_out(iota[0:EP, 0:P], CC), bc_in(dlof[:, cols], P), ALU.is_equal)
                v.tensor_tensor(comp_oh[:, :, P:P + EK], bc_out(iota[0:EP, 0:EK], CC), bc_in(dhif[:, cols], EK),
                                ALU.is_equal).then_inc(comp_link, 1)
                dve.wait_ge(comp_link, 2 * i + 1)
                v.tensor_tensor(comp_oh[:, :, P + EK:], comp_oh[:, :, P:P + EK], bc_in(df[:, cols], EK),
                                ALU.mult).then_inc(comp_link, 1)
                dve.wait_ge(comp_link, 2 * i + 2)
                v.tensor_tensor(comp_oh[:, :, P:P + EK], comp_oh[:, :, P:P + EK], bc_in(sf[:, cols], EK),
                                ALU.mult).then_inc(comp_built, 1)

            comp_step(0, True)
            with dve.Fori(1, EC // CC) as i:
                comp_step(i, False)
            dve.wait_ge(comp_done, 1)
            v.tensor_copy(ce_i[:, 0, :], banks[2][:, 0:EK])
            v.tensor_copy(ce_i[:, 1, :], banks[2][:, EK:2 * EK])
            link(v.tensor_scalar(nsm[0:1, 6:7], nsm[0:1, 5:6], float(P - 1), None, ALU.add))
            link(v.tensor_copy(scal_i[0:1, 3:4], nsm[0:1, 6:7]))
            link(v.tensor_scalar(scal_i[0:1, 3:4], scal_i[0:1, 3:4], 7, None, ALU.arith_shift_right))
            link(v.tensor_scalar(scal_i[0:1, 1:2], scal_i[0:1, 3:4], 1.0, None, ALU.max))
            link(v.tensor_scalar(nsm[0:1, 6:7], scal_i[0:1, 1:2], float(LG - 1), None, ALU.add))
            link(v.tensor_copy(scal_i[0:1, 3:4], nsm[0:1, 6:7]))
            v.tensor_scalar(scal_i[0:1, 4:5], scal_i[0:1, 3:4], 2, None, ALU.arith_shift_right).then_inc(comp_ready, 1)

            dve.wait_ge(vecs_loaded, 16 * (3 * LA + LB))
            link(v.tensor_reduce(bsum[:, :], bias[:, 0:LA, :], AX.X, ALU.add))
            link(v.tensor_scalar(bsum[:, :], bsum[:, :], -1.0 / D, None, ALU.mult))
            for l in range(LA):
                link(v.tensor_scalar(bias[:, l, :], bias[:, l, :], bsum[:, l:l + 1], None, ALU.add))

            for l in range(L):
                dve.wait_ge(wraw_loaded, 32 * (l + 1))
                v.tensor_tensor(wraw[:, 1, :, :].rearrange("p c n -> p (c n)"),
                                wraw[:, 1, :, :].rearrange("p c n -> p (c n)"),
                                wraw[:, 0, :, :].rearrange("p c n -> p (c n)"), ALU.add).then_inc(w_summed, 1)
                for k in range(8):
                    m, c = k // KC, k % KC
                    i = 8 * l + k
                    if l < LA:
                        dve.wait_ge(w_copied, i + 1)
                        link(v.tensor_scalar(wneg[:, k % 2:k % 2 + 1], wsum[:, k % 2:k % 2 + 1], -1.0 / D, None, ALU.mult))
                        v.tensor_scalar(wcen[:, k % 2, :], wtmp[:, k % 2, :], wneg[:, k % 2:k % 2 + 1], None,
                                        ALU.add).then_inc(w_centred, 1)
                        full = wcen[:, k % 2, :]
                    else:
                        full = wraw[:, 1 - m, c, :]
                    dve.wait_ge(w_high, i + 1)
                    v.tensor_tensor(W[:, 2 * m + 1, c, :], full, W[:, 2 * m, c, :].bitcast(F32),
                                    ALU.subtract).then_inc(w_low, 1)

            def stats(n0, q, first):
                for j in range(QUAD):
                    row = X[:, j, :, :].rearrange("p c k -> p (c k)")
                    dve.wait_ge(a_loaded[j], 16 * (n0 + q) + 16)
                    if n0:
                        dve.wait_ge(a_h_loaded[j], 16 * q + 16)
                        v.tensor_tensor(XR[:, j, :], XR[:, j, :], row, ALU.add).then_inc(a_x1_added, 1)
                        dve.wait_ge(a_x1_added, QUAD * q + j + 1)
                        row = XR[:, j, :]
                    if j == 0 and not first:
                        dve.wait_ge(a_out, QUAD * (n0 + q))
                    v.bn_stats(mvb[:, j, :], row).then_inc(a_link, 1)
                wait_alone(dve, a_link, (QUAD + 1) * (n0 + q) + QUAD)
                for j in range(QUAD):
                    last = v.bn_aggr(mv[:, j, :], mvb[:, j, :])
                last.then_inc(a_stats, 1)
                dve.wait_ge(a_std, n0 + q + 1)
                v.reciprocal(ms[:, 1, :], ms[:, 0, :]).then_inc(a_link, 1)
                dve.wait_ge(a_link, (QUAD + 1) * (n0 + q) + QUAD + 1)
                v.scalar_tensor_tensor(ms[:, 2, :], mv[:, :, 0], -1.0, ms[:, 1, :], ALU.mult, ALU.mult).then_inc(a_norm, 1)

            stats(0, 0, True)
            with dve.Fori(1, NQ) as q:
                stats(0, q, False)

            chunks = dve.value_load(scal_i[0:1, 1:2], min_val=1, max_val=EK)
            qh0, nh0 = first_heavy(dve)
            groups = dve.value_load(scal_i[0:1, 4:5], min_val=1, max_val=EK // LG)
            dve.wait_ge(look_done, groups)
            c_bk, c_lo, c_pl, c_ph, c_pos, c_ok, c_t, c_u = (c_f[:, k, :] for k in range(8))
            link(v.tensor_scalar(c_ok, slot[:, 0:EK], nsm[:, 5:6], None, ALU.is_lt))
            link(v.tensor_copy(c_i[:, 0, :], ctab[:, :, 2]))
            link(v.tensor_scalar(c_i[:, 1, :], c_i[:, 0, :], 7, None, ALU.arith_shift_right))
            link(v.tensor_scalar(c_i[:, 2, :], c_i[:, 0, :], P - 1, None, ALU.bitwise_and))
            link(v.tensor_copy(c_lo, c_i[:, 2, :]))
            link(v.tensor_copy(c_bk, c_i[:, 1, :]))
            link(v.tensor_scalar(c_bk, c_bk, 1.0, None, ALU.add))
            link(v.tensor_tensor(c_bk, c_bk, c_ok, ALU.mult))
            link(v.tensor_scalar(c_bk, c_bk, -1.0, None, ALU.add))
            with dve.Fori(0, nh0 * QUAD) as k:
                b = within(k + qh0 * QUAD, 0, NT - 1)
                v.tensor_scalar(c_t, c_bk, iota[:, ds(b, 1)], 0.0, ALU.is_equal, ALU.add,
                                accum_out=cnt_pb[:, ds(b, 1)]).then_inc(buck_link, 1)
                dve.wait_ge(buck_link, k + 1)
            v.tensor_scalar(ub[:, 5, :], cnt_pb[:, :], 0.0, None, ALU.add).then_inc(buck_counted, 1)
            dve.wait_ge(buck_based, 1)
            tot, units, ucum, base, isheavy, _spare = (ub[:, k, :] for k in range(6))
            link(v.tensor_copy(tot, banks[4][:, P:P + NT]))
            link(v.tensor_scalar(ub[:, 5, :], tot, float(UNIT - 1), None, ALU.add))
            link(v.tensor_copy(ub_i[:, 0, :], ub[:, 5, :]))
            link(v.tensor_scalar(ub_i[:, 0, :], ub_i[:, 0, :], 8, None, ALU.arith_shift_right))
            link(v.tensor_copy(units, ub_i[:, 0, :]))
            link(v.tensor_scalar(units, units, 1.0, None, ALU.max))
            link(v.tensor_scalar(isheavy, iota[:, 0:NT], nsm[:, 9:10], None, ALU.is_ge))
            link(v.tensor_tensor(units, units, isheavy, ALU.mult))
            link(v.tensor_tensor_scan(ucum, ones[:, 0:NT], units, 0.0, ALU.mult, ALU.add))
            link(v.tensor_tensor(ucum, ucum, units, ALU.subtract))
            link(v.tensor_scalar(base, ucum, float(UNIT), None, ALU.mult))
            link(v.tensor_tensor(base, base, banks[4][:, 0:NT], ALU.add))
            link(v.memset(c_pos, 0.0))
            with dve.Fori(0, nh0 * QUAD) as k:
                b = within(k + qh0 * QUAD, 0, NT - 1)
                v.tensor_scalar(c_t, c_bk, iota[:, ds(b, 1)], None, ALU.is_equal).then_inc(buck2_link, 1)
                dve.wait_ge(buck2_link, 4 * k + 1)
                v.tensor_tensor_scan(c_u, ones[:, 0:EK], c_t, base[:, ds(b, 1)], ALU.mult, ALU.add).then_inc(buck2_link, 1)
                dve.wait_ge(buck2_link, 4 * k + 2)
                v.tensor_tensor(c_u, c_u, c_t, ALU.mult).then_inc(buck2_link, 1)
                dve.wait_ge(buck2_link, 4 * k + 3)
                v.tensor_tensor(c_pos, c_pos, c_u, ALU.add).then_inc(buck2_link, 1)
                dve.wait_ge(buck2_link, 4 * k + 4)
            link(v.tensor_scalar(c_pos, c_pos, -1.0, None, ALU.add))
            link(v.tensor_copy(c_i[:, 0, :], c_pos))
            link(v.tensor_scalar(c_i[:, 1, :], c_i[:, 0, :], 7, None, ALU.arith_shift_right))
            link(v.tensor_scalar(c_i[:, 2, :], c_i[:, 0, :], P - 1, None, ALU.bitwise_and))
            link(v.tensor_copy(c_ph, c_i[:, 1, :]))
            link(v.tensor_copy(c_pl, c_i[:, 2, :]))

            def place_step(i, static):
                if not static:
                    dve.wait_ge(place_used, i)
                v.tensor_scalar(buck_oh[:, 0:P], iota[:, 0:P], c_pl[:, ds(i, 1)], None, ALU.is_equal)
                v.tensor_scalar(buck_eq[:, :], iota[:, :], c_ph[:, ds(i, 1)], None, ALU.is_equal).then_inc(place_link, 1)
                dve.wait_ge(place_link, i + 1)
                v.tensor_scalar(buck_oh[:, P:P + CH], buck_eq[:, :], ctab[:, ds(i, 1), 0], None, ALU.mult)
                v.tensor_scalar(buck_oh[:, P + CH:P + 2 * CH], buck_eq[:, :], c_lo[:, ds(i, 1)], None, ALU.mult)
                v.tensor_scalar(buck_oh[:, P + 2 * CH:], buck_eq[:, :], ctab[:, ds(i, 1), 3], None,
                                ALU.mult).then_inc(place_built, 1)

            place_step(0, True)
            with dve.If(chunks > 1):
                with dve.Fori(1, chunks) as i:
                    place_step(i, False)
            dve.wait_ge(place_done, 1)
            v.tensor_copy(edge_row[:, :], banks[5][:, 0:CH])
            v.tensor_copy(edge_dw[:, :, 0], banks[6][:, 0:CH])
            link(v.tensor_copy(edge_dw[:, :, 1], banks[7][:, 0:CH]))
            link(v.tensor_copy(unit_i[0:1, 0, :], ucum[0:1, :]))
            link(v.tensor_scalar(unit_i[0:1, 1, :], units[0:1, :], -1.0, 0.0, ALU.add, ALU.max))
            link(v.tensor_tensor(tot[0:1, :], ucum[0:1, :], iota[0:1, 0:NT], ALU.subtract))
            link(v.tensor_scalar(tot[0:1, :], tot[0:1, :], nsm[0:1, 9:10], 0.0, ALU.add, ALU.max))
            link(v.tensor_copy(unit_i[0:1, 2, :], tot[0:1, :]))
            link(v.tensor_tensor(nsm[0:1, 10:11], tot[0:1, NT - 1:NT], units[0:1, NT - 1:NT], ALU.add))
            link(v.tensor_scalar(nsm[0:1, 10:11], nsm[0:1, 10:11], -1.0, None, ALU.add))
            v.tensor_copy(scal_i[0:1, 2:3], nsm[0:1, 10:11]).then_inc(tables_ready, 1)
            dve.wait_ge(tables_ready, 1)
            qh, nh = first_heavy(dve)
            dve.sem_inc(xlo_ready, 2)
            dve.sem_inc(hb_ready, HB_CREDIT)
            dve.sem_inc(ln_chain, 3)

            def split(l, q, j):
                n = (l * NQ + q) * QUAD + j
                dve.wait_ge(xhi_ready, n + 1)
                v.tensor_tensor(xlo[:, j % 2, :, :].rearrange("p c k -> p (c k)"), psT[j % 2][:, :],
                                xhi[:, j % 2, :, :].bitcast(F32).rearrange("p c k -> p (c k)"),
                                ALU.subtract).then_inc(xlo_ready, 1)

            def back(l, q, j, n):
                dve.wait_ge(std_ready, n + 1)
                v.reciprocal(stat[:, j % 2, 2:3], stat[:, j % 2, 1:2]).then_inc(ln_chain, 1)
                dve.wait_ge(ln_chain, 3 * n + 4)
                v.scalar_tensor_tensor(T1[:, :], HB[:, j % 2, :], stat[:, j % 2, 2:3], gain[:, l, :],
                                       ALU.mult, ALU.mult).then_inc(ln_chain, 1)
                dve.wait_ge(ln_chain, 3 * n + 5)
                v.tensor_tensor(T2[:, :], T1[:, :], shift[:, l, :], ALU.add).then_inc(ln_chain, 1)
                dve.wait_ge(ln_chain, 3 * n + 6)
                dve.wait_ge(xr_ready, n + 1)
                dve.wait_ge(out_stored[j], 16 * (l * NQ + q) + 16)
                v.scalar_tensor_tensor(OUT[:, j, :], T2[:, :], 0.0, XR[:, j, :], ALU.max, ALU.add).then_inc(out_ready, 1)

            def tile(l, q, j, h=None):
                n = (l * NQ + q) * QUAD + j
                if h is not None:
                    hn = QUAD * (l * nh + h) + j
                    dve.wait_ge(vhi_ready, hn + 1)
                    v.tensor_tensor(vlo[:, j % 2, :, :].rearrange("p c k -> p (c k)"), psV[:, :],
                                    vhi[:, j % 2, :, :].bitcast(F32).rearrange("p c k -> p (c k)"),
                                    ALU.subtract).then_inc(vlo_ready, 1)
                if j < QUAD - 1:
                    split(l, q, j + 1)
                else:
                    with dve.If(q < NQ - 1):
                        split(l, within(q + 1, 1, NQ - 1), 0)
                if l < LA:
                    if j:
                        back(l, q, j - 1, (l * NQ + q) * QUAD + j - 1)
                    else:
                        with dve.If(q > 0):
                            back(l, quad_before(q), QUAD - 1, (l * NQ + q) * QUAD - 1)
                dve.wait_ge(h_ready, n + 1 + H_CREDIT)
                if LA <= l < L - 1:
                    if l > LA or j >= 2:
                        dve.wait_ge(out_ready, n + 1 + OUT_CREDIT - 2)
                    else:
                        dve.wait_ge(out_ready, n + 1 + OUT_CREDIT - 2)
                v.tensor_tensor(HB[:, j % 2, :], psH[j % 2][:, :], bias[:, l, :], ALU.add).then_inc(hb_ready, 1)
                if l == L - 1:
                    dve.wait_ge(hb_ready, n + 1 + HB_CREDIT)
                    wait_alone(dve, x1_loaded[j], 16 * q + 16)
                    with dve.If(q > 0):
                        wait_alone(dve, fin_stored[j], 16 * q)
                    v.tensor_tensor(OUT[:, j, :], HB[:, j % 2, :], XR[:, j, :], ALU.add).then_inc(out_ready, 1)

            for l in range(L):
                if l == LA:
                    with dve.Fori(0, NQ) as q:
                        stats(NQ, q, False)
                if l == L - 1:
                    for j in range(QUAD):
                        dve.wait_ge(out_stored[j], 16 * (l * NQ + 1))
                split(l, 0, 0)
                with dve.If(qh > 0):
                    with dve.Fori(0, qh) as q:
                        for j in range(QUAD):
                            tile(l, q, j)
                for q, h in heavy_quads(dve, qh, nh):
                    for j in range(QUAD):
                        tile(l, q, j, h)
                if l < LA:
                    back(l, NQ - 1, QUAD - 1, (l + 1) * NT - 1)


_INS = ["x", "src", "dst", "L0_gnn_W_l", "L0_gnn_W_r", "L0_gnn_b", "L0_gnn_ln_g", "L0_gnn_ln_b",
        "L1_gnn_Ws_self", "L1_gnn_Ws_neigh", "L1_gnn_bs"]


def kernel(**inputs):
    import numpy as _np
    import concourse.bacc as _bacc
    from concourse import mybir as _mybir
    from concourse.bass_utils import run_bass_kernel_spmd as _run

    nc = _bacc.Bacc("TRN2", target_bir_lowering=False, num_devices=1)
    arrays, args = {}, []
    for name in _INS:
        a = _np.ascontiguousarray(inputs[name])
        arrays[f"in_{name}"] = a
        args.append(nc.dram_tensor(f"in_{name}", a.shape, _mybir.dt.from_np(a.dtype), kind="ExternalInput").ap())
    shape = inputs["x"].shape
    args.append(nc.dram_tensor("out_0", shape, _mybir.dt.float32, kind="ExternalOutput").ap())
    build_gnn(nc, *args)
    r = _run(nc, [arrays], core_ids=[0])
    return r.results[0]["out_0"]
```

```python
import concourse.bass as bass
from concourse import mybir
from contextlib import ExitStack

F32 = mybir.dt.float32
F32R = mybir.dt.float32r
BF16 = mybir.dt.bfloat16
I32 = mybir.dt.int32
ALU = mybir.AluOpType
ACT = mybir.ActivationFunctionType
AX = mybir.AxisListType
ds = bass.ds

P = 128
LN_EPS = 1e-5


def build_gnn(nc, x, src, dst, W_l, W_r, b0, ln_g, ln_b, Ws_self, Ws_neigh, b1, out):
    N, D = x.shape
    E = src.shape[0]
    KC = D // P
    LA, LB = W_l.shape[0], Ws_self.shape[0]
    L = LA + LB
    QUAD = 4
    NQ = -(-N // (QUAD * P))
    NT = NQ * QUAD
    NP = NT * P
    EP = max(p for p in range(1, P + 1) if E % p == 0)
    EC = E // EP
    CB = max(b for b in range(1, 7) if EC % (2 * b) == 0)
    LG = 8
    EK = -(-E // (P * LG)) * LG
    UNIT = 2 * P
    CH = 2 * (NT + E // UNIT + 1)

    FAR = 1 << 20

    node_tab = nc.dram_tensor("node_tab", (NP, 2), F32, kind="Internal").ap()
    comp_tab = nc.dram_tensor("comp_tab", (P * EK, 2), I32, kind="Internal").ap()
    edge_tab = nc.dram_tensor("edge_tab", (P * CH, 4), F32, kind="Internal").ap()
    H = [nc.dram_tensor(f"h{l}", (NP, D), F32, kind="Internal").ap() for l in range(L)]
    x1_dram = nc.dram_tensor("x1", (NP, D), F32, kind="Internal").ap()
    wp = [nc.dram_tensor(f"wp{l}", (P, 4, KC * D), F32, kind="Internal").ap() for l in range(L)]

    ctx = ExitStack()
    with ctx:
        def sb(name, shape, dt):
            return ctx.enter_context(nc.sbuf_tensor(name, shape, dt))

        def sem(name):
            return ctx.enter_context(nc.semaphore(name))

        banks = [ctx.enter_context(nc.psum_tensor(f"bank{i}", [P, 512], F32)) for i in range(8)]

        diff_i = sb("diff_i", [P, P], I32)
        iota_i = sb("iota_i", [P, CH], I32)
        slot_i = sb("slot_i", [P, P], I32)
        nid_i = sb("nid_i", [P, P], I32)
        diff = sb("diff", [P, P], F32)
        iota = sb("iota", [P, CH], F32)
        slot = sb("slot", [P, P], F32)
        nid = sb("nid", [P, P], F32)
        iota_b = sb("iota_b", [P, P], BF16)
        ident = sb("ident", [P, P], F32)
        below = sb("below", [P, P], F32)
        ones = sb("ones", [P, P], F32)
        zeros = sb("zeros", [P, CH], F32)
        ones_row = sb("ones_row", [P, QUAD * EK], F32)
        eps = sb("eps", [P, 1], F32)

        bias = sb("bias", [P, L, D], F32)
        gain = sb("gain", [P, LA, D], F32)
        shift = sb("shift", [P, LA, D], F32)
        bsum = sb("bsum", [P, LA], F32)

        G = sb("G", [P, QUAD, 2, KC, P], F32)
        wraw = G[:, :, :, :, :].rearrange("p (a b) c d k -> p a (b c d k)", a=2) \
            .rearrange("p a (c n) -> p a c n", c=KC)
        wsum = sb("wsum", [P, 2], F32)
        wneg = sb("wneg", [P, 2], F32)
        OUT = sb("OUT", [P, QUAD, D], F32)
        wtmp, wcen = OUT[:, 0:2, :], OUT[:, 2:4, :]
        W = sb("W", [P, 4, KC, D], F32R)

        src_i = sb("src_i", [EP, EC], I32)
        dst_i = sb("dst_i", [EP, EC], I32)
        dhi_i = sb("dhi_i", [EP, EC], I32)
        dlo_i = sb("dlo_i", [EP, EC], I32)
        e_f = sb("e_f", [EP, 8, EC], F32)
        dhi_b = sb("dhi_b", [EP, EC], BF16)
        dlo_b = sb("dlo_b", [EP, EC], BF16)
        self_b = sb("self_b", [EP, EC], BF16)
        ends_i = sb("ends_i", [EP, EC, 2], I32)
        comp_i = sb("comp_i", [EP, EC], I32)
        stage_ci = sb("stage_ci", [EP, 2, CB], I32)
        stage_ce = sb("stage_ce", [EP, 2, CB, 2], I32)
        oh_hi = sb("oh_hi", [EP, 2, CB, NT], BF16)
        oh_lo = sb("oh_lo", [EP, 2, CB, 2, P], BF16)
        nd = sb("nd", [NT, 12, P], F32)
        ntab = sb("ntab", [NT, P, 2], F32)
        nsm = sb("nsm", [P, 16], F32)
        qa_t = sb("qa_t", [P, 2, NT], F32)
        qt_i = sb("qt_i", [P, 3, NT], I32)
        qt_f = sb("qt_f", [P, 2, NT], F32)
        work = sb("work", [P, 5, D], F32)
        HB, T1, T2, SQ = work[:, 0:2, :], work[:, 2, :], work[:, 3, :], work[:, 4, :]
        perm_oh = work[:, :, :].rearrange("p a d -> p (a d)")[:, 0:2 * QUAD * (P + 2 * NT)] \
            .rearrange("p (b c k) -> p b c k", b=2, c=QUAD)
        pos_node_i = sb("pos_node_i", [P, NT], I32)
        pos_read_i = sb("pos_read_i", [P, NT], I32)
        pos_f = sb("pos_f", [P, 2, NT], F32)
        own = sb("own", [P, NT], F32)
        ce_i = sb("ce_i", [P, EK, 2], I32)
        ctab = sb("ctab", [P, EK, 4], F32)
        c_i = sb("c_i", [P, 4, EK], I32)
        c_f = sb("c_f", [P, 8, EK], F32)
        cnt_pb = sb("cnt_pb", [P, NT], F32)
        ub = sb("ub", [P, 7, NT], F32)
        ub_i = sb("ub_i", [P, 2, NT], I32)
        bk_eq = sb("bk_eq", [P, QUAD, EK], F32)
        bk_cum = sb("bk_cum", [P, QUAD, EK], F32)
        bk_sum = sb("bk_sum", [P, EK], F32)
        put_i = sb("put_i", [P, EK], I32)
        put_r = sb("put_r", [P, EK, 4], F32)
        stage_pi = sb("stage_pi", [P, LG], I32)
        stage_pr = sb("stage_pr", [P, LG, 4], F32)
        edges_b = sb("edges_b", [P, CH, 4], F32)
        edge_row = edges_b[:, :, 0].bitcast(I32)
        edge_dw = edges_b[:, :, 1:3]
        scal_i = sb("scal_i", [1, 8], I32)
        unit_i = sb("unit_i", [1, 3, NT], I32)
        small_i = sb("small_i", [P, 2], I32)
        stage_c = sb("stage_c", [P, LG, 2], I32)
        looked = sb("looked", [P, LG, 2, 2], F32)

        X = sb("X", [P, QUAD, KC, P], F32)
        XR = sb("XR", [P, QUAD, D], F32)
        xhi = sb("xhi", [P, 2, KC, P], F32R)
        xlo = sb("xlo", [P, 2, KC, P], F32R)
        vhi = sb("vhi", [P, 2, KC, P], F32R)
        vlo = sb("vlo", [P, 2, KC, P], F32R)
        stat = sb("stat", [P, 2, 4], F32)
        mvb = sb("mvb", [P, 2, QUAD, 6], F32)
        mv = sb("mv", [P, 2, QUAD, 2], F32)
        ms = sb("ms", [P, 2, 3, QUAD], F32)
        ymvb = sb("ymvb", [P, 6], F32)
        ymv = sb("ymv", [P, 2, 2], F32)
        ystat = sb("ystat", [P, 2, 4], F32)
        Y = sb("Y", [P, QUAD, D], F32)
        row_in = [X[:, :, :, :].rearrange("p q c k -> p q (c k)"), XR[:, :, :]]
        row_out = G[:, :, :, :, :].rearrange("p (b a) c d k -> p b (a c) (d k)", b=2)
        S = sb("S", [P, QUAD, 3, P], F32)
        XG = sb("XG", [P, 2, KC, P], F32)
        XS = sb("XS", [P, 2, P], F32)
        stage_i = sb("stage_i", [P, QUAD, 2], I32)
        stage_f = sb("stage_f", [P, QUAD, 5], F32)
        xstage_i = sb("xstage_i", [P, 2], I32)
        xstage_f = sb("xstage_f", [P, 4], F32)
        astage = sb("astage", [P, 2 * QUAD], I32)

        edges_loaded = sem("edges_loaded")
        consts_made = sem("consts_made")
        consts_cast = sem("consts_cast")
        dve_chain = sem("dve_chain")
        cnt_built = sem("cnt_built")
        cnt_used = sem("cnt_used")
        cnt_done = sem("cnt_done")
        cnt_link = sem("cnt_link")
        others_counted = sem("others_counted")
        others_based = sem("others_based")
        heavy_counted = sem("heavy_counted")
        heavy_based = sem("heavy_based")
        tab_built = sem("tab_built")
        tab_stored = sem("tab_stored")
        qa_turned = sem("qa_turned")
        qa_split = sem("qa_split")
        perm_link = sem("perm_link")
        perm_built = sem("perm_built")
        perm_used = sem("perm_used")
        perm_done = sem("perm_done")
        pos_ready = sem("pos_ready")
        comp_zeroed = sem("comp_zeroed")
        comp_placed = sem("comp_placed")
        comp_staged = sem("comp_staged")
        comp_stored = [sem(f"comp_stored{i}") for i in range(2)]
        comp_loaded = sem("comp_loaded")
        comp_ready = sem("comp_ready")
        look_staged = sem("look_staged")
        look_loaded = sem("look_loaded")
        look_done = sem("look_done")
        buck_link = sem("buck_link")
        buck_counted = sem("buck_counted")
        buck_based = sem("buck_based")
        buck2_link = sem("buck2_link")
        edge_zeroed = sem("edge_zeroed")
        edge_placed = sem("edge_placed")
        put_staged = sem("put_staged")
        put_stored = sem("put_stored")
        edges_back = sem("edges_back")
        tables_ready = sem("tables_ready")
        vecs_loaded = sem("vecs_loaded")
        vec_link = sem("vec_link")
        wraw_loaded = sem("wraw_loaded")
        wp_stored = sem("wp_stored")
        w_summed = sem("w_summed")
        w_turned = sem("w_turned")
        w_copied = sem("w_copied")
        w_link = sem("w_link")
        w_centred = sem("w_centred")
        w_high = sem("w_high")
        w_low = sem("w_low")
        W_loaded = [sem(f"W_loaded{i}") for i in range(2)]
        a_staged = sem("a_staged")
        a_loaded = [sem(f"a_loaded{j}") for j in range(2 * QUAD)]
        a_stats = sem("a_stats")
        a_link = sem("a_link")
        a_std = sem("a_std")
        a_norm = sem("a_norm")
        a_out = sem("a_out")
        a_stored = [sem(f"a_stored{j}") for j in range(2 * QUAD)]
        y_staged = sem("y_staged")
        y_loaded = [sem(f"y_loaded{j}") for j in range(QUAD)]
        x1_ready = sem("x1_ready")
        x1_stored = [sem(f"x1_stored{j}") for j in range(QUAD)]
        y_link = sem("y_link")
        y_stats = sem("y_stats")
        y_std = sem("y_std")
        y_norm = sem("y_norm")
        x_loaded = [sem(f"x_loaded{j}") for j in range(QUAD)]
        x1_loaded = [sem(f"x1_loaded{j}") for j in range(QUAD)]
        out_stored = [sem(f"out_stored{j}") for j in range(QUAD)]
        xt_ready = sem("xt_ready")
        xhi_ready = sem("xhi_ready")
        xlo_ready = sem("xlo_ready")
        xr_ready = sem("xr_ready")
        h_ready = sem("h_ready")
        hb_ready = sem("hb_ready")
        sq_ready = sem("sq_ready")
        std_ready = sem("std_ready")
        ln_chain = sem("ln_chain")
        out_ready = sem("out_ready")
        g_staged = sem("g_staged")
        g_loaded = [sem(f"g_loaded{j}") for j in range(QUAD)]
        s_built = sem("s_built")
        v_ready = sem("v_ready")
        vhi_ready = sem("vhi_ready")
        vlo_ready = sem("vlo_ready")
        xg_staged = sem("xg_staged")
        xg_loaded = sem("xg_loaded")
        xs_built = sem("xs_built")
        xg_used = sem("xg_used")
        fin_staged = sem("fin_staged")
        fin_stored = [sem(f"fin_stored{j}") for j in range(QUAD)]

        waits_passed = {e: sem(f"waits_passed_{e}") for e in ("SP", "Pool", "DVE")}

        H_CREDIT = QUAD
        OUT_CREDIT = QUAD
        HB_CREDIT = 2
        V_CREDIT = QUAD

        psT = [banks[0], banks[1]]
        psH = [banks[2], banks[3]]
        psV = banks[4]

        block = ctx.enter_context(nc.Block())

        def wait_alone(eng, name, value):
            eng.wait_ge(name, value)
            eng.sem_inc(waits_passed[eng.engine.name], 1)

        def within(value, low, high):
            return nc.s_assert_within(value, low, high,
                                      skip_runtime_bounds_check_because="the tables and loops keep it there")

        def heavy_quads(eng, qh, nh):
            with eng.Fori(0, nh) as h:
                yield within(qh + h, 0, NQ - 1), h

        def quad_before(q):
            return within(q - 1, 0, NQ - 2)

        def first_heavy(eng):
            return (eng.value_load(scal_i[0:1, 0:1], min_val=0, max_val=NQ - 1),
                    eng.value_load(scal_i[0:1, 5:6], min_val=1, max_val=NQ))

        @block.sync
        def _(sp):
            sp.dma_start(src_i[:, :], src.rearrange("(p c) -> p c", p=EP)).then_inc(edges_loaded, 16)
            sp.dma_start(dst_i[:, :], dst.rearrange("(p c) -> p c", p=EP)).then_inc(edges_loaded, 16)
            for l in range(LA):
                sp.dma_start(bias[:, l, :], b0[l, :].partition_broadcast(P)).then_inc(vecs_loaded, 16)
                sp.dma_start(gain[:, l, :], ln_g[l, :].partition_broadcast(P)).then_inc(vecs_loaded, 16)
                sp.dma_start(shift[:, l, :], ln_b[l, :].partition_broadcast(P)).then_inc(vecs_loaded, 16)
            for l in range(LB):
                sp.dma_start(bias[:, LA + l, :], b1[l, :].partition_broadcast(P)).then_inc(vecs_loaded, 16)
            sp.wait_ge(consts_made, 10)
            sp.dma_start(comp_tab.rearrange("(p c) t -> p (c t)", p=P), zeros[:, 0:2 * EK].bitcast(I32)).then_inc(comp_zeroed, 16)
            for k in range(4):
                sp.dma_start(edge_tab.rearrange("(p c) t -> p (c t)", p=P)[:, k * CH:(k + 1) * CH], zeros[:, :]).then_inc(edge_zeroed, 16)
            sp.wait_ge(tab_built, 1)
            sp.dma_start(node_tab.rearrange("(p c) t -> p (c t)", p=NT),
                         ntab[:, :, :].rearrange("p c t -> p (c t)")).then_inc(tab_stored, 16)
            for l in range(L):
                wa, wb = (W_l[l], W_r[l]) if l < LA else (Ws_neigh[l - LA], Ws_self[l - LA])
                if l:
                    sp.wait_ge(w_low, 8 * l)
                sp.dma_start(wraw[:, 0, :, :], wa.rearrange("(c p) n -> p c n", p=P)).then_inc(wraw_loaded, 16)
                sp.dma_start(wraw[:, 1, :, :], wb.rearrange("(c p) n -> p c n", p=P)).then_inc(wraw_loaded, 16)
                sp.wait_ge(w_low, 8 * (l + 1))
                sp.dma_start(wp[l], W[:, :, :, :].bitcast(F32).rearrange("p m c n -> p m (c n)")).then_inc(wp_stored, 16)
                sp.wait_ge(wp_stored, 16 * (l + 1))

            with sp.Fori(0, NQ // 2) as i:
                for b in range(2):
                    for j in range(QUAD):
                        t = QUAD * (2 * i + b) + j
                        wait_alone(sp, a_out, t + 1)
                        sp.dma_start(H[0][ds(t * P, P), :], row_out[:, b, j, :]).then_inc(a_stored[QUAD * b + j], 16)
            for k in range(2 * QUAD):
                sp.wait_ge(a_stored[k], 16 * NQ // 2)

            def load_tile(l, q, j):
                n = (l * NQ + q) * QUAD + j
                wait_alone(sp, h_ready, n + 1)
                if l < LA:
                    if not (l == 0 and isinstance(q, int) and q == 0):
                        wait_alone(sp, xr_ready, n + 1 - QUAD)
                sp.dma_start(X[:, j, :, :], H[l][ds((QUAD * q + j) * P, P), :]
                             .rearrange("p (c k) -> p c k", c=KC)).then_inc(x_loaded[j], 16)

            def load_x1(q, j):
                wait_alone(sp, out_ready, ((L - 1) * NQ + q) * QUAD + j + 1)
                sp.dma_start(XR[:, j, :], x1_dram[ds((QUAD * q + j) * P, P), :]).then_inc(x1_loaded[j], 16)

            def store_tile(l, q, j):
                n = (l * NQ + q) * QUAD + j
                wait_alone(sp, out_ready, n + 1 + OUT_CREDIT)
                sp.dma_start(H[l + 1][ds((QUAD * q + j) * P, P), :], OUT[:, j, :]).then_inc(out_stored[j], 16)

            def store_x1(q, j):
                wait_alone(sp, x1_ready, QUAD * q + j + 1)
                sp.dma_start(x1_dram[ds((QUAD * q + j) * P, P), :], Y[:, j, :]).then_inc(x1_stored[j], 16)

            for l in range(L):
                if l:
                    sp.wait_ge(h_ready, l * NT + H_CREDIT)
                sp.dma_start(W[:, 0:2, :, :].bitcast(F32).rearrange("p m c n -> p m (c n)"), wp[l][:, 0:2, :]).then_inc(W_loaded[0], 16)
                sp.dma_start(W[:, 2:4, :, :].bitcast(F32).rearrange("p m c n -> p m (c n)"), wp[l][:, 2:4, :]).then_inc(W_loaded[1], 16)
                for j in range(QUAD):
                    if l:
                        sp.wait_ge(out_stored[j], 16 * (l * NQ + 1))
                for j in range(QUAD):
                    load_tile(l, 0, j)
                    if l == L - 1:
                        load_x1(0, j)
                with sp.Fori(0, NQ - 1) as q:
                    for j in range(QUAD):
                        load_tile(l, q + 1, j)
                        if l == L - 1:
                            load_x1(q + 1, j)
                        if l == LA - 1:
                            store_x1(q, j)
                        if l < L - 1:
                            store_tile(l, q, j)
                if l < L - 1:
                    for j in range(QUAD):
                        if l == LA - 1:
                            store_x1(NQ - 1, j)
                        store_tile(l, NQ - 1, j)
                if l == LA - 1:
                    for j in range(QUAD):
                        sp.wait_ge(x1_stored[j], 16 * NQ)

        @block.gpsimd
        def _(pool):
            nc.gpsimd.iota(diff_i[:, :], [[1, P]], 0, -1).then_inc(consts_made, 1)
            nc.gpsimd.iota(iota_i[:, :], [[1, CH]], 0, 0).then_inc(consts_made, 1)
            nc.gpsimd.iota(slot_i[:, :], [[P, P]], 0, 1).then_inc(consts_made, 1)
            nc.gpsimd.iota(nid_i[:, :], [[1, P]], 0, P).then_inc(consts_made, 1)
            nc.gpsimd.memset(ones[:, :], 1.0).then_inc(consts_made, 1)
            nc.gpsimd.memset(zeros[:, :], 0.0).then_inc(consts_made, 1)
            nc.gpsimd.memset(ones_row[:, :], 1.0).then_inc(consts_made, 1)
            nc.gpsimd.memset(eps[:, :], LN_EPS).then_inc(consts_made, 1)
            nc.gpsimd.memset(ctab[:, :, :], 0.0).then_inc(consts_made, 1)
            nc.gpsimd.memset(cnt_pb[:, :], 0.0).then_inc(consts_made, 1)

            pool.wait_ge(comp_placed, 1)
            pool.wait_ge(comp_zeroed, 16)

            def compact(g, b, free):
                if free is not None:
                    wait_alone(pool, comp_stored[b], 16 * CB * free)
                nc.gpsimd.tensor_copy(stage_ci[:, b, :], comp_i[:, ds(g * CB, CB)]).then_inc(comp_staged, 1)
                nc.gpsimd.tensor_copy(stage_ce[:, b, :, :], ends_i[:, ds(g * CB, CB), :]).then_inc(comp_staged, 1)
                wait_alone(pool, comp_staged, 2 * g + 2)
                for c in range(CB):
                    pool.indirect_dma_start(
                        out=comp_tab, out_offset=bass.IndirectOffsetOnAxis(ap=stage_ci[:, b, c:c + 1], axis=0),
                        in_=stage_ce[:, b, c, :], in_offset=None, bounds_check=P * EK - 1,
                        oob_is_err=False).then_inc(comp_stored[b], 16)

            for b in range(2):
                compact(b, b, None)
            with pool.Fori(1, EC // (2 * CB)) as i:
                for b in range(2):
                    compact(2 * i + b, b, i)
            for b in range(2):
                pool.wait_ge(comp_stored[b], 16 * EC // 2)
            pool.dma_start(ce_i[:, :, :].rearrange("p c t -> p (c t)"),
                           comp_tab.rearrange("(p c) t -> p (c t)", p=P)).then_inc(comp_loaded, 16)

            pool.wait_ge(comp_loaded, 16)
            pool.wait_ge(comp_ready, 1)
            pool.wait_ge(tab_stored, 16)
            chunk_groups = pool.value_load(scal_i[0:1, 4:5], min_val=1, max_val=EK // LG)
            with pool.Fori(0, chunk_groups) as g:
                nc.gpsimd.tensor_copy(stage_c[:, :, :], ce_i[:, ds(LG * g, LG), :]).then_inc(look_staged, 1)
                wait_alone(pool, look_staged, g + 1)
                for c in range(LG):
                    for e in range(2):
                        pool.indirect_dma_start(
                            out=looked[:, c, e, :], out_offset=None, in_=node_tab,
                            in_offset=bass.IndirectOffsetOnAxis(ap=stage_c[:, c, e:e + 1], axis=0)).then_inc(look_loaded, 16)
                wait_alone(pool, look_loaded, 32 * LG * (g + 1))
                nc.gpsimd.tensor_copy(ctab[:, ds(LG * g, LG), :].rearrange("p a t -> p (a t)"),
                                      looked[:, :, :, :].rearrange("p c e t -> p (c e t)")).then_inc(look_done, 1)
                wait_alone(pool, look_done, g + 1)

            def gather_x(i, b, free):
                for j in range(QUAD):
                    t = QUAD * (2 * i + b) + j
                    if free:
                        wait_alone(pool, a_out, t + 1 - 2 * QUAD)
                    nc.gpsimd.tensor_copy(astage[:, QUAD * b + j:QUAD * b + j + 1], pos_read_i[:, ds(t, 1)]).then_inc(a_staged, 1)
                    wait_alone(pool, a_staged, t + 1)
                    pool.indirect_dma_start(
                        out=row_in[b][:, j, :], out_offset=None, in_=x,
                        in_offset=bass.IndirectOffsetOnAxis(ap=astage[:, QUAD * b + j:QUAD * b + j + 1], axis=0)
                        ).then_inc(a_loaded[QUAD * b + j], 16)

            pool.wait_ge(pos_ready, 1)
            for b in range(2):
                gather_x(0, b, False)
            with pool.Fori(1, NQ // 2) as i:
                for b in range(2):
                    gather_x(i, b, True)

            pool.wait_ge(edge_placed, 1)
            pool.wait_ge(edge_zeroed, 64)
            with pool.Fori(0, chunk_groups) as g:
                nc.gpsimd.tensor_copy(stage_pi[:, :], put_i[:, ds(LG * g, LG)]).then_inc(put_staged, 1)
                nc.gpsimd.tensor_copy(stage_pr[:, :, 0].bitcast(I32), put_r[:, ds(LG * g, LG), 0].bitcast(I32)).then_inc(put_staged, 1)
                nc.gpsimd.tensor_copy(stage_pr[:, :, 1:4], put_r[:, ds(LG * g, LG), 1:4]).then_inc(put_staged, 1)
                wait_alone(pool, put_staged, 3 * g + 3)
                for c in range(LG):
                    pool.indirect_dma_start(
                        out=edge_tab, out_offset=bass.IndirectOffsetOnAxis(ap=stage_pi[:, c:c + 1], axis=0),
                        in_=stage_pr[:, c, :], in_offset=None, bounds_check=P * CH - 1,
                        oob_is_err=False).then_inc(put_stored, 16)
                wait_alone(pool, put_stored, 16 * LG * (g + 1))
            pool.dma_start(edges_b[:, :, :].rearrange("p c t -> p (c t)"),
                           edge_tab.rearrange("(p c) t -> p (c t)", p=P)).then_inc(edges_back, 16)
            pool.wait_ge(edges_back, 16)
            pool.wait_ge(tables_ready, 1)
            qh, nh = first_heavy(pool)
            extra_all = pool.value_load(scal_i[0:1, 2:3], min_val=0, max_val=E // UNIT + 1)

            def gather_neighbours(l, q, h, j):
                t = QUAD * q + j
                hn = QUAD * (l * nh + h) + j
                unit = pool.value_load(unit_i[0:1, 0, ds(t, 1)], min_val=0, max_val=CH // 2 - 1)
                more = pool.value_load(unit_i[0:1, 1, ds(t, 1)], min_val=0, max_val=E // UNIT)
                extra = pool.value_load(unit_i[0:1, 2, ds(t, 1)], min_val=0, max_val=CH // 2)
                wait_alone(pool, v_ready, hn + 1)
                nc.gpsimd.tensor_copy(stage_i[:, j, :], edge_row[:, ds(2 * unit, 2)]).then_inc(g_staged, 1)
                nc.gpsimd.tensor_copy(stage_f[:, j, 0:4].rearrange("p (a t) -> p a t", a=2),
                                      edge_dw[:, ds(2 * unit, 2), :]).then_inc(g_staged, 1)
                nc.gpsimd.tensor_copy(stage_f[:, j, 4:5], own[:, ds(QUAD * q + j, 1)]).then_inc(g_staged, 1)
                wait_alone(pool, g_staged, 3 * hn + 3)
                for c in range(2):
                    pool.indirect_dma_start(
                        out=G[:, j, c, :, :].rearrange("p c k -> p (c k)"), out_offset=None, in_=H[l],
                        in_offset=bass.IndirectOffsetOnAxis(ap=stage_i[:, j, c:c + 1], axis=0)).then_inc(g_loaded[j], 16)
                for c in range(2):
                    nc.gpsimd.tensor_scalar(S[:, j, c, :], iota[:, 0:P], stage_f[:, j, 2 * c:2 * c + 1],
                                            stage_f[:, j, 2 * c + 1:2 * c + 2], ALU.is_equal, ALU.mult)
                nc.gpsimd.tensor_scalar(S[:, j, 2, :], ident[:, :], stage_f[:, j, 4:5], None,
                                        ALU.mult).then_inc(s_built, 1)
                with pool.If(more > 0):
                    with pool.Fori(0, more) as k:
                        e = l * extra_all + extra + k
                        u = within(unit + k + 1, 1, CH // 2 - 1)
                        wait_alone(pool, xg_used, e + 1)
                        nc.gpsimd.tensor_copy(xstage_i[:, :], edge_row[:, ds(2 * u, 2)]).then_inc(xg_staged, 1)
                        nc.gpsimd.tensor_copy(xstage_f[:, :].rearrange("p (a t) -> p a t", a=2),
                                              edge_dw[:, ds(2 * u, 2), :]).then_inc(xg_staged, 1)
                        wait_alone(pool, xg_staged, 2 * e + 2)
                        for c in range(2):
                            pool.indirect_dma_start(
                                out=XG[:, c, :, :].rearrange("p c k -> p (c k)"), out_offset=None, in_=H[l],
                                in_offset=bass.IndirectOffsetOnAxis(ap=xstage_i[:, c:c + 1], axis=0)).then_inc(xg_loaded, 16)
                        nc.gpsimd.tensor_scalar(XS[:, 0, :], iota[:, 0:P], xstage_f[:, 0:1],
                                                xstage_f[:, 1:2], ALU.is_equal, ALU.mult)
                        nc.gpsimd.tensor_scalar(XS[:, 1, :], iota[:, 0:P], xstage_f[:, 2:3],
                                                xstage_f[:, 3:4], ALU.is_equal, ALU.mult).then_inc(xs_built, 1)

            def gather_x_again(q, j):
                n = QUAD * q + j
                wait_alone(pool, out_ready, (LA - 1) * NT + n + 1)
                with pool.If(q > 0):
                    wait_alone(pool, x1_stored[j], 16 * q)
                nc.gpsimd.tensor_copy(astage[:, j:j + 1], pos_read_i[:, ds(n, 1)]).then_inc(y_staged, 1)
                wait_alone(pool, y_staged, n + 1)
                pool.indirect_dma_start(
                    out=Y[:, j, :], out_offset=None, in_=x,
                    in_offset=bass.IndirectOffsetOnAxis(ap=astage[:, j:j + 1], axis=0)).then_inc(y_loaded[j], 16)

            pool.sem_inc(fin_staged, QUAD)

            def scatter_out(q, j):
                n = QUAD * q + j
                if not isinstance(q, int):
                    n = within(n, 0, NT - 1)
                wait_alone(pool, out_ready, (L - 1) * NT + n + 1 + OUT_CREDIT)
                nc.gpsimd.tensor_copy(astage[:, j:j + 1], pos_node_i[:, ds(n, 1)]).then_inc(fin_staged, 1)
                wait_alone(pool, fin_staged, n + 1 + QUAD)
                pool.indirect_dma_start(
                    out=out, out_offset=bass.IndirectOffsetOnAxis(ap=astage[:, j:j + 1], axis=0),
                    in_=OUT[:, j, :], in_offset=None, bounds_check=N - 1, oob_is_err=False).then_inc(fin_stored[j], 16)

            for l in range(L):
                for j in range(QUAD):
                    if l == 0:
                        pool.wait_ge(a_stored[j], 16 * NQ // 2)
                        pool.wait_ge(a_stored[QUAD + j], 16 * NQ // 2)
                    else:
                        pool.wait_ge(out_stored[j], 16 * (l * NQ + 1))
                if l < L - 1:
                    if l == LA - 1:
                        with pool.If(qh > 0):
                            with pool.Fori(0, qh) as q:
                                for j in range(QUAD):
                                    gather_x_again(q, j)
                    for q, h in heavy_quads(pool, qh, nh):
                        for j in range(QUAD):
                            gather_neighbours(l, q, h, j)
                            if l == LA - 1:
                                gather_x_again(q, j)
                else:
                    with pool.If(qh > 1):
                        with pool.Fori(1, qh) as q:
                            for j in range(QUAD):
                                scatter_out(quad_before(q), j)
                    for q, h in heavy_quads(pool, qh, nh):
                        for j in range(QUAD):
                            gather_neighbours(l, q, h, j)
                        with pool.If(q > 0):
                            for j in range(QUAD):
                                scatter_out(quad_before(q), j)
                    for j in range(QUAD):
                        scatter_out(NQ - 1, j)
            for j in range(QUAD):
                pool.wait_ge(fin_stored[j], 16 * NQ)

        @block.tensor
        def _(pe):
            mm = nc.tensor.matmul
            pe.wait_ge(consts_cast, 1)

            pe.wait_ge(others_counted, 1)
            mm(banks[7][0:EP, 0:1], below[0:EP, 0:EP], e_f[:, 5, EC - 1:EC], start=True, stop=True)
            mm(banks[7][:, 2:3], ones[0:EP, :], e_f[:, 5, EC - 1:EC], start=True, stop=True).then_inc(others_based, 1)

            cnt = banks[5][0:NT, 0:2 * P]
            mm(cnt, zeros[:, 0:NT], zeros[:, 0:2 * P], start=True, stop=False, skip_group_check=True)
            with pe.Fori(0, EC // (2 * CB)) as i:
                for b in range(2):
                    pe.wait_ge(cnt_built, 2 * i + b + 1)
                    for c in range(CB):
                        last = mm(cnt, oh_hi[:, b, c, :], oh_lo[:, b, c, :, :].rearrange("p a k -> p (a k)"),
                                  start=False, stop=False, skip_group_check=True)
                    last.then_inc(cnt_used, 1)
            mm(cnt, zeros[:, 0:NT], zeros[:, 0:2 * P], start=False, stop=True, skip_group_check=True).then_inc(cnt_done, 1)

            pe.wait_ge(heavy_counted, 1)
            mm(banks[6][0:NT, 0:1], below[0:NT, 0:NT], nd[:, 6, P - 1:P], start=True, stop=True)
            mm(banks[6][:, 2:3], ones[0:NT, :], nd[:, 6, P - 1:P], start=True, stop=True).then_inc(heavy_based, 1)

            pe.wait_ge(tab_built, 1)
            mm(banks[0][:, 0:NT], nd[:, 8, :], ident[0:NT, 0:NT], start=True, stop=True)
            mm(banks[0][:, P:P + NT], nd[:, 3, :], ident[0:NT, 0:NT], start=True, stop=True).then_inc(qa_turned, 1)

            perm = banks[1][:, 0:2 * NT]
            mm(perm, zeros[:, 0:P], zeros[:, 0:2 * NT], start=True, stop=False, skip_group_check=True)
            with pe.Fori(0, NQ // 2) as i:
                for b in range(2):
                    pe.wait_ge(perm_built, 2 * i + b + 1)
                    for c in range(QUAD):
                        last = mm(perm, perm_oh[:, b, c, 0:P], perm_oh[:, b, c, P:], start=False, stop=False,
                                  skip_group_check=True)
                    last.then_inc(perm_used, 1)
            mm(perm, zeros[:, 0:P], zeros[:, 0:2 * NT], start=False, stop=True, skip_group_check=True).then_inc(perm_done, 1)

            for l in range(L):
                for k in range(8):
                    m, c = k // KC, k % KC
                    if l < LA:
                        if k == 0:
                            pe.wait_ge(w_summed, l + 1)
                        if 8 * l + k >= 2:
                            pe.wait_ge(w_copied, 8 * l + k - 1)
                        for nb in range(KC):
                            last = nc.tensor.transpose(banks[6 + k % 2][:, nb * P:(nb + 1) * P],
                                                       wraw[:, 1 - m, nb, c * P:(c + 1) * P], ident[:, :])
                        last.then_inc(w_turned, 1)

            pe.wait_ge(buck_counted, 1)
            mm(banks[4][:, 0:NT], below[:, :], cnt_pb[:, :], start=True, stop=True)
            mm(banks[4][:, P:P + NT], ones[:, :], cnt_pb[:, :], start=True, stop=True).then_inc(buck_based, 1)

            pe.wait_ge(tables_ready, 1)
            qh, nh = first_heavy(pe)
            extra_all = pe.value_load(scal_i[0:1, 2:3], min_val=0, max_val=E // UNIT + 1)
            pe.sem_inc(h_ready, H_CREDIT)
            pe.sem_inc(v_ready, V_CREDIT)
            pe.sem_inc(xg_used, 1)

            def turn(l, q, j):
                n = (l * NQ + q) * QUAD + j
                pe.wait_ge(x_loaded[j], 16 * (l * NQ + q) + 16)
                pe.wait_ge(xlo_ready, n + 1)
                for c in range(KC):
                    last = nc.tensor.transpose(psT[j % 2][:, c * P:(c + 1) * P], X[:, j, c, :], ident[:, :])
                last.then_inc(xt_ready, 1)

            def products(h, hi, lo, w, first, final):
                last = None
                for c in range(KC):
                    mm(h, hi[:, c, :], W[:, w, c, :], start=first and c == 0, stop=False, skip_group_check=True)
                    mm(h, hi[:, c, :], W[:, w + 1, c, :], start=False, stop=False, skip_group_check=True)
                    last = mm(h, lo[:, c, :], W[:, w, c, :], start=False, stop=final and c == KC - 1,
                              skip_group_check=True)
                return last

            def tile(l, q, j, h=None):
                n = (l * NQ + q) * QUAD + j
                if j < QUAD - 1:
                    turn(l, q, j + 1)
                else:
                    with pe.If(q < NQ - 1):
                        turn(l, within(q + 1, 1, NQ - 1), 0)
                if h is not None:
                    t = QUAD * q + j
                    hq = l * nh + h
                    hn = QUAD * hq + j
                    more = pe.value_load(unit_i[0:1, 1, ds(t, 1)], min_val=0, max_val=E // UNIT)
                    extra = pe.value_load(unit_i[0:1, 2, ds(t, 1)], min_val=0, max_val=CH // 2)
                    pe.wait_ge(g_loaded[j], 32 * hq + 32)
                    pe.wait_ge(s_built, hn + 1)
                    for c in range(2):
                        for f in range(KC):
                            mm(psV[:, f * P:(f + 1) * P], G[:, j, c, f, :], S[:, j, c, :],
                               start=c == 0 and f == 0, stop=False, skip_group_check=True)
                    with pe.If(more > 0):
                        with pe.Fori(0, more) as k:
                            e = l * extra_all + extra + k
                            pe.wait_ge(xg_loaded, 32 * e + 32)
                            pe.wait_ge(xs_built, e + 1)
                            for c in range(2):
                                for f in range(KC):
                                    last = mm(psV[:, f * P:(f + 1) * P], XG[:, c, f, :], XS[:, c, :],
                                              start=False, stop=False, skip_group_check=True)
                            last.then_inc(xg_used, 1)
                    for f in range(KC):
                        last = mm(psV[:, f * P:(f + 1) * P], X[:, j, f, :], S[:, j, 2, :],
                                  start=False, stop=True, skip_group_check=True)
                    last.then_inc(v_ready, 1)
                pe.wait_ge(xlo_ready, n + 1 + 2)
                pe.wait_ge(hb_ready, n + 1)
                last = products(psH[j % 2][:, :], xhi[:, j % 2], xlo[:, j % 2], 0, True, h is None)
                if h is not None:
                    pe.wait_ge(W_loaded[1], 16 * (l + 1))
                    pe.wait_ge(vlo_ready, hn + 1)
                    last = products(psH[j % 2][:, :], vhi[:, j % 2], vlo[:, j % 2], 2, False, True)
                last.then_inc(h_ready, 1)

            for l in range(L):
                turn(l, 0, 0)
                pe.wait_ge(W_loaded[0], 16 * (l + 1))
                with pe.If(qh > 0):
                    with pe.Fori(0, qh) as q:
                        for j in range(QUAD):
                            tile(l, q, j)
                for q, h in heavy_quads(pe, qh, nh):
                    for j in range(QUAD):
                        tile(l, q, j, h)

        @block.scalar
        def _(act):
            for l in range(L):
                for k in range(8):
                    m, c = k // KC, k % KC
                    i = 8 * l + k
                    if l < LA:
                        act.wait_ge(w_turned, i + 1)
                        if i >= 2:
                            act.wait_ge(w_low, i - 1)
                        nc.scalar.activation(wtmp[:, k % 2, :], banks[6 + k % 2][:, :], ACT.Copy,
                                             accum_out=wsum[:, k % 2:k % 2 + 1]).then_inc(w_copied, 1)
                        act.wait_ge(w_centred, i + 1)
                        if l and k == 0:
                            act.wait_ge(wp_stored, 16 * l)
                        nc.scalar.copy(W[:, 2 * m, c, :], wcen[:, k % 2, :]).then_inc(w_high, 1)
                    else:
                        if k == 0:
                            act.wait_ge(w_summed, l + 1)
                            act.wait_ge(wp_stored, 16 * l)
                        nc.scalar.copy(W[:, 2 * m, c, :], wraw[:, 1 - m, c, :]).then_inc(w_high, 1)

            def normalise(i, b, free):
                s = 2 * i + b
                act.wait_ge(a_stats, s + 1)
                nc.scalar.activation(ms[:, b, 0, :], mv[:, b, :, 1], ACT.Sqrt, bias=eps[:, 0:1]).then_inc(a_std, 1)
                act.wait_ge(a_norm, s + 1)
                for j in range(QUAD):
                    if free:
                        act.wait_ge(a_stored[QUAD * b + j], 16 * i)
                    nc.scalar.activation(row_out[:, b, j, :], row_in[b][:, j, :], ACT.Relu, bias=ms[:, b, 2, j:j + 1],
                                         scale=ms[:, b, 1, j:j + 1]).then_inc(a_out, 1)

            for b in range(2):
                normalise(0, b, False)
            with act.Fori(1, NQ // 2) as i:
                for b in range(2):
                    normalise(i, b, True)

            act.wait_ge(tables_ready, 1)
            qh, nh = first_heavy(act)
            act.sem_inc(out_ready, OUT_CREDIT)
            for j in range(QUAD):
                act.sem_inc(out_stored[j], 16)

            def split(l, q, j):
                n = (l * NQ + q) * QUAD + j
                act.wait_ge(xt_ready, n + 1)
                act.wait_ge(h_ready, n + 1 + H_CREDIT - 2)
                nc.scalar.copy(xhi[:, j % 2, :, :].rearrange("p c k -> p (c k)"), psT[j % 2][:, :]).then_inc(xhi_ready, 1)
                if l < LA:
                    act.wait_ge(out_ready, n + 1)
                    nc.scalar.copy(XR[:, j, :], X[:, j, :, :].rearrange("p c k -> p (c k)")).then_inc(xr_ready, 1)

            def normalise_x1(q, j, m):
                act.wait_ge(y_norm, m + 1 + 2)
                act.wait_ge(out_stored[j], 16 * ((LA - 1) * NQ + q) + 16)
                nc.scalar.activation(OUT[:, j, :], Y[:, j, :], ACT.Relu, bias=ystat[:, j % 2, 2:3],
                                     scale=ystat[:, j % 2, 1:2]).then_inc(out_ready, 1)

            def back(l, q, j, n):
                act.wait_ge(hb_ready, n + 1 + HB_CREDIT)
                if l < LA:
                    nc.scalar.activation(SQ, HB[:, j % 2, :], ACT.Square,
                                         accum_out=stat[:, j % 2, 0:1]).then_inc(sq_ready, 1)
                    act.wait_ge(sq_ready, n + 1)
                    nc.scalar.activation(stat[:, j % 2, 1:2], stat[:, j % 2, 0:1], ACT.Sqrt,
                                         bias=eps[:, 0:1], scale=1.0 / D).then_inc(std_ready, 1)
                    if l == LA - 1:
                        m = n - (LA - 1) * NT
                        act.wait_ge(y_stats, m + 1)
                        nc.scalar.activation(ystat[:, j % 2, 0:1], ymv[:, j % 2, 1:2], ACT.Sqrt,
                                             bias=eps[:, 0:1]).then_inc(y_std, 1)
                elif l < L - 1:
                    act.wait_ge(out_stored[j], 16 * (l * NQ + q) + 16)
                    nc.scalar.activation(OUT[:, j, :], HB[:, j % 2, :], ACT.Relu).then_inc(out_ready, 1)

            def tile(l, q, j, h=None):
                if h is not None:
                    hn = QUAD * (l * nh + h) + j
                    n = (l * NQ + q) * QUAD + j
                    act.wait_ge(v_ready, hn + 1 + V_CREDIT)
                    act.wait_ge(h_ready, n + 1 + H_CREDIT - 2)
                    nc.scalar.copy(vhi[:, j % 2, :, :].rearrange("p c k -> p (c k)"), psV[:, :]).then_inc(vhi_ready, 1)
                if j < QUAD - 1:
                    split(l, q, j + 1)
                else:
                    with act.If(q < NQ - 1):
                        split(l, within(q + 1, 1, NQ - 1), 0)
                if l == LA - 1:
                    if j >= 2:
                        normalise_x1(q, j - 2, QUAD * q + j - 2)
                    else:
                        with act.If(q > 0):
                            normalise_x1(quad_before(q), QUAD + j - 2, QUAD * q + j - 2)
                if l < L - 1:
                    if j:
                        back(l, q, j - 1, (l * NQ + q) * QUAD + j - 1)
                    else:
                        with act.If(q > 0):
                            back(l, quad_before(q), QUAD - 1, (l * NQ + q) * QUAD - 1)

            for l in range(L):
                split(l, 0, 0)
                with act.If(qh > 0):
                    with act.Fori(0, qh) as q:
                        for j in range(QUAD):
                            tile(l, q, j)
                for q, h in heavy_quads(act, qh, nh):
                    for j in range(QUAD):
                        tile(l, q, j, h)
                if l == LA - 1:
                    normalise_x1(NQ - 1, QUAD - 2, NT - 2)
                if l < L - 1:
                    back(l, NQ - 1, QUAD - 1, (l + 1) * NT - 1)
                if l == LA - 1:
                    normalise_x1(NQ - 1, QUAD - 1, NT - 1)

        @block.vector
        def _(dve):
            v = nc.vector
            chain = [0]

            def link(ins):
                chain[0] += 1
                ins.then_inc(dve_chain, 1)
                dve.wait_ge(dve_chain, chain[0])

            def bc_in(ap, n):
                return ap.unsqueeze(2).broadcast_to([ap.shape[0], ap.shape[1], n])

            def bc_out(ap, n):
                return ap.unsqueeze(1).broadcast_to([ap.shape[0], n, ap.shape[1]])

            dve.wait_ge(consts_made, 10)
            v.tensor_copy(iota[:, :], iota_i[:, :])
            v.tensor_copy(slot[:, :], slot_i[:, :])
            v.tensor_copy(nid[:, :], nid_i[:, :])
            v.tensor_copy(iota_b[:, :], iota_i[:, 0:P])
            link(v.tensor_copy(diff[:, :], diff_i[:, :]))
            v.tensor_scalar(ident[:, :], diff[:, :], 0.0, None, ALU.is_equal)
            v.tensor_scalar(below[:, :], diff[:, :], 0.0, None, ALU.is_gt).then_inc(consts_cast, 1)

            sf, df, dhif, dlof, ns, cum, cp, tmp = (e_f[:, k, :] for k in range(8))
            dve.wait_ge(edges_loaded, 32)
            v.tensor_copy(sf, src_i[:, :])
            v.tensor_copy(df, dst_i[:, :])
            v.tensor_scalar(dhi_i[:, :], dst_i[:, :], 7, None, ALU.arith_shift_right)
            link(v.tensor_scalar(dlo_i[:, :], dst_i[:, :], P - 1, None, ALU.bitwise_and))
            v.tensor_copy(dhi_b[:, :], dhi_i[:, :])
            v.tensor_copy(dlo_b[:, :], dlo_i[:, :])
            v.tensor_tensor(self_b[:, :], sf, df, ALU.is_equal)
            v.tensor_copy(ends_i[:, :, 0], src_i[:, :])
            v.tensor_copy(ends_i[:, :, 1], dst_i[:, :])
            link(v.tensor_tensor(ns, sf, df, ALU.not_equal))
            v.tensor_tensor_scan(cum, ones[0:EP, 0:EC], ns, 0.0, ALU.mult, ALU.add).then_inc(others_counted, 1)
            dve.wait_ge(others_based, 1)
            link(v.tensor_copy(nsm[0:EP, 4:5], banks[7][0:EP, 0:1]))
            link(v.tensor_copy(nsm[:, 5:6], banks[7][:, 2:3]))
            link(v.tensor_scalar(cp, cum, nsm[0:EP, 4:5], -1.0, ALU.add, ALU.add))
            link(v.tensor_tensor(cp, cp, ns, ALU.mult))
            link(v.tensor_copy(dhi_i[:, :], cp))
            link(v.tensor_scalar(dlo_i[:, :], dhi_i[:, :], P - 1, None, ALU.bitwise_and))
            link(v.tensor_scalar(dhi_i[:, :], dhi_i[:, :], 7, None, ALU.arith_shift_right))
            v.tensor_copy(dlof, dlo_i[:, :])
            link(v.tensor_copy(dhif, dhi_i[:, :]))
            link(v.scalar_tensor_tensor(cp, dlof, float(EK), dhif, ALU.mult, ALU.add))
            link(v.scalar_tensor_tensor(cp, cp, -float(FAR), ns, ALU.add, ALU.mult))
            v.tensor_scalar(comp_i[:, :], cp, float(FAR), None, ALU.add).then_inc(comp_placed, 1)
            link(v.tensor_scalar(nsm[0:1, 6:7], nsm[0:1, 5:6], float(P * LG - 1), None, ALU.add))
            link(v.tensor_copy(scal_i[0:1, 3:4], nsm[0:1, 6:7]))
            link(v.tensor_scalar(scal_i[0:1, 3:4], scal_i[0:1, 3:4], 10, None, ALU.arith_shift_right))
            v.tensor_scalar(scal_i[0:1, 4:5], scal_i[0:1, 3:4], 1.0, None, ALU.max).then_inc(comp_ready, 1)

            def count_step(i, b, static):
                if not static:
                    dve.wait_ge(cnt_used, i - 1)
                cols = ds(i * CB, CB)
                v.tensor_tensor(oh_hi[:, b, :, :], bc_out(iota_b[0:EP, 0:NT], CB), bc_in(dhi_b[:, cols], NT), ALU.is_equal)
                v.tensor_tensor(oh_lo[:, b, :, 0, :], bc_out(iota_b[0:EP, :], CB), bc_in(dlo_b[:, cols], P),
                                ALU.is_equal).then_inc(cnt_link, 1)
                dve.wait_ge(cnt_link, i + 1)
                v.tensor_tensor(oh_lo[:, b, :, 1, :], oh_lo[:, b, :, 0, :], bc_in(self_b[:, cols], P),
                                ALU.mult).then_inc(cnt_built, 1)

            for b in range(2):
                count_step(b, b, True)
            with dve.Fori(1, EC // (2 * CB)) as i:
                for b in range(2):
                    count_step(2 * i + b, b, False)

            cntf, loops, inv, owna, heavy, other, hcum, hexc, pos, none, okn, t0 = (nd[:, k, :] for k in range(12))
            dve.wait_ge(cnt_done, 1)
            v.tensor_copy(loops, banks[5][0:NT, P:2 * P])
            link(v.tensor_copy(cntf, banks[5][0:NT, 0:P]))
            link(v.tensor_scalar(t0, cntf, 1.0, None, ALU.max))
            v.tensor_scalar(none, cntf, 0.5, None, ALU.is_lt)
            v.tensor_tensor(other, cntf, loops, ALU.not_equal)
            v.tensor_scalar(okn, nid[0:NT, :], float(N), None, ALU.is_lt)
            link(v.reciprocal(inv, t0))
            link(v.tensor_tensor(heavy, none, other, ALU.max))
            link(v.tensor_tensor(heavy, heavy, okn, ALU.mult))
            link(v.tensor_tensor(t0, loops, inv, ALU.mult))
            link(v.tensor_scalar(t0, t0, -1.0, None, ALU.add))
            link(v.tensor_tensor(owna, t0, heavy, ALU.mult))
            v.tensor_tensor_scan(hcum, ones[0:NT, :], heavy, 0.0, ALU.mult, ALU.add).then_inc(heavy_counted, 1)
            dve.wait_ge(heavy_based, 1)
            link(v.tensor_copy(nsm[0:NT, 0:1], banks[6][0:NT, 0:1]))
            link(v.tensor_copy(nsm[:, 1:2], banks[6][:, 2:3]))
            link(v.tensor_tensor(hexc, hcum, heavy, ALU.subtract))
            link(v.tensor_scalar(hexc, hexc, nsm[0:NT, 0:1], None, ALU.add))
            link(v.tensor_scalar(nsm[:, 2:3], nsm[:, 1:2], -1.0, float(NP), ALU.mult, ALU.add))
            link(v.tensor_tensor(pos, nid[0:NT, :], hexc, ALU.subtract))
            link(v.tensor_scalar(t0, hexc, nsm[0:NT, 2:3], None, ALU.add))
            link(v.tensor_tensor(t0, t0, pos, ALU.subtract))
            link(v.tensor_tensor(t0, t0, heavy, ALU.mult))
            link(v.tensor_tensor(pos, pos, t0, ALU.add))
            v.tensor_copy(ntab[:, :, 0], pos)
            v.tensor_copy(ntab[:, :, 1], inv).then_inc(tab_built, 1)
            link(v.tensor_copy(small_i[:, 0:1], nsm[:, 2:3]))
            link(v.tensor_scalar(small_i[:, 1:2], small_i[:, 0:1], 9, None, ALU.arith_shift_right))
            link(v.tensor_scalar(nsm[:, 3:4], small_i[:, 1:2], float(NQ - 1), None, ALU.min))
            link(v.tensor_scalar(nsm[:, 9:10], nsm[:, 3:4], float(QUAD), None, ALU.mult))
            link(v.tensor_copy(scal_i[0:1, 0:1], nsm[0:1, 3:4]))
            link(v.tensor_scalar(nsm[:, 11:12], nsm[:, 3:4], -1.0, float(NQ), ALU.mult, ALU.add))
            link(v.tensor_copy(scal_i[0:1, 5:6], nsm[0:1, 11:12]))

            dve.wait_ge(qa_turned, 1)
            v.tensor_copy(qa_t[:, 1, :], banks[0][:, P:P + NT])
            v.tensor_copy(qt_i[:, 0, :], banks[0][:, 0:NT])
            link(v.tensor_copy(qa_t[:, 0, :], banks[0][:, 0:NT]))
            v.tensor_scalar(qt_i[:, 1, :], qt_i[:, 0, :], 7, None, ALU.arith_shift_right)
            link(v.tensor_scalar(qt_i[:, 2, :], qt_i[:, 0, :], P - 1, None, ALU.bitwise_and))
            v.tensor_copy(qt_f[:, 0, :], qt_i[:, 1, :])
            link(v.tensor_copy(qt_f[:, 1, :], qt_i[:, 2, :]))

            def perm_step(i, b, static):
                if not static:
                    dve.wait_ge(perm_used, i - 1)
                cols = ds(i * QUAD, QUAD)
                oh = perm_oh[:, b, :, :]
                v.tensor_tensor(oh[:, :, 0:P], bc_out(iota[:, 0:P], QUAD), bc_in(qt_f[:, 1, cols], P), ALU.is_equal)
                v.tensor_tensor(oh[:, :, P:P + NT], bc_out(iota[:, 0:NT], QUAD), bc_in(qt_f[:, 0, cols], NT),
                                ALU.is_equal).then_inc(perm_link, 1)
                dve.wait_ge(perm_link, 2 * i + 1)
                v.tensor_tensor(oh[:, :, P + NT:], oh[:, :, P:P + NT], bc_in(qa_t[:, 1, cols], NT),
                                ALU.mult).then_inc(perm_link, 1)
                dve.wait_ge(perm_link, 2 * i + 2)
                v.tensor_tensor(oh[:, :, P:P + NT], oh[:, :, P:P + NT], bc_in(slot[:, cols], NT),
                                ALU.mult).then_inc(perm_built, 1)

            for b in range(2):
                perm_step(b, b, True)
            with dve.Fori(1, NQ // 2) as i:
                for b in range(2):
                    perm_step(2 * i + b, b, False)
            dve.wait_ge(perm_done, 1)
            v.tensor_copy(own[:, :], banks[1][:, NT:2 * NT])
            v.tensor_copy(pos_node_i[:, :], banks[1][:, 0:NT])
            link(v.tensor_copy(pos_f[:, 0, :], banks[1][:, 0:NT]))
            v.tensor_scalar(pos_read_i[:, :], pos_f[:, 0, :], float(N - 1), None, ALU.min).then_inc(pos_ready, 1)

            dve.wait_ge(vecs_loaded, 16 * (3 * LA + LB))
            link(v.tensor_reduce(bsum[:, :], bias[:, 0:LA, :], AX.X, ALU.add))
            link(v.tensor_scalar(bsum[:, :], bsum[:, :], -1.0 / D, None, ALU.mult))
            for l in range(LA):
                link(v.tensor_scalar(bias[:, l, :], bias[:, l, :], bsum[:, l:l + 1], None, ALU.add))

            for l in range(L):
                dve.wait_ge(wraw_loaded, 32 * (l + 1))
                v.tensor_tensor(wraw[:, 1, :, :].rearrange("p c n -> p (c n)"),
                                wraw[:, 1, :, :].rearrange("p c n -> p (c n)"),
                                wraw[:, 0, :, :].rearrange("p c n -> p (c n)"), ALU.add).then_inc(w_summed, 1)
                for k in range(8):
                    m, c = k // KC, k % KC
                    i = 8 * l + k
                    if l < LA:
                        dve.wait_ge(w_copied, i + 1)
                        link(v.tensor_scalar(wneg[:, k % 2:k % 2 + 1], wsum[:, k % 2:k % 2 + 1], -1.0 / D, None, ALU.mult))
                        v.tensor_scalar(wcen[:, k % 2, :], wtmp[:, k % 2, :], wneg[:, k % 2:k % 2 + 1], None,
                                        ALU.add).then_inc(w_centred, 1)
                        full = wcen[:, k % 2, :]
                    else:
                        full = wraw[:, 1 - m, c, :]
                    dve.wait_ge(w_high, i + 1)
                    v.tensor_tensor(W[:, 2 * m + 1, c, :], full, W[:, 2 * m, c, :].bitcast(F32),
                                    ALU.subtract).then_inc(w_low, 1)

            def stats(i, b, free):
                s = 2 * i + b
                if free:
                    dve.wait_ge(a_out, QUAD * (s - 1))
                for j in range(QUAD):
                    dve.wait_ge(a_loaded[QUAD * b + j], 16 * i + 16)
                    v.bn_stats(mvb[:, b, j, :], row_in[b][:, j, :]).then_inc(a_link, 1)
                wait_alone(dve, a_link, (QUAD + 1) * s + QUAD)
                for j in range(QUAD):
                    last = v.bn_aggr(mv[:, b, j, :], mvb[:, b, j, :])
                last.then_inc(a_stats, 1)
                dve.wait_ge(a_std, s + 1)
                v.reciprocal(ms[:, b, 1, :], ms[:, b, 0, :]).then_inc(a_link, 1)
                dve.wait_ge(a_link, (QUAD + 1) * s + QUAD + 1)
                v.scalar_tensor_tensor(ms[:, b, 2, :], mv[:, b, :, 0], -1.0, ms[:, b, 1, :], ALU.mult,
                                       ALU.mult).then_inc(a_norm, 1)

            for b in range(2):
                stats(0, b, False)
            with dve.Fori(1, NQ // 2) as i:
                for b in range(2):
                    stats(i, b, True)

            qh0, nh0 = first_heavy(dve)
            groups = dve.value_load(scal_i[0:1, 4:5], min_val=1, max_val=EK // LG)
            dve.wait_ge(look_done, groups)
            c_bk, c_lo, c_pl, c_ph, c_pos, c_ok, c_put, _c = (c_f[:, k, :] for k in range(8))
            link(v.tensor_scalar(c_ok, slot[:, 0:EK], nsm[:, 5:6], None, ALU.is_lt))
            link(v.tensor_copy(c_i[:, 0, :], ctab[:, :, 2]))
            link(v.tensor_scalar(c_i[:, 1, :], c_i[:, 0, :], 7, None, ALU.arith_shift_right))
            link(v.tensor_scalar(c_i[:, 2, :], c_i[:, 0, :], P - 1, None, ALU.bitwise_and))
            link(v.tensor_copy(c_lo, c_i[:, 2, :]))
            link(v.tensor_copy(c_bk, c_i[:, 1, :]))
            link(v.tensor_scalar(c_bk, c_bk, 1.0, None, ALU.add))
            link(v.tensor_tensor(c_bk, c_bk, c_ok, ALU.mult))
            link(v.tensor_scalar(c_bk, c_bk, -1.0, None, ALU.add))
            def in_buckets(k):
                b = within(k + qh0, 0, NQ - 1)
                v.tensor_tensor(bk_eq[:, :, :], bc_in(iota[:, ds(QUAD * b, QUAD)], EK), bc_out(c_bk, QUAD),
                                ALU.is_equal).then_inc(buck_link, 1)
                return ds(QUAD * b, QUAD), ds(QUAD * b, 1)

            with dve.Fori(0, nh0) as k:
                four, _ = in_buckets(k)
                dve.wait_ge(buck_link, 2 * k + 1)
                v.tensor_reduce(cnt_pb[:, four], bk_eq[:, :, :], AX.X, ALU.add).then_inc(buck_link, 1)
                dve.wait_ge(buck_link, 2 * k + 2)
            v.tensor_scalar(ub[:, 5, :], cnt_pb[:, :], 0.0, None, ALU.add).then_inc(buck_counted, 1)
            dve.wait_ge(buck_based, 1)
            tot, units, ucum, base, isheavy, _spare, before = (ub[:, k, :] for k in range(7))
            link(v.tensor_copy(tot, banks[4][:, P:P + NT]))
            link(v.tensor_scalar(ub[:, 5, :], tot, float(UNIT - 1), None, ALU.add))
            link(v.tensor_copy(ub_i[:, 0, :], ub[:, 5, :]))
            link(v.tensor_scalar(ub_i[:, 0, :], ub_i[:, 0, :], 8, None, ALU.arith_shift_right))
            link(v.tensor_copy(units, ub_i[:, 0, :]))
            link(v.tensor_scalar(units, units, 1.0, None, ALU.max))
            link(v.tensor_scalar(isheavy, iota[:, 0:NT], nsm[:, 9:10], None, ALU.is_ge))
            link(v.tensor_tensor(units, units, isheavy, ALU.mult))
            link(v.tensor_tensor_scan(ucum, ones[:, 0:NT], units, 0.0, ALU.mult, ALU.add))
            link(v.tensor_tensor(ucum, ucum, units, ALU.subtract))
            link(v.tensor_scalar(base, ucum, float(UNIT), None, ALU.mult))
            link(v.tensor_tensor(base, base, banks[4][:, 0:NT], ALU.add))
            link(v.tensor_tensor_scan(before, ones[:, 0:NT], cnt_pb[:, :], 0.0, ALU.mult, ALU.add))
            link(v.tensor_tensor(before, before, cnt_pb[:, :], ALU.subtract))
            link(v.tensor_tensor(base, base, before, ALU.subtract))
            link(v.memset(c_pos, 0.0))
            heavy_counts = dve.value_load(scal_i[0:1, 5:6], min_val=1, max_val=NQ)

            def in_buckets_again(k):
                b = within(k + qh0, 0, NQ - 1)
                v.tensor_tensor(bk_eq[:, :, :], bc_in(iota[:, ds(QUAD * b, QUAD)], EK), bc_out(c_bk, QUAD),
                                ALU.is_equal).then_inc(buck2_link, 1)
                return ds(QUAD * b, QUAD), ds(QUAD * b, 1)

            with dve.Fori(0, heavy_counts) as k:
                four, one = in_buckets_again(k)
                dve.wait_ge(buck2_link, 6 * k + 1)
                v.tensor_tensor_scan(bk_cum[:, :, :].rearrange("p b c -> p (b c)"), ones_row[:, :],
                                     bk_eq[:, :, :].rearrange("p b c -> p (b c)"), before[:, one],
                                     ALU.mult, ALU.add).then_inc(buck2_link, 1)
                dve.wait_ge(buck2_link, 6 * k + 2)
                v.tensor_tensor(bk_cum[:, :, :], bk_cum[:, :, :], bc_in(base[:, four], EK), ALU.add).then_inc(buck2_link, 1)
                dve.wait_ge(buck2_link, 6 * k + 3)
                v.tensor_tensor(bk_cum[:, :, :], bk_cum[:, :, :], bk_eq[:, :, :], ALU.mult).then_inc(buck2_link, 1)
                dve.wait_ge(buck2_link, 6 * k + 4)
                v.tensor_reduce(bk_sum[:, :], bk_cum[:, :, :].rearrange("p b c -> p c b"), AX.X, ALU.add).then_inc(buck2_link, 1)
                dve.wait_ge(buck2_link, 6 * k + 5)
                v.tensor_tensor(c_pos, c_pos, bk_sum[:, :], ALU.add).then_inc(buck2_link, 1)
                dve.wait_ge(buck2_link, 6 * k + 6)
            link(v.tensor_scalar(c_pos, c_pos, -1.0, 0.0, ALU.add, ALU.max))
            link(v.tensor_copy(c_i[:, 0, :], c_pos))
            v.tensor_scalar(c_i[:, 1, :], c_i[:, 0, :], 7, None, ALU.arith_shift_right)
            link(v.tensor_scalar(c_i[:, 2, :], c_i[:, 0, :], P - 1, None, ALU.bitwise_and))
            v.tensor_copy(c_ph, c_i[:, 1, :])
            link(v.tensor_copy(c_pl, c_i[:, 2, :]))
            link(v.scalar_tensor_tensor(c_put, c_pl, float(CH), c_ph, ALU.mult, ALU.add))
            link(v.scalar_tensor_tensor(c_put, c_put, -float(FAR), c_ok, ALU.add, ALU.mult))
            v.tensor_scalar(put_i[:, :], c_put, float(FAR), None, ALU.add)
            v.tensor_copy(put_r[:, :, 0].bitcast(I32), ctab[:, :, 0])
            v.tensor_copy(put_r[:, :, 1], c_lo)
            v.tensor_copy(put_r[:, :, 2], ctab[:, :, 3])
            v.memset(put_r[:, :, 3], 0.0).then_inc(edge_placed, 1)
            link(v.tensor_copy(unit_i[0:1, 0, :], ucum[0:1, :]))
            link(v.tensor_scalar(unit_i[0:1, 1, :], units[0:1, :], -1.0, 0.0, ALU.add, ALU.max))
            link(v.tensor_tensor(tot[0:1, :], ucum[0:1, :], iota[0:1, 0:NT], ALU.subtract))
            link(v.tensor_scalar(tot[0:1, :], tot[0:1, :], nsm[0:1, 9:10], 0.0, ALU.add, ALU.max))
            link(v.tensor_copy(unit_i[0:1, 2, :], tot[0:1, :]))
            link(v.tensor_tensor(nsm[0:1, 10:11], tot[0:1, NT - 1:NT], units[0:1, NT - 1:NT], ALU.add))
            link(v.tensor_scalar(nsm[0:1, 10:11], nsm[0:1, 10:11], -1.0, None, ALU.add))
            v.tensor_copy(scal_i[0:1, 2:3], nsm[0:1, 10:11]).then_inc(tables_ready, 1)
            dve.wait_ge(tables_ready, 1)
            qh, nh = first_heavy(dve)
            dve.sem_inc(xlo_ready, 2)
            dve.sem_inc(hb_ready, HB_CREDIT)
            dve.sem_inc(y_link, 3)
            dve.sem_inc(y_norm, 2)
            dve.sem_inc(ln_chain, 3)

            def split(l, q, j):
                n = (l * NQ + q) * QUAD + j
                dve.wait_ge(xhi_ready, n + 1)
                v.tensor_tensor(xlo[:, j % 2, :, :].rearrange("p c k -> p (c k)"), psT[j % 2][:, :],
                                xhi[:, j % 2, :, :].bitcast(F32).rearrange("p c k -> p (c k)"),
                                ALU.subtract).then_inc(xlo_ready, 1)

            def back(l, q, j, n):
                dve.wait_ge(std_ready, n + 1)
                v.reciprocal(stat[:, j % 2, 2:3], stat[:, j % 2, 1:2]).then_inc(ln_chain, 1)
                dve.wait_ge(ln_chain, 3 * n + 4)
                v.scalar_tensor_tensor(T1, HB[:, j % 2, :], stat[:, j % 2, 2:3], gain[:, l, :],
                                       ALU.mult, ALU.mult).then_inc(ln_chain, 1)
                dve.wait_ge(ln_chain, 3 * n + 5)
                v.tensor_tensor(T2, T1, shift[:, l, :], ALU.add).then_inc(ln_chain, 1)
                dve.wait_ge(ln_chain, 3 * n + 6)
                dve.wait_ge(xr_ready, n + 1)
                if l < LA - 1:
                    dve.wait_ge(out_stored[j], 16 * (l * NQ + q) + 16)
                    v.scalar_tensor_tensor(OUT[:, j, :], T2, 0.0, XR[:, j, :], ALU.max, ALU.add).then_inc(out_ready, 1)
                    return
                m = n - (LA - 1) * NT
                v.scalar_tensor_tensor(T1, T2, 0.0, XR[:, j, :], ALU.max, ALU.add).then_inc(y_link, 1)
                dve.wait_ge(y_link, 3 * m + 4)
                wait_alone(dve, y_loaded[j], 16 * q + 16)
                v.tensor_tensor(Y[:, j, :], Y[:, j, :], T1, ALU.add).then_inc(x1_ready, 1)
                dve.wait_ge(x1_ready, m + 1)
                v.bn_stats(ymvb[:, :], Y[:, j, :]).then_inc(y_link, 1)
                wait_alone(dve, y_link, 3 * m + 5)
                v.bn_aggr(ymv[:, j % 2, :], ymvb[:, :]).then_inc(y_stats, 1)

            def x1_scale(j, m):
                dve.wait_ge(y_std, m + 1)
                v.reciprocal(ystat[:, j % 2, 1:2], ystat[:, j % 2, 0:1]).then_inc(y_link, 1)
                dve.wait_ge(y_link, 3 * m + 6)
                v.scalar_tensor_tensor(ystat[:, j % 2, 2:3], ymv[:, j % 2, 0:1], -1.0, ystat[:, j % 2, 1:2],
                                       ALU.mult, ALU.mult).then_inc(y_norm, 1)

            def tile(l, q, j, h=None):
                n = (l * NQ + q) * QUAD + j
                if h is not None:
                    hn = QUAD * (l * nh + h) + j
                    dve.wait_ge(vhi_ready, hn + 1)
                    v.tensor_tensor(vlo[:, j % 2, :, :].rearrange("p c k -> p (c k)"), psV[:, :],
                                    vhi[:, j % 2, :, :].bitcast(F32).rearrange("p c k -> p (c k)"),
                                    ALU.subtract).then_inc(vlo_ready, 1)
                if j < QUAD - 1:
                    split(l, q, j + 1)
                else:
                    with dve.If(q < NQ - 1):
                        split(l, within(q + 1, 1, NQ - 1), 0)
                if l < LA:
                    if j:
                        back(l, q, j - 1, (l * NQ + q) * QUAD + j - 1)
                    else:
                        with dve.If(q > 0):
                            back(l, quad_before(q), QUAD - 1, (l * NQ + q) * QUAD - 1)
                dve.wait_ge(h_ready, n + 1 + H_CREDIT)
                if LA <= l < L - 1:
                    if l > LA or j >= 2:
                        dve.wait_ge(out_ready, n + 1 + OUT_CREDIT - 2)
                    else:
                        dve.wait_ge(out_ready, n + 1 + OUT_CREDIT - 2)
                v.tensor_tensor(HB[:, j % 2, :], psH[j % 2][:, :], bias[:, l, :], ALU.add).then_inc(hb_ready, 1)
                if l == LA - 1:
                    if j:
                        x1_scale(j - 1, QUAD * q + j - 1)
                    else:
                        with dve.If(q > 0):
                            x1_scale(QUAD - 1, QUAD * q - 1)
                if l == L - 1:
                    dve.wait_ge(hb_ready, n + 1 + HB_CREDIT)
                    wait_alone(dve, x1_loaded[j], 16 * q + 16)
                    with dve.If(q > 0):
                        wait_alone(dve, fin_stored[j], 16 * q)
                    v.tensor_tensor(OUT[:, j, :], HB[:, j % 2, :], XR[:, j, :], ALU.add).then_inc(out_ready, 1)

            for l in range(L):
                if l == L - 1:
                    for j in range(QUAD):
                        dve.wait_ge(out_stored[j], 16 * (l * NQ + 1))
                split(l, 0, 0)
                with dve.If(qh > 0):
                    with dve.Fori(0, qh) as q:
                        for j in range(QUAD):
                            tile(l, q, j)
                for q, h in heavy_quads(dve, qh, nh):
                    for j in range(QUAD):
                        tile(l, q, j, h)
                if l < LA:
                    back(l, NQ - 1, QUAD - 1, (l + 1) * NT - 1)
                if l == LA - 1:
                    x1_scale(QUAD - 1, NT - 1)


_INS = ["x", "src", "dst", "L0_gnn_W_l", "L0_gnn_W_r", "L0_gnn_b", "L0_gnn_ln_g", "L0_gnn_ln_b",
        "L1_gnn_Ws_self", "L1_gnn_Ws_neigh", "L1_gnn_bs"]


def kernel(**inputs):
    import numpy as _np
    import concourse.bacc as _bacc
    from concourse import mybir as _mybir
    from concourse.bass_utils import run_bass_kernel_spmd as _run

    nc = _bacc.Bacc("TRN2", target_bir_lowering=False, num_devices=1)
    arrays, args = {}, []
    for name in _INS:
        a = _np.ascontiguousarray(inputs[name])
        arrays[f"in_{name}"] = a
        args.append(nc.dram_tensor(f"in_{name}", a.shape, _mybir.dt.from_np(a.dtype), kind="ExternalInput").ap())
    shape = inputs["x"].shape
    args.append(nc.dram_tensor("out_0", shape, _mybir.dt.float32, kind="ExternalOutput").ap())
    build_gnn(nc, *args)
    r = _run(nc, [arrays], core_ids=[0])
    return r.results[0]["out_0"]
```

```python
import concourse.bass as bass
from concourse import mybir
from contextlib import ExitStack

F32 = mybir.dt.float32
F32R = mybir.dt.float32r
BF16 = mybir.dt.bfloat16
I32 = mybir.dt.int32
ALU = mybir.AluOpType
ACT = mybir.ActivationFunctionType
AX = mybir.AxisListType
ds = bass.ds

P = 128
LN_EPS = 1e-5


def build_gnn(nc, x, src, dst, W_l, W_r, b0, ln_g, ln_b, Ws_self, Ws_neigh, b1, out):
    N, D = x.shape
    E = src.shape[0]
    KC = D // P
    LA, LB = W_l.shape[0], Ws_self.shape[0]
    L = LA + LB
    QUAD = 4
    NQ = -(-N // (QUAD * P))
    NT = NQ * QUAD
    NP = NT * P
    EP = max(p for p in range(1, P + 1) if E % p == 0)
    EC = E // EP
    CB = max(b for b in range(1, 7) if EC % (2 * b) == 0)
    LG = 8
    EK = -(-E // (P * LG)) * LG
    UNIT = 2 * P
    CH = 2 * (NT + E // UNIT + 1)

    FAR = 1 << 20

    node_tab = nc.dram_tensor("node_tab", (NP, 2), F32, kind="Internal").ap()
    comp_tab = nc.dram_tensor("comp_tab", (P * EK, 2), I32, kind="Internal").ap()
    edge_tab = nc.dram_tensor("edge_tab", (P * CH, 4), F32, kind="Internal").ap()
    H = [nc.dram_tensor(f"h{l}", (NP, D), F32, kind="Internal").ap() for l in range(L)]
    x1_dram = nc.dram_tensor("x1", (NP, D), F32, kind="Internal").ap()
    wp = [nc.dram_tensor(f"wp{l}", (P, 4, KC * D), F32, kind="Internal").ap() for l in range(L)]

    ctx = ExitStack()
    with ctx:
        def sb(name, shape, dt):
            return ctx.enter_context(nc.sbuf_tensor(name, shape, dt))

        def sem(name):
            return ctx.enter_context(nc.semaphore(name))

        banks = [ctx.enter_context(nc.psum_tensor(f"bank{i}", [P, 512], F32)) for i in range(8)]

        diff_i = sb("diff_i", [P, P], I32)
        iota_i = sb("iota_i", [P, CH], I32)
        slot_i = sb("slot_i", [P, P], I32)
        nid_i = sb("nid_i", [P, P], I32)
        diff = sb("diff", [P, P], F32)
        iota = sb("iota", [P, CH], F32)
        slot = sb("slot", [P, P], F32)
        nid = sb("nid", [P, P], F32)
        iota_b = sb("iota_b", [P, P], BF16)
        ident = sb("ident", [P, P], F32)
        below = sb("below", [P, P], F32)
        ones = sb("ones", [P, P], F32)
        zeros = sb("zeros", [P, CH], F32)
        ones_row = sb("ones_row", [P, QUAD * EK], F32)
        eps = sb("eps", [P, 1], F32)

        bias = sb("bias", [P, L, D], F32)
        gain = sb("gain", [P, LA, D], F32)
        shift = sb("shift", [P, LA, D], F32)
        bsum = sb("bsum", [P, LA], F32)

        G = sb("G", [P, QUAD, 2, D], F32)
        wraw = G[:, :, :, :].rearrange("p (a b) c d -> p a (b c d)", a=2) \
            .rearrange("p a (c n) -> p a c n", c=KC)
        wsum = sb("wsum", [P, 2], F32)
        wneg = sb("wneg", [P, 2], F32)
        OUT = sb("OUT", [P, QUAD, D], F32)
        wtmp, wcen = OUT[:, 0:2, :], OUT[:, 2:4, :]
        W = sb("W", [P, 4, KC, D], F32R)

        src_i = sb("src_i", [EP, EC], I32)
        dst_i = sb("dst_i", [EP, EC], I32)
        dhi_i = sb("dhi_i", [EP, EC], I32)
        dlo_i = sb("dlo_i", [EP, EC], I32)
        e_f = sb("e_f", [EP, 8, EC], F32)
        dhi_b = sb("dhi_b", [EP, EC], BF16)
        dlo_b = sb("dlo_b", [EP, EC], BF16)
        self_b = sb("self_b", [EP, EC], BF16)
        ends_i = sb("ends_i", [EP, EC, 2], I32)
        comp_i = sb("comp_i", [EP, EC], I32)
        stage_ci = sb("stage_ci", [EP, 2, CB], I32)
        stage_ce = sb("stage_ce", [EP, 2, CB, 2], I32)
        oh_hi = sb("oh_hi", [EP, 2, CB, NT], BF16)
        oh_lo = sb("oh_lo", [EP, 2, CB, 2, P], BF16)
        Y = sb("Y", [P, QUAD, D], F32)
        nd = Y[0:NT, :, :].rearrange("p a d -> p (a d)")[:, 0:12 * P].rearrange("p (k c) -> p k c", k=12)
        ntab = sb("ntab", [NT, P, 2], F32)
        nsm = sb("nsm", [P, 16], F32)
        qa_t = sb("qa_t", [P, 2, NT], F32)
        qt_i = sb("qt_i", [P, 3, NT], I32)
        qt_f = sb("qt_f", [P, 2, NT], F32)
        work = sb("work", [P, 5, D], F32)
        HB, T1, T2, SQ = work[:, 0:2, :], work[:, 2, :], work[:, 3, :], work[:, 4, :]
        perm_oh = work[:, :, :].rearrange("p a d -> p (a d)")[:, 0:2 * QUAD * (P + 2 * NT)] \
            .rearrange("p (b c k) -> p b c k", b=2, c=QUAD)
        pos_node_i = sb("pos_node_i", [P, NT], I32)
        pos_read_i = sb("pos_read_i", [P, NT], I32)
        pos_f = sb("pos_f", [P, 2, NT], F32)
        own = sb("own", [P, NT], F32)
        ce_i = sb("ce_i", [P, EK, 2], I32)
        ctab = sb("ctab", [P, EK, 4], F32)
        c_i = sb("c_i", [P, 4, EK], I32)
        c_f = sb("c_f", [P, 8, EK], F32)
        cnt_pb = sb("cnt_pb", [P, NT], F32)
        ub = sb("ub", [P, 7, NT], F32)
        ub_i = sb("ub_i", [P, 2, NT], I32)
        bk_eq = sb("bk_eq", [P, QUAD, EK], F32)
        bk_cum = sb("bk_cum", [P, QUAD, EK], F32)
        bk_sum = sb("bk_sum", [P, EK], F32)
        put_i = sb("put_i", [P, EK], I32)
        put_r = sb("put_r", [P, EK, 4], F32)
        stage_pi = sb("stage_pi", [P, LG], I32)
        stage_pr = sb("stage_pr", [P, LG, 4], F32)
        edges_b = sb("edges_b", [P, CH, 4], F32)
        edge_row = edges_b[:, :, 0].bitcast(I32)
        edge_dw = edges_b[:, :, 1:3]
        scal_i = sb("scal_i", [1, 8], I32)
        unit_i = sb("unit_i", [1, 3, NT], I32)
        small_i = sb("small_i", [P, 2], I32)
        stage_c = sb("stage_c", [P, LG, 2], I32)
        looked = sb("looked", [P, LG, 2, 2], F32)

        X = sb("X", [P, QUAD, KC, P], F32)
        XR = sb("XR", [P, QUAD, D], F32)
        xhi = sb("xhi", [P, 2, KC, P], F32R)
        xlo = sb("xlo", [P, 2, KC, P], F32R)
        vhi = sb("vhi", [P, KC, P], F32R)
        vlo = sb("vlo", [P, KC, P], F32R)
        stat = sb("stat", [P, 2, 4], F32)
        mvb = sb("mvb", [P, 2, QUAD, 6], F32)
        mv = sb("mv", [P, 2, QUAD, 2], F32)
        ms = sb("ms", [P, 2, 3, QUAD], F32)
        ymvb = sb("ymvb", [P, 6], F32)
        ymv = sb("ymv", [P, 2, 2], F32)
        ystat = sb("ystat", [P, 2, 4], F32)
        row_in = [X[:, :, :, :].rearrange("p q c k -> p q (c k)"), XR[:, :, :]]
        row_out = G[:, :, :, :].rearrange("p (b a) c d -> p b (a c) d", b=2)
        S = sb("S", [P, QUAD, 2, P], F32R)
        ghi = sb("ghi", [P, 2, D], F32R)
        glo = sb("glo", [P, 2, D], F32R)
        V = sb("V", [P, D], F32)
        XG = sb("XG", [P, 2, D], F32)
        XS = sb("XS", [P, 2, P], F32)
        stage_i = sb("stage_i", [P, QUAD, 2], I32)
        stage_f = sb("stage_f", [P, QUAD, 4], F32)
        xstage_i = sb("xstage_i", [P, 2], I32)
        xstage_f = sb("xstage_f", [P, 4], F32)
        astage = sb("astage", [P, 2 * QUAD], I32)

        edges_loaded = sem("edges_loaded")
        consts_made = sem("consts_made")
        consts_cast = sem("consts_cast")
        dve_chain = sem("dve_chain")
        cnt_built = sem("cnt_built")
        cnt_used = sem("cnt_used")
        cnt_done = sem("cnt_done")
        cnt_link = sem("cnt_link")
        others_counted = sem("others_counted")
        others_based = sem("others_based")
        heavy_counted = sem("heavy_counted")
        heavy_based = sem("heavy_based")
        tab_built = sem("tab_built")
        tab_stored = sem("tab_stored")
        qa_turned = sem("qa_turned")
        qa_split = sem("qa_split")
        perm_link = sem("perm_link")
        perm_built = sem("perm_built")
        perm_used = sem("perm_used")
        perm_done = sem("perm_done")
        pos_ready = sem("pos_ready")
        comp_zeroed = sem("comp_zeroed")
        comp_placed = sem("comp_placed")
        comp_staged = sem("comp_staged")
        comp_stored = [sem(f"comp_stored{i}") for i in range(2)]
        comp_loaded = sem("comp_loaded")
        comp_ready = sem("comp_ready")
        look_staged = sem("look_staged")
        look_loaded = sem("look_loaded")
        look_done = sem("look_done")
        buck_link = sem("buck_link")
        buck_counted = sem("buck_counted")
        buck_based = sem("buck_based")
        buck2_link = sem("buck2_link")
        edge_zeroed = sem("edge_zeroed")
        edge_placed = sem("edge_placed")
        put_staged = sem("put_staged")
        put_stored = sem("put_stored")
        edges_back = sem("edges_back")
        tables_ready = sem("tables_ready")
        vecs_loaded = sem("vecs_loaded")
        vec_link = sem("vec_link")
        wraw_loaded = sem("wraw_loaded")
        wp_stored = sem("wp_stored")
        w_summed = sem("w_summed")
        w_turned = sem("w_turned")
        w_copied = sem("w_copied")
        w_link = sem("w_link")
        w_centred = sem("w_centred")
        w_high = sem("w_high")
        w_low = sem("w_low")
        W_loaded = [sem(f"W_loaded{i}") for i in range(2)]
        a_staged = sem("a_staged")
        a_loaded = [sem(f"a_loaded{j}") for j in range(2 * QUAD)]
        a_stats = sem("a_stats")
        a_link = sem("a_link")
        a_std = sem("a_std")
        a_norm = sem("a_norm")
        a_out = sem("a_out")
        a_stored = [sem(f"a_stored{j}") for j in range(2 * QUAD)]
        y_staged = sem("y_staged")
        y_loaded = [sem(f"y_loaded{j}") for j in range(QUAD)]
        x1_ready = sem("x1_ready")
        x1_stored = [sem(f"x1_stored{j}") for j in range(QUAD)]
        residual_added = sem("residual_added")
        y_summed = sem("y_summed")
        y_rstd = sem("y_rstd")
        y_stats = sem("y_stats")
        y_std = sem("y_std")
        y_norm = sem("y_norm")
        x_loaded = [sem(f"x_loaded{j}") for j in range(QUAD)]
        x1_loaded = [sem(f"x1_loaded{j}") for j in range(QUAD)]
        out_stored = [sem(f"out_stored{j}") for j in range(QUAD)]
        xt_ready = sem("xt_ready")
        xhi_ready = sem("xhi_ready")
        xlo_ready = sem("xlo_ready")
        xr_ready = sem("xr_ready")
        h_ready = sem("h_ready")
        hb_ready = sem("hb_ready")
        sq_ready = sem("sq_ready")
        std_ready = sem("std_ready")
        rstd_ready = sem("rstd_ready")
        h_scaled = sem("h_scaled")
        h_shifted = sem("h_shifted")
        out_ready = sem("out_ready")
        g_staged = sem("g_staged")
        g_loaded = [sem(f"g_loaded{j}") for j in range(QUAD)]
        s_built = sem("s_built")
        ghi_ready = sem("ghi_ready")
        glo_ready = sem("glo_ready")
        g_summed = sem("g_summed")
        v_ready = sem("v_ready")
        v_turned = sem("v_turned")
        vhi_ready = sem("vhi_ready")
        vlo_ready = sem("vlo_ready")
        xg_staged = sem("xg_staged")
        xg_loaded = sem("xg_loaded")
        xs_built = sem("xs_built")
        xg_used = sem("xg_used")
        fin_staged = sem("fin_staged")
        fin_stored = [sem(f"fin_stored{j}") for j in range(QUAD)]

        waits_passed = {e: sem(f"waits_passed_{e}") for e in ("SP", "Pool", "DVE")}

        H_CREDIT = QUAD
        OUT_CREDIT = QUAD
        HB_CREDIT = 2
        RES_CREDIT = QUAD
        XR_CREDIT = QUAD
        LAG = QUAD
        S_CREDIT = QUAD
        G_CREDIT = QUAD

        psT = [banks[0], banks[1]]
        psH = [banks[2], banks[3]]
        psV, psVT = banks[4], banks[5]

        block = ctx.enter_context(nc.Block())

        def wait_alone(eng, name, value):
            eng.wait_ge(name, value)
            eng.sem_inc(waits_passed[eng.engine.name], 1)

        def within(value, low, high):
            return nc.s_assert_within(value, low, high,
                                      skip_runtime_bounds_check_because="the tables and loops keep it there")

        def heavy_quads(eng, qh, nh):
            with eng.Fori(0, nh) as h:
                yield within(qh + h, 0, NQ - 1), h

        def quad_before(q):
            return within(q - 1, 0, NQ - 2)

        def first_heavy(eng):
            return (eng.value_load(scal_i[0:1, 0:1], min_val=0, max_val=NQ - 1),
                    eng.value_load(scal_i[0:1, 5:6], min_val=1, max_val=NQ))

        @block.sync
        def _(sp):
            sp.dma_start(src_i[:, :], src.rearrange("(p c) -> p c", p=EP)).then_inc(edges_loaded, 16)
            sp.dma_start(dst_i[:, :], dst.rearrange("(p c) -> p c", p=EP)).then_inc(edges_loaded, 16)
            for l in range(LA):
                sp.dma_start(bias[:, l, :], b0[l, :].partition_broadcast(P)).then_inc(vecs_loaded, 16)
                sp.dma_start(gain[:, l, :], ln_g[l, :].partition_broadcast(P)).then_inc(vecs_loaded, 16)
                sp.dma_start(shift[:, l, :], ln_b[l, :].partition_broadcast(P)).then_inc(vecs_loaded, 16)
            for l in range(LB):
                sp.dma_start(bias[:, LA + l, :], b1[l, :].partition_broadcast(P)).then_inc(vecs_loaded, 16)
            sp.wait_ge(consts_made, 10)
            sp.dma_start(comp_tab.rearrange("(p c) t -> p (c t)", p=P), zeros[:, 0:2 * EK].bitcast(I32)).then_inc(comp_zeroed, 16)
            for k in range(4):
                sp.dma_start(edge_tab.rearrange("(p c) t -> p (c t)", p=P)[:, k * CH:(k + 1) * CH], zeros[:, :]).then_inc(edge_zeroed, 16)
            sp.wait_ge(tab_built, 1)
            sp.dma_start(node_tab.rearrange("(p c) t -> p (c t)", p=NT),
                         ntab[:, :, :].rearrange("p c t -> p (c t)")).then_inc(tab_stored, 16)
            for l in range(L):
                wa, wb = (W_l[l], W_r[l]) if l < LA else (Ws_neigh[l - LA], Ws_self[l - LA])
                if l:
                    sp.wait_ge(w_low, 8 * l)
                sp.dma_start(wraw[:, 0, :, :], wa.rearrange("(c p) n -> p c n", p=P)).then_inc(wraw_loaded, 16)
                sp.dma_start(wraw[:, 1, :, :], wb.rearrange("(c p) n -> p c n", p=P)).then_inc(wraw_loaded, 16)
                sp.wait_ge(w_low, 8 * (l + 1))
                sp.dma_start(wp[l], W[:, :, :, :].bitcast(F32).rearrange("p m c n -> p m (c n)")).then_inc(wp_stored, 16)
                sp.wait_ge(wp_stored, 16 * (l + 1))

            with sp.Fori(0, NQ // 2) as i:
                for b in range(2):
                    for j in range(QUAD):
                        t = QUAD * (2 * i + b) + j
                        wait_alone(sp, a_out, t + 1)
                        sp.dma_start(H[0][ds(t * P, P), :], row_out[:, b, j, :]).then_inc(a_stored[QUAD * b + j], 16)
            for k in range(2 * QUAD):
                sp.wait_ge(a_stored[k], 16 * NQ // 2)

            def load_tile(l, q, j):
                n = (l * NQ + q) * QUAD + j
                wait_alone(sp, h_ready, n + 1)
                if l < LA:
                    wait_alone(sp, xr_ready, n + 1)
                sp.dma_start(X[:, j, :, :], H[l][ds((QUAD * q + j) * P, P), :]
                             .rearrange("p (c k) -> p c k", c=KC)).then_inc(x_loaded[j], 16)

            def load_x1(q, j):
                wait_alone(sp, out_ready, ((L - 1) * NQ + q) * QUAD + j + 1)
                sp.dma_start(XR[:, j, :], x1_dram[ds((QUAD * q + j) * P, P), :]).then_inc(x1_loaded[j], 16)

            def store_tile(l, q, j):
                n = (l * NQ + q) * QUAD + j
                wait_alone(sp, out_ready, n + 1 + OUT_CREDIT)
                sp.dma_start(H[l + 1][ds((QUAD * q + j) * P, P), :], OUT[:, j, :]).then_inc(out_stored[j], 16)

            def store_x1(q, j):
                wait_alone(sp, x1_ready, QUAD * q + j + 1 + LAG)
                sp.dma_start(x1_dram[ds((QUAD * q + j) * P, P), :], Y[:, j, :]).then_inc(x1_stored[j], 16)

            def store(l, q, j):
                if l == LA - 1:
                    store_x1(q, j)
                store_tile(l, q, j)

            for l in range(L):
                if l:
                    sp.wait_ge(h_ready, l * NT + H_CREDIT)
                sp.dma_start(W[:, 0:2, :, :].bitcast(F32).rearrange("p m c n -> p m (c n)"), wp[l][:, 0:2, :]).then_inc(W_loaded[0], 16)
                sp.dma_start(W[:, 2:4, :, :].bitcast(F32).rearrange("p m c n -> p m (c n)"), wp[l][:, 2:4, :]).then_inc(W_loaded[1], 16)
                for j in range(QUAD):
                    if l:
                        sp.wait_ge(out_stored[j], 16 * (l * NQ + 1))
                for j in range(QUAD):
                    load_tile(l, 0, j)
                    if l == L - 1:
                        load_x1(0, j)
                for j in range(QUAD):
                    load_tile(l, 1, j)
                    if l == L - 1:
                        load_x1(1, j)
                    elif j == QUAD - 1:
                        store(l, 0, 0)
                with sp.Fori(1, NQ - 1) as q:
                    for j in range(QUAD):
                        load_tile(l, q + 1, j)
                        if l == L - 1:
                            load_x1(q + 1, j)
                        elif j < QUAD - 1:
                            store(l, within(q - 1, 0, NQ - 3), j + 1)
                        else:
                            store(l, q, 0)
                if l < L - 1:
                    for q, j in [(NQ - 2, j) for j in range(1, QUAD)] + [(NQ - 1, j) for j in range(QUAD)]:
                        store(l, q, j)
                if l == LA - 1:
                    for j in range(QUAD):
                        sp.wait_ge(x1_stored[j], 16 * (NQ + 1))

        @block.gpsimd
        def _(pool):
            nc.gpsimd.iota(diff_i[:, :], [[1, P]], 0, -1).then_inc(consts_made, 1)
            nc.gpsimd.iota(iota_i[:, :], [[1, CH]], 0, 0).then_inc(consts_made, 1)
            nc.gpsimd.iota(slot_i[:, :], [[P, P]], 0, 1).then_inc(consts_made, 1)
            nc.gpsimd.iota(nid_i[:, :], [[1, P]], 0, P).then_inc(consts_made, 1)
            nc.gpsimd.memset(ones[:, :], 1.0).then_inc(consts_made, 1)
            nc.gpsimd.memset(zeros[:, :], 0.0).then_inc(consts_made, 1)
            nc.gpsimd.memset(ones_row[:, :], 1.0).then_inc(consts_made, 1)
            nc.gpsimd.memset(eps[:, :], LN_EPS).then_inc(consts_made, 1)
            nc.gpsimd.memset(ctab[:, :, :], 0.0).then_inc(consts_made, 1)
            nc.gpsimd.memset(cnt_pb[:, :], 0.0).then_inc(consts_made, 1)

            pool.wait_ge(comp_placed, 1)
            pool.wait_ge(comp_zeroed, 16)

            def compact(g, b, free):
                if free is not None:
                    wait_alone(pool, comp_stored[b], 16 * CB * free)
                nc.gpsimd.tensor_copy(stage_ci[:, b, :], comp_i[:, ds(g * CB, CB)]).then_inc(comp_staged, 1)
                nc.gpsimd.tensor_copy(stage_ce[:, b, :, :], ends_i[:, ds(g * CB, CB), :]).then_inc(comp_staged, 1)
                wait_alone(pool, comp_staged, 2 * g + 2)
                for c in range(CB):
                    pool.indirect_dma_start(
                        out=comp_tab, out_offset=bass.IndirectOffsetOnAxis(ap=stage_ci[:, b, c:c + 1], axis=0),
                        in_=stage_ce[:, b, c, :], in_offset=None, bounds_check=P * EK - 1,
                        oob_is_err=False).then_inc(comp_stored[b], 16)

            for b in range(2):
                compact(b, b, None)
            with pool.Fori(1, EC // (2 * CB)) as i:
                for b in range(2):
                    compact(2 * i + b, b, i)
            for b in range(2):
                pool.wait_ge(comp_stored[b], 16 * EC // 2)
            pool.dma_start(ce_i[:, :, :].rearrange("p c t -> p (c t)"),
                           comp_tab.rearrange("(p c) t -> p (c t)", p=P)).then_inc(comp_loaded, 16)

            pool.wait_ge(comp_loaded, 16)
            pool.wait_ge(comp_ready, 1)
            pool.wait_ge(tab_stored, 16)
            chunk_groups = pool.value_load(scal_i[0:1, 4:5], min_val=1, max_val=EK // LG)
            with pool.Fori(0, chunk_groups) as g:
                nc.gpsimd.tensor_copy(stage_c[:, :, :], ce_i[:, ds(LG * g, LG), :]).then_inc(look_staged, 1)
                wait_alone(pool, look_staged, g + 1)
                for c in range(LG):
                    for e in range(2):
                        pool.indirect_dma_start(
                            out=looked[:, c, e, :], out_offset=None, in_=node_tab,
                            in_offset=bass.IndirectOffsetOnAxis(ap=stage_c[:, c, e:e + 1], axis=0)).then_inc(look_loaded, 16)
                wait_alone(pool, look_loaded, 32 * LG * (g + 1))
                nc.gpsimd.tensor_copy(ctab[:, ds(LG * g, LG), :].rearrange("p a t -> p (a t)"),
                                      looked[:, :, :, :].rearrange("p c e t -> p (c e t)")).then_inc(look_done, 1)
                wait_alone(pool, look_done, g + 1)

            def gather_x(i, b, free):
                for j in range(QUAD):
                    t = QUAD * (2 * i + b) + j
                    if free:
                        wait_alone(pool, a_out, t + 1 - 2 * QUAD)
                    nc.gpsimd.tensor_copy(astage[:, QUAD * b + j:QUAD * b + j + 1], pos_read_i[:, ds(t, 1)]).then_inc(a_staged, 1)
                    wait_alone(pool, a_staged, t + 1)
                    pool.indirect_dma_start(
                        out=row_in[b][:, j, :], out_offset=None, in_=x,
                        in_offset=bass.IndirectOffsetOnAxis(ap=astage[:, QUAD * b + j:QUAD * b + j + 1], axis=0)
                        ).then_inc(a_loaded[QUAD * b + j], 16)

            pool.wait_ge(pos_ready, 1)
            for b in range(2):
                gather_x(0, b, False)
            with pool.Fori(1, NQ // 2) as i:
                for b in range(2):
                    gather_x(i, b, True)

            pool.wait_ge(edge_placed, 1)
            pool.wait_ge(edge_zeroed, 64)
            with pool.Fori(0, chunk_groups) as g:
                nc.gpsimd.tensor_copy(stage_pi[:, :], put_i[:, ds(LG * g, LG)]).then_inc(put_staged, 1)
                nc.gpsimd.tensor_copy(stage_pr[:, :, 0].bitcast(I32), put_r[:, ds(LG * g, LG), 0].bitcast(I32)).then_inc(put_staged, 1)
                nc.gpsimd.tensor_copy(stage_pr[:, :, 1:4], put_r[:, ds(LG * g, LG), 1:4]).then_inc(put_staged, 1)
                wait_alone(pool, put_staged, 3 * g + 3)
                for c in range(LG):
                    pool.indirect_dma_start(
                        out=edge_tab, out_offset=bass.IndirectOffsetOnAxis(ap=stage_pi[:, c:c + 1], axis=0),
                        in_=stage_pr[:, c, :], in_offset=None, bounds_check=P * CH - 1,
                        oob_is_err=False).then_inc(put_stored, 16)
                wait_alone(pool, put_stored, 16 * LG * (g + 1))
            pool.dma_start(edges_b[:, :, :].rearrange("p c t -> p (c t)"),
                           edge_tab.rearrange("(p c) t -> p (c t)", p=P)).then_inc(edges_back, 16)
            pool.wait_ge(edges_back, 16)
            pool.wait_ge(tables_ready, 1)
            qh, nh = first_heavy(pool)
            extra_all = pool.value_load(scal_i[0:1, 2:3], min_val=0, max_val=E // UNIT + 1)

            def gather_neighbours(l, q, h, j):
                t = QUAD * q + j
                hn = QUAD * (l * nh + h) + j
                unit = pool.value_load(unit_i[0:1, 0, ds(t, 1)], min_val=0, max_val=CH // 2 - 1)
                more = pool.value_load(unit_i[0:1, 1, ds(t, 1)], min_val=0, max_val=E // UNIT)
                extra = pool.value_load(unit_i[0:1, 2, ds(t, 1)], min_val=0, max_val=CH // 2)
                wait_alone(pool, glo_ready, hn + 1)
                wait_alone(pool, g_summed, hn + 1)
                nc.gpsimd.tensor_copy(stage_i[:, j, :], edge_row[:, ds(2 * unit, 2)]).then_inc(g_staged, 1)
                nc.gpsimd.tensor_copy(stage_f[:, j, :].rearrange("p (a t) -> p a t", a=2),
                                      edge_dw[:, ds(2 * unit, 2), :]).then_inc(g_staged, 1)
                wait_alone(pool, g_staged, 2 * hn + 2)
                for c in range(2):
                    pool.indirect_dma_start(
                        out=G[:, j, c, :], out_offset=None, in_=H[l],
                        in_offset=bass.IndirectOffsetOnAxis(ap=stage_i[:, j, c:c + 1], axis=0)).then_inc(g_loaded[j], 16)
                for c in range(2):
                    last = nc.gpsimd.tensor_scalar(S[:, j, c, :], iota[:, 0:P], stage_f[:, j, 2 * c:2 * c + 1],
                                                   None, ALU.is_equal)
                last.then_inc(s_built, 1)
                with pool.If(more > 0):
                    with pool.Fori(0, more) as k:
                        e = l * extra_all + extra + k
                        u = within(unit + k + 1, 1, CH // 2 - 1)
                        wait_alone(pool, xg_used, e + 1)
                        nc.gpsimd.tensor_copy(xstage_i[:, :], edge_row[:, ds(2 * u, 2)]).then_inc(xg_staged, 1)
                        nc.gpsimd.tensor_copy(xstage_f[:, :].rearrange("p (a t) -> p a t", a=2),
                                              edge_dw[:, ds(2 * u, 2), :]).then_inc(xg_staged, 1)
                        wait_alone(pool, xg_staged, 2 * e + 2)
                        for c in range(2):
                            pool.indirect_dma_start(
                                out=XG[:, c, :], out_offset=None, in_=H[l],
                                in_offset=bass.IndirectOffsetOnAxis(ap=xstage_i[:, c:c + 1], axis=0)).then_inc(xg_loaded, 16)
                        nc.gpsimd.tensor_scalar(XS[:, 0, :], iota[:, 0:P], xstage_f[:, 0:1],
                                                xstage_f[:, 1:2], ALU.is_equal, ALU.mult)
                        nc.gpsimd.tensor_scalar(XS[:, 1, :], iota[:, 0:P], xstage_f[:, 2:3],
                                                xstage_f[:, 3:4], ALU.is_equal, ALU.mult).then_inc(xs_built, 1)

            def gather_x_again(q, j):
                n = QUAD * q + j
                wait_alone(pool, out_ready, (LA - 1) * NT + n + 1)
                wait_alone(pool, x1_stored[j], 16 * q + 16)
                nc.gpsimd.tensor_copy(astage[:, j:j + 1], pos_read_i[:, ds(n, 1)]).then_inc(y_staged, 1)
                wait_alone(pool, y_staged, n + 1 + LAG)
                pool.indirect_dma_start(
                    out=Y[:, j, :], out_offset=None, in_=x,
                    in_offset=bass.IndirectOffsetOnAxis(ap=astage[:, j:j + 1], axis=0)).then_inc(y_loaded[j], 16)

            def gather_x_lagged(q, j):
                if j >= 2:
                    gather_x_again(q, j - 2)
                else:
                    with pool.If(q > 0):
                        gather_x_again(quad_before(q), QUAD + j - 2)

            pool.sem_inc(y_staged, LAG)
            for j in range(QUAD):
                pool.sem_inc(x1_stored[j], 16)
            pool.sem_inc(fin_staged, QUAD)

            def scatter_out(q, j):
                n = QUAD * q + j
                if not isinstance(q, int):
                    n = within(n, 0, NT - 1)
                wait_alone(pool, out_ready, (L - 1) * NT + n + 1 + OUT_CREDIT)
                nc.gpsimd.tensor_copy(astage[:, j:j + 1], pos_node_i[:, ds(n, 1)]).then_inc(fin_staged, 1)
                wait_alone(pool, fin_staged, n + 1 + QUAD)
                pool.indirect_dma_start(
                    out=out, out_offset=bass.IndirectOffsetOnAxis(ap=astage[:, j:j + 1], axis=0),
                    in_=OUT[:, j, :], in_offset=None, bounds_check=N - 1, oob_is_err=False).then_inc(fin_stored[j], 16)

            for l in range(L):
                for j in range(QUAD):
                    if l == 0:
                        pool.wait_ge(a_stored[j], 16 * NQ // 2)
                        pool.wait_ge(a_stored[QUAD + j], 16 * NQ // 2)
                    else:
                        pool.wait_ge(out_stored[j], 16 * (l * NQ + 1))
                if l < L - 1:
                    if l == LA - 1:
                        with pool.If(qh > 0):
                            with pool.Fori(0, qh) as q:
                                for j in range(QUAD):
                                    gather_x_lagged(q, j)
                    for q, h in heavy_quads(pool, qh, nh):
                        for j in range(QUAD):
                            gather_neighbours(l, q, h, j)
                            if l == LA - 1:
                                gather_x_lagged(q, j)
                    if l == LA - 1:
                        for j in (QUAD - 2, QUAD - 1):
                            gather_x_again(NQ - 1, j)
                else:
                    with pool.If(qh > 1):
                        with pool.Fori(1, qh) as q:
                            for j in range(QUAD):
                                scatter_out(quad_before(q), j)
                    for q, h in heavy_quads(pool, qh, nh):
                        for j in range(QUAD):
                            gather_neighbours(l, q, h, j)
                        with pool.If(q > 0):
                            for j in range(QUAD):
                                scatter_out(quad_before(q), j)
                    for j in range(QUAD):
                        scatter_out(NQ - 1, j)
            for j in range(QUAD):
                pool.wait_ge(fin_stored[j], 16 * NQ)

        @block.tensor
        def _(pe):
            mm = nc.tensor.matmul
            pe.wait_ge(consts_cast, 1)

            pe.wait_ge(others_counted, 1)
            mm(banks[7][0:EP, 0:1], below[0:EP, 0:EP], e_f[:, 5, EC - 1:EC], start=True, stop=True)
            mm(banks[7][:, 2:3], ones[0:EP, :], e_f[:, 5, EC - 1:EC], start=True, stop=True).then_inc(others_based, 1)

            cnt = banks[5][0:NT, 0:2 * P]
            mm(cnt, zeros[:, 0:NT], zeros[:, 0:2 * P], start=True, stop=False, skip_group_check=True)
            with pe.Fori(0, EC // (2 * CB)) as i:
                for b in range(2):
                    pe.wait_ge(cnt_built, 2 * i + b + 1)
                    for c in range(CB):
                        last = mm(cnt, oh_hi[:, b, c, :], oh_lo[:, b, c, :, :].rearrange("p a k -> p (a k)"),
                                  start=False, stop=False, skip_group_check=True)
                    last.then_inc(cnt_used, 1)
            mm(cnt, zeros[:, 0:NT], zeros[:, 0:2 * P], start=False, stop=True, skip_group_check=True).then_inc(cnt_done, 1)

            pe.wait_ge(heavy_counted, 1)
            mm(banks[6][0:NT, 0:1], below[0:NT, 0:NT], nd[:, 6, P - 1:P], start=True, stop=True)
            mm(banks[6][:, 2:3], ones[0:NT, :], nd[:, 6, P - 1:P], start=True, stop=True).then_inc(heavy_based, 1)

            pe.wait_ge(tab_built, 1)
            mm(banks[0][:, 0:NT], nd[:, 8, :], ident[0:NT, 0:NT], start=True, stop=True)
            mm(banks[0][:, P:P + NT], nd[:, 3, :], ident[0:NT, 0:NT], start=True, stop=True).then_inc(qa_turned, 1)

            perm = banks[1][:, 0:2 * NT]
            mm(perm, zeros[:, 0:P], zeros[:, 0:2 * NT], start=True, stop=False, skip_group_check=True)
            with pe.Fori(0, NQ // 2) as i:
                for b in range(2):
                    pe.wait_ge(perm_built, 2 * i + b + 1)
                    for c in range(QUAD):
                        last = mm(perm, perm_oh[:, b, c, 0:P], perm_oh[:, b, c, P:], start=False, stop=False,
                                  skip_group_check=True)
                    last.then_inc(perm_used, 1)
            mm(perm, zeros[:, 0:P], zeros[:, 0:2 * NT], start=False, stop=True, skip_group_check=True).then_inc(perm_done, 1)

            for l in range(L):
                for k in range(8):
                    m, c = k // KC, k % KC
                    if l < LA:
                        if k == 0:
                            pe.wait_ge(w_summed, l + 1)
                        if 8 * l + k >= 2:
                            pe.wait_ge(w_copied, 8 * l + k - 1)
                        for nb in range(KC):
                            last = nc.tensor.transpose(banks[6 + k % 2][:, nb * P:(nb + 1) * P],
                                                       wraw[:, 1 - m, nb, c * P:(c + 1) * P], ident[:, :])
                        last.then_inc(w_turned, 1)

            pe.wait_ge(buck_counted, 1)
            mm(banks[4][:, 0:NT], below[:, :], cnt_pb[:, :], start=True, stop=True)
            mm(banks[4][:, P:P + NT], ones[:, :], cnt_pb[:, :], start=True, stop=True).then_inc(buck_based, 1)

            pe.wait_ge(tables_ready, 1)
            qh, nh = first_heavy(pe)
            extra_all = pe.value_load(scal_i[0:1, 2:3], min_val=0, max_val=E // UNIT + 1)
            pe.sem_inc(h_ready, H_CREDIT)
            pe.sem_inc(g_summed, S_CREDIT)
            pe.sem_inc(xg_used, 1)

            def turn(l, q, j):
                n = (l * NQ + q) * QUAD + j
                pe.wait_ge(x_loaded[j], 16 * (l * NQ + q) + 16)
                pe.wait_ge(xlo_ready, n + 1)
                for c in range(KC):
                    last = nc.tensor.transpose(psT[j % 2][:, c * P:(c + 1) * P], X[:, j, c, :], ident[:, :])
                last.then_inc(xt_ready, 1)

            def sum_neighbours(l, q, h, j):
                t = QUAD * q + j
                hn = QUAD * (l * nh + h) + j
                more = pe.value_load(unit_i[0:1, 1, ds(t, 1)], min_val=0, max_val=E // UNIT)
                extra = pe.value_load(unit_i[0:1, 2, ds(t, 1)], min_val=0, max_val=CH // 2)
                pe.wait_ge(glo_ready, hn + 1 + G_CREDIT)
                pe.wait_ge(s_built, hn + 1)
                for c, part in ((0, ghi), (0, glo), (1, ghi)):
                    mm(psV[:, :], S[:, j, c, :], part[:, c, :], start=c == 0 and part is ghi, stop=False,
                       skip_group_check=True)
                with pe.If(more > 0):
                    with pe.Fori(0, more) as k:
                        e = l * extra_all + extra + k
                        pe.wait_ge(xg_loaded, 32 * e + 32)
                        pe.wait_ge(xs_built, e + 1)
                        for c in range(2):
                            last = mm(psV[:, :], XS[:, c, :], XG[:, c, :], start=False, stop=False, skip_group_check=True)
                        last.then_inc(xg_used, 1)
                mm(psV[:, :], S[:, j, 1, :], glo[:, 1, :], start=False, stop=True,
                   skip_group_check=True).then_inc(g_summed, 1)

            def turn_v(l, h, j):
                pe.wait_ge(v_ready, QUAD * (l * nh + h) + j + 1)
                for c in range(KC):
                    last = nc.tensor.transpose(psVT[:, c * P:(c + 1) * P], V[:, c * P:(c + 1) * P], ident[:, :])
                last.then_inc(v_turned, 1)

            def products(h, hi, lo, w, chunks, first, final):
                last = None
                for c in chunks:
                    mm(h, hi[:, c, :], W[:, w, c, :], start=first and c == 0, stop=False, skip_group_check=True)
                    mm(h, hi[:, c, :], W[:, w + 1, c, :], start=False, stop=False, skip_group_check=True)
                    last = mm(h, lo[:, c, :], W[:, w, c, :], start=False, stop=final and c == KC - 1,
                              skip_group_check=True)
                return last

            def tile(l, q, j):
                n = (l * NQ + q) * QUAD + j
                if j < QUAD - 1:
                    turn(l, q, j + 1)
                else:
                    with pe.If(q < NQ - 1):
                        turn(l, within(q + 1, 1, NQ - 1), 0)
                pe.wait_ge(xlo_ready, n + 1 + 2)
                pe.wait_ge(hb_ready, n + 1)
                products(psH[j % 2][:, :], xhi[:, j % 2], xlo[:, j % 2], 0, range(KC), True, True).then_inc(h_ready, 1)

            def heavy_tile(l, q, h, j):
                n = (l * NQ + q) * QUAD + j
                acc = psH[j % 2][:, :]
                pe.wait_ge(xlo_ready, n + 1 + 2)
                pe.wait_ge(hb_ready, n + 1)
                products(acc, xhi[:, j % 2], xlo[:, j % 2], 0, range(KC), True, False)
                if j < QUAD - 1:
                    turn(l, q, j + 1)
                else:
                    with pe.If(q < NQ - 1):
                        turn(l, within(q + 1, 1, NQ - 1), 0)
                pe.wait_ge(W_loaded[1], 16 * (l + 1))
                pe.wait_ge(vlo_ready, QUAD * (l * nh + h) + j + 1)
                products(acc, vhi, vlo, 2, range(KC // 2), False, False)
                if j < QUAD - 1:
                    sum_neighbours(l, q, h, j + 1)
                else:
                    with pe.If(q < NQ - 1):
                        sum_neighbours(l, within(q + 1, 1, NQ - 1), h + 1, 0)
                products(acc, vhi, vlo, 2, range(KC // 2, KC), False, True).then_inc(h_ready, 1)
                if j < QUAD - 1:
                    turn_v(l, h, j + 1)
                else:
                    with pe.If(q < NQ - 1):
                        turn_v(l, h + 1, 0)

            for l in range(L):
                turn(l, 0, 0)
                pe.wait_ge(W_loaded[0], 16 * (l + 1))
                with pe.If(qh > 0):
                    with pe.Fori(0, qh) as q:
                        for j in range(QUAD):
                            tile(l, q, j)
                sum_neighbours(l, qh, 0, 0)
                turn_v(l, 0, 0)
                for q, h in heavy_quads(pe, qh, nh):
                    for j in range(QUAD):
                        heavy_tile(l, q, h, j)

        @block.scalar
        def _(act):
            for l in range(L):
                for k in range(8):
                    m, c = k // KC, k % KC
                    i = 8 * l + k
                    if l < LA:
                        act.wait_ge(w_turned, i + 1)
                        if i >= 2:
                            act.wait_ge(w_low, i - 1)
                        nc.scalar.activation(wtmp[:, k % 2, :], banks[6 + k % 2][:, :], ACT.Copy,
                                             accum_out=wsum[:, k % 2:k % 2 + 1]).then_inc(w_copied, 1)
                        act.wait_ge(w_centred, i + 1)
                        if l and k == 0:
                            act.wait_ge(wp_stored, 16 * l)
                        nc.scalar.copy(W[:, 2 * m, c, :], wcen[:, k % 2, :]).then_inc(w_high, 1)
                    else:
                        if k == 0:
                            act.wait_ge(w_summed, l + 1)
                            act.wait_ge(wp_stored, 16 * l)
                        nc.scalar.copy(W[:, 2 * m, c, :], wraw[:, 1 - m, c, :]).then_inc(w_high, 1)

            def normalise(i, b, free):
                s = 2 * i + b
                act.wait_ge(a_stats, s + 1)
                nc.scalar.activation(ms[:, b, 0, :], mv[:, b, :, 1], ACT.Sqrt, bias=eps[:, 0:1]).then_inc(a_std, 1)
                act.wait_ge(a_norm, s + 1)
                for j in range(QUAD):
                    if free:
                        act.wait_ge(a_stored[QUAD * b + j], 16 * i)
                    nc.scalar.activation(row_out[:, b, j, :], row_in[b][:, j, :], ACT.Relu, bias=ms[:, b, 2, j:j + 1],
                                         scale=ms[:, b, 1, j:j + 1]).then_inc(a_out, 1)

            for b in range(2):
                normalise(0, b, False)
            with act.Fori(1, NQ // 2) as i:
                for b in range(2):
                    normalise(i, b, True)

            act.wait_ge(tables_ready, 1)
            qh, nh = first_heavy(act)
            act.sem_inc(out_ready, OUT_CREDIT)
            act.sem_inc(xr_ready, XR_CREDIT)
            act.sem_inc(y_std, LAG)
            for j in range(QUAD):
                act.sem_inc(out_stored[j], 16)

            def split(l, q, j):
                n = (l * NQ + q) * QUAD + j
                act.wait_ge(xt_ready, n + 1)
                act.wait_ge(h_ready, n + 1 + H_CREDIT - 2)
                nc.scalar.copy(xhi[:, j % 2, :, :].rearrange("p c k -> p (c k)"), psT[j % 2][:, :]).then_inc(xhi_ready, 1)
                if l < LA:
                    if l < LA - 1:
                        act.wait_ge(out_ready, n + 1)
                    else:
                        act.wait_ge(residual_added, n - l * NT + 1)
                    nc.scalar.copy(XR[:, j, :], X[:, j, :, :].rearrange("p c k -> p (c k)")).then_inc(xr_ready, 1)

            def weigh(l, q, h, j):
                hq = l * nh + h
                act.wait_ge(g_loaded[j], 32 * hq + 32)
                act.wait_ge(s_built, QUAD * hq + j + 1)
                act.wait_ge(g_summed, QUAD * hq + j + S_CREDIT)
                for c in range(2):
                    nc.scalar.activation(ghi[:, c, :], G[:, j, c, :], ACT.Copy,
                                         scale=stage_f[:, j, 2 * c + 1:2 * c + 2]).then_inc(ghi_ready, 1)

            def normalise_x1(l, q, j):
                act.wait_ge(y_norm, QUAD * q + j + 1 + LAG)
                act.wait_ge(out_stored[j], 16 * ((LA - 1) * NQ + q) + 16)
                nc.scalar.activation(OUT[:, j, :], Y[:, j, :], ACT.Relu, bias=ystat[:, j % 2, 2:3],
                                     scale=ystat[:, j % 2, 1:2]).then_inc(out_ready, 1)

            def x1_root(l, q, j):
                act.wait_ge(y_stats, QUAD * q + j + 1 + LAG)
                nc.scalar.activation(ystat[:, j % 2, 0:1], ymv[:, j % 2, 1:2], ACT.Sqrt,
                                     bias=eps[:, 0:1]).then_inc(y_std, 1)

            def back(l, q, j):
                n = (l * NQ + q) * QUAD + j
                act.wait_ge(hb_ready, n + 1 + HB_CREDIT)
                if l < LA:
                    nc.scalar.activation(SQ, HB[:, j % 2, :], ACT.Square,
                                         accum_out=stat[:, j % 2, 0:1]).then_inc(sq_ready, 1)
                    act.wait_ge(sq_ready, n + 1)
                    nc.scalar.activation(stat[:, j % 2, 1:2], stat[:, j % 2, 0:1], ACT.Sqrt,
                                         bias=eps[:, 0:1], scale=1.0 / D).then_inc(std_ready, 1)
                elif l < L - 1:
                    act.wait_ge(out_stored[j], 16 * (l * NQ + q) + 16)
                    nc.scalar.activation(OUT[:, j, :], HB[:, j % 2, :], ACT.Relu).then_inc(out_ready, 1)

            def split_next(l, q, j):
                if j < QUAD - 1:
                    split(l, q, j + 1)
                else:
                    with act.If(q < NQ - 1):
                        split(l, within(q + 1, 1, NQ - 1), 0)

            def lagged(lag, l, q, j, do):
                if j >= lag:
                    do(l, q, j - lag)
                else:
                    with act.If(q > 0):
                        do(l, quad_before(q), QUAD + j - lag)

            def tile(l, q, j, h=None):
                if h is None:
                    split_next(l, q, j)
                else:
                    act.wait_ge(v_turned, QUAD * (l * nh + h) + j + 1)
                    nc.scalar.copy(vhi[:, :, :].rearrange("p c k -> p (c k)"), psVT[:, :]).then_inc(vhi_ready, 1)
                    if j < QUAD - 1:
                        weigh(l, q, h, j + 1)
                    else:
                        with act.If(q < NQ - 1):
                            weigh(l, within(q + 1, 1, NQ - 1), h + 1, 0)
                if l < L - 1:
                    lagged(1, l, q, j, back)
                if h is not None:
                    split_next(l, q, j)
                if l == LA - 1:
                    lagged(4, l, q, j, normalise_x1)
                    lagged(3, l, q, j, x1_root)

            for l in range(L):
                if l == LA - 1:
                    act.wait_ge(out_ready, l * NT + OUT_CREDIT)
                split(l, 0, 0)
                with act.If(qh > 0):
                    with act.Fori(0, qh) as q:
                        for j in range(QUAD):
                            tile(l, q, j)
                weigh(l, qh, 0, 0)
                for q, h in heavy_quads(act, qh, nh):
                    for j in range(QUAD):
                        tile(l, q, j, h)
                if l < L - 1:
                    back(l, NQ - 1, QUAD - 1)
                if l == LA - 1:
                    for j in range(QUAD):
                        normalise_x1(l, NQ - 1, j)
                        if j < QUAD - 1:
                            x1_root(l, NQ - 1, j + 1)

        @block.vector
        def _(dve):
            v = nc.vector
            chain = [0]

            def link(ins):
                chain[0] += 1
                ins.then_inc(dve_chain, 1)
                dve.wait_ge(dve_chain, chain[0])

            def bc_in(ap, n):
                return ap.unsqueeze(2).broadcast_to([ap.shape[0], ap.shape[1], n])

            def bc_out(ap, n):
                return ap.unsqueeze(1).broadcast_to([ap.shape[0], n, ap.shape[1]])

            dve.wait_ge(consts_made, 10)
            v.tensor_copy(iota[:, :], iota_i[:, :])
            v.tensor_copy(slot[:, :], slot_i[:, :])
            v.tensor_copy(nid[:, :], nid_i[:, :])
            v.tensor_copy(iota_b[:, :], iota_i[:, 0:P])
            link(v.tensor_copy(diff[:, :], diff_i[:, :]))
            v.tensor_scalar(ident[:, :], diff[:, :], 0.0, None, ALU.is_equal)
            v.tensor_scalar(below[:, :], diff[:, :], 0.0, None, ALU.is_gt).then_inc(consts_cast, 1)

            sf, df, dhif, dlof, ns, cum, cp, tmp = (e_f[:, k, :] for k in range(8))
            dve.wait_ge(edges_loaded, 32)
            v.tensor_copy(sf, src_i[:, :])
            v.tensor_copy(df, dst_i[:, :])
            v.tensor_scalar(dhi_i[:, :], dst_i[:, :], 7, None, ALU.arith_shift_right)
            link(v.tensor_scalar(dlo_i[:, :], dst_i[:, :], P - 1, None, ALU.bitwise_and))
            v.tensor_copy(dhi_b[:, :], dhi_i[:, :])
            v.tensor_copy(dlo_b[:, :], dlo_i[:, :])
            v.tensor_tensor(self_b[:, :], sf, df, ALU.is_equal)
            v.tensor_copy(ends_i[:, :, 0], src_i[:, :])
            v.tensor_copy(ends_i[:, :, 1], dst_i[:, :])
            link(v.tensor_tensor(ns, sf, df, ALU.not_equal))
            v.tensor_tensor_scan(cum, ones[0:EP, 0:EC], ns, 0.0, ALU.mult, ALU.add).then_inc(others_counted, 1)
            dve.wait_ge(others_based, 1)
            link(v.tensor_copy(nsm[0:EP, 4:5], banks[7][0:EP, 0:1]))
            link(v.tensor_copy(nsm[:, 5:6], banks[7][:, 2:3]))
            link(v.tensor_scalar(cp, cum, nsm[0:EP, 4:5], -1.0, ALU.add, ALU.add))
            link(v.tensor_tensor(cp, cp, ns, ALU.mult))
            link(v.tensor_copy(dhi_i[:, :], cp))
            link(v.tensor_scalar(dlo_i[:, :], dhi_i[:, :], P - 1, None, ALU.bitwise_and))
            link(v.tensor_scalar(dhi_i[:, :], dhi_i[:, :], 7, None, ALU.arith_shift_right))
            v.tensor_copy(dlof, dlo_i[:, :])
            link(v.tensor_copy(dhif, dhi_i[:, :]))
            link(v.scalar_tensor_tensor(cp, dlof, float(EK), dhif, ALU.mult, ALU.add))
            link(v.scalar_tensor_tensor(cp, cp, -float(FAR), ns, ALU.add, ALU.mult))
            v.tensor_scalar(comp_i[:, :], cp, float(FAR), None, ALU.add).then_inc(comp_placed, 1)
            link(v.tensor_scalar(nsm[0:1, 6:7], nsm[0:1, 5:6], float(P * LG - 1), None, ALU.add))
            link(v.tensor_copy(scal_i[0:1, 3:4], nsm[0:1, 6:7]))
            link(v.tensor_scalar(scal_i[0:1, 3:4], scal_i[0:1, 3:4], 10, None, ALU.arith_shift_right))
            v.tensor_scalar(scal_i[0:1, 4:5], scal_i[0:1, 3:4], 1.0, None, ALU.max).then_inc(comp_ready, 1)

            def count_step(i, b, static):
                if not static:
                    dve.wait_ge(cnt_used, i - 1)
                cols = ds(i * CB, CB)
                v.tensor_tensor(oh_hi[:, b, :, :], bc_out(iota_b[0:EP, 0:NT], CB), bc_in(dhi_b[:, cols], NT), ALU.is_equal)
                v.tensor_tensor(oh_lo[:, b, :, 0, :], bc_out(iota_b[0:EP, :], CB), bc_in(dlo_b[:, cols], P),
                                ALU.is_equal).then_inc(cnt_link, 1)
                dve.wait_ge(cnt_link, i + 1)
                v.tensor_tensor(oh_lo[:, b, :, 1, :], oh_lo[:, b, :, 0, :], bc_in(self_b[:, cols], P),
                                ALU.mult).then_inc(cnt_built, 1)

            for b in range(2):
                count_step(b, b, True)
            with dve.Fori(1, EC // (2 * CB)) as i:
                for b in range(2):
                    count_step(2 * i + b, b, False)

            cntf, loops, inv, owna, heavy, other, hcum, hexc, pos, none, okn, t0 = (nd[:, k, :] for k in range(12))
            dve.wait_ge(cnt_done, 1)
            v.tensor_copy(loops, banks[5][0:NT, P:2 * P])
            link(v.tensor_copy(cntf, banks[5][0:NT, 0:P]))
            link(v.tensor_scalar(t0, cntf, 1.0, None, ALU.max))
            v.tensor_scalar(none, cntf, 0.5, None, ALU.is_lt)
            v.tensor_tensor(other, cntf, loops, ALU.not_equal)
            v.tensor_scalar(okn, nid[0:NT, :], float(N), None, ALU.is_lt)
            link(v.reciprocal(inv, t0))
            link(v.tensor_tensor(heavy, none, other, ALU.max))
            link(v.tensor_tensor(heavy, heavy, okn, ALU.mult))
            link(v.tensor_tensor(t0, loops, inv, ALU.mult))
            link(v.tensor_scalar(t0, t0, -1.0, None, ALU.add))
            link(v.tensor_tensor(owna, t0, heavy, ALU.mult))
            v.tensor_tensor_scan(hcum, ones[0:NT, :], heavy, 0.0, ALU.mult, ALU.add).then_inc(heavy_counted, 1)
            dve.wait_ge(heavy_based, 1)
            link(v.tensor_copy(nsm[0:NT, 0:1], banks[6][0:NT, 0:1]))
            link(v.tensor_copy(nsm[:, 1:2], banks[6][:, 2:3]))
            link(v.tensor_tensor(hexc, hcum, heavy, ALU.subtract))
            link(v.tensor_scalar(hexc, hexc, nsm[0:NT, 0:1], None, ALU.add))
            link(v.tensor_scalar(nsm[:, 2:3], nsm[:, 1:2], -1.0, float(NP), ALU.mult, ALU.add))
            link(v.tensor_tensor(pos, nid[0:NT, :], hexc, ALU.subtract))
            link(v.tensor_scalar(t0, hexc, nsm[0:NT, 2:3], None, ALU.add))
            link(v.tensor_tensor(t0, t0, pos, ALU.subtract))
            link(v.tensor_tensor(t0, t0, heavy, ALU.mult))
            link(v.tensor_tensor(pos, pos, t0, ALU.add))
            v.tensor_copy(ntab[:, :, 0], pos)
            v.tensor_copy(ntab[:, :, 1], inv).then_inc(tab_built, 1)
            link(v.tensor_copy(small_i[:, 0:1], nsm[:, 2:3]))
            link(v.tensor_scalar(small_i[:, 1:2], small_i[:, 0:1], 9, None, ALU.arith_shift_right))
            link(v.tensor_scalar(nsm[:, 3:4], small_i[:, 1:2], float(NQ - 1), None, ALU.min))
            link(v.tensor_scalar(nsm[:, 9:10], nsm[:, 3:4], float(QUAD), None, ALU.mult))
            link(v.tensor_copy(scal_i[0:1, 0:1], nsm[0:1, 3:4]))
            link(v.tensor_scalar(nsm[:, 11:12], nsm[:, 3:4], -1.0, float(NQ), ALU.mult, ALU.add))
            link(v.tensor_copy(scal_i[0:1, 5:6], nsm[0:1, 11:12]))

            dve.wait_ge(qa_turned, 1)
            v.tensor_copy(qa_t[:, 1, :], banks[0][:, P:P + NT])
            v.tensor_copy(qt_i[:, 0, :], banks[0][:, 0:NT])
            link(v.tensor_copy(qa_t[:, 0, :], banks[0][:, 0:NT]))
            v.tensor_scalar(qt_i[:, 1, :], qt_i[:, 0, :], 7, None, ALU.arith_shift_right)
            link(v.tensor_scalar(qt_i[:, 2, :], qt_i[:, 0, :], P - 1, None, ALU.bitwise_and))
            v.tensor_copy(qt_f[:, 0, :], qt_i[:, 1, :])
            link(v.tensor_copy(qt_f[:, 1, :], qt_i[:, 2, :]))

            def perm_step(i, b, static):
                if not static:
                    dve.wait_ge(perm_used, i - 1)
                cols = ds(i * QUAD, QUAD)
                oh = perm_oh[:, b, :, :]
                v.tensor_tensor(oh[:, :, 0:P], bc_out(iota[:, 0:P], QUAD), bc_in(qt_f[:, 1, cols], P), ALU.is_equal)
                v.tensor_tensor(oh[:, :, P:P + NT], bc_out(iota[:, 0:NT], QUAD), bc_in(qt_f[:, 0, cols], NT),
                                ALU.is_equal).then_inc(perm_link, 1)
                dve.wait_ge(perm_link, 2 * i + 1)
                v.tensor_tensor(oh[:, :, P + NT:], oh[:, :, P:P + NT], bc_in(qa_t[:, 1, cols], NT),
                                ALU.mult).then_inc(perm_link, 1)
                dve.wait_ge(perm_link, 2 * i + 2)
                v.tensor_tensor(oh[:, :, P:P + NT], oh[:, :, P:P + NT], bc_in(slot[:, cols], NT),
                                ALU.mult).then_inc(perm_built, 1)

            for b in range(2):
                perm_step(b, b, True)
            with dve.Fori(1, NQ // 2) as i:
                for b in range(2):
                    perm_step(2 * i + b, b, False)
            dve.wait_ge(perm_done, 1)
            v.tensor_copy(own[:, :], banks[1][:, NT:2 * NT])
            v.tensor_copy(pos_node_i[:, :], banks[1][:, 0:NT])
            link(v.tensor_copy(pos_f[:, 0, :], banks[1][:, 0:NT]))
            v.tensor_scalar(pos_read_i[:, :], pos_f[:, 0, :], float(N - 1), None, ALU.min).then_inc(pos_ready, 1)

            dve.wait_ge(vecs_loaded, 16 * (3 * LA + LB))
            link(v.tensor_reduce(bsum[:, :], bias[:, 0:LA, :], AX.X, ALU.add))
            link(v.tensor_scalar(bsum[:, :], bsum[:, :], -1.0 / D, None, ALU.mult))
            for l in range(LA):
                link(v.tensor_scalar(bias[:, l, :], bias[:, l, :], bsum[:, l:l + 1], None, ALU.add))

            for l in range(L):
                dve.wait_ge(wraw_loaded, 32 * (l + 1))
                v.tensor_tensor(wraw[:, 1, :, :].rearrange("p c n -> p (c n)"),
                                wraw[:, 1, :, :].rearrange("p c n -> p (c n)"),
                                wraw[:, 0, :, :].rearrange("p c n -> p (c n)"), ALU.add).then_inc(w_summed, 1)
                for k in range(8):
                    m, c = k // KC, k % KC
                    i = 8 * l + k
                    if l < LA:
                        dve.wait_ge(w_copied, i + 1)
                        link(v.tensor_scalar(wneg[:, k % 2:k % 2 + 1], wsum[:, k % 2:k % 2 + 1], -1.0 / D, None, ALU.mult))
                        v.tensor_scalar(wcen[:, k % 2, :], wtmp[:, k % 2, :], wneg[:, k % 2:k % 2 + 1], None,
                                        ALU.add).then_inc(w_centred, 1)
                        full = wcen[:, k % 2, :]
                    else:
                        full = wraw[:, 1 - m, c, :]
                    dve.wait_ge(w_high, i + 1)
                    v.tensor_tensor(W[:, 2 * m + 1, c, :], full, W[:, 2 * m, c, :].bitcast(F32),
                                    ALU.subtract).then_inc(w_low, 1)

            def stats(i, b, free):
                s = 2 * i + b
                if free:
                    dve.wait_ge(a_out, QUAD * (s - 1))
                for j in range(QUAD):
                    dve.wait_ge(a_loaded[QUAD * b + j], 16 * i + 16)
                    v.bn_stats(mvb[:, b, j, :], row_in[b][:, j, :]).then_inc(a_link, 1)
                wait_alone(dve, a_link, (QUAD + 1) * s + QUAD)
                for j in range(QUAD):
                    last = v.bn_aggr(mv[:, b, j, :], mvb[:, b, j, :])
                last.then_inc(a_stats, 1)
                dve.wait_ge(a_std, s + 1)
                v.reciprocal(ms[:, b, 1, :], ms[:, b, 0, :]).then_inc(a_link, 1)
                dve.wait_ge(a_link, (QUAD + 1) * s + QUAD + 1)
                v.scalar_tensor_tensor(ms[:, b, 2, :], mv[:, b, :, 0], -1.0, ms[:, b, 1, :], ALU.mult,
                                       ALU.mult).then_inc(a_norm, 1)

            for b in range(2):
                stats(0, b, False)
            with dve.Fori(1, NQ // 2) as i:
                for b in range(2):
                    stats(i, b, True)

            qh0, nh0 = first_heavy(dve)
            groups = dve.value_load(scal_i[0:1, 4:5], min_val=1, max_val=EK // LG)
            dve.wait_ge(look_done, groups)
            c_bk, c_lo, c_pl, c_ph, c_pos, c_ok, c_put, _c = (c_f[:, k, :] for k in range(8))
            link(v.tensor_scalar(c_ok, slot[:, 0:EK], nsm[:, 5:6], None, ALU.is_lt))
            link(v.tensor_copy(c_i[:, 0, :], ctab[:, :, 2]))
            link(v.tensor_scalar(c_i[:, 1, :], c_i[:, 0, :], 7, None, ALU.arith_shift_right))
            link(v.tensor_scalar(c_i[:, 2, :], c_i[:, 0, :], P - 1, None, ALU.bitwise_and))
            link(v.tensor_copy(c_lo, c_i[:, 2, :]))
            link(v.tensor_copy(c_bk, c_i[:, 1, :]))
            link(v.tensor_scalar(c_bk, c_bk, 1.0, None, ALU.add))
            link(v.tensor_tensor(c_bk, c_bk, c_ok, ALU.mult))
            link(v.tensor_scalar(c_bk, c_bk, -1.0, None, ALU.add))
            def in_buckets(k):
                b = within(k + qh0, 0, NQ - 1)
                v.tensor_tensor(bk_eq[:, :, :], bc_in(iota[:, ds(QUAD * b, QUAD)], EK), bc_out(c_bk, QUAD),
                                ALU.is_equal).then_inc(buck_link, 1)
                return ds(QUAD * b, QUAD), ds(QUAD * b, 1)

            with dve.Fori(0, nh0) as k:
                four, _ = in_buckets(k)
                dve.wait_ge(buck_link, 2 * k + 1)
                v.tensor_reduce(cnt_pb[:, four], bk_eq[:, :, :], AX.X, ALU.add).then_inc(buck_link, 1)
                dve.wait_ge(buck_link, 2 * k + 2)
            v.tensor_scalar(ub[:, 5, :], cnt_pb[:, :], 0.0, None, ALU.add).then_inc(buck_counted, 1)
            dve.wait_ge(buck_based, 1)
            tot, units, ucum, base, isheavy, _spare, before = (ub[:, k, :] for k in range(7))
            link(v.tensor_copy(tot, banks[4][:, P:P + NT]))
            link(v.tensor_scalar(ub[:, 5, :], tot, float(UNIT - 1), None, ALU.add))
            link(v.tensor_copy(ub_i[:, 0, :], ub[:, 5, :]))
            link(v.tensor_scalar(ub_i[:, 0, :], ub_i[:, 0, :], 8, None, ALU.arith_shift_right))
            link(v.tensor_copy(units, ub_i[:, 0, :]))
            link(v.tensor_scalar(units, units, 1.0, None, ALU.max))
            link(v.tensor_scalar(isheavy, iota[:, 0:NT], nsm[:, 9:10], None, ALU.is_ge))
            link(v.tensor_tensor(units, units, isheavy, ALU.mult))
            link(v.tensor_tensor_scan(ucum, ones[:, 0:NT], units, 0.0, ALU.mult, ALU.add))
            link(v.tensor_tensor(ucum, ucum, units, ALU.subtract))
            link(v.tensor_scalar(base, ucum, float(UNIT), None, ALU.mult))
            link(v.tensor_tensor(base, base, banks[4][:, 0:NT], ALU.add))
            link(v.tensor_tensor_scan(before, ones[:, 0:NT], cnt_pb[:, :], 0.0, ALU.mult, ALU.add))
            link(v.tensor_tensor(before, before, cnt_pb[:, :], ALU.subtract))
            link(v.tensor_tensor(base, base, before, ALU.subtract))
            link(v.memset(c_pos, 0.0))
            heavy_counts = dve.value_load(scal_i[0:1, 5:6], min_val=1, max_val=NQ)

            def in_buckets_again(k):
                b = within(k + qh0, 0, NQ - 1)
                v.tensor_tensor(bk_eq[:, :, :], bc_in(iota[:, ds(QUAD * b, QUAD)], EK), bc_out(c_bk, QUAD),
                                ALU.is_equal).then_inc(buck2_link, 1)
                return ds(QUAD * b, QUAD), ds(QUAD * b, 1)

            with dve.Fori(0, heavy_counts) as k:
                four, one = in_buckets_again(k)
                dve.wait_ge(buck2_link, 6 * k + 1)
                v.tensor_tensor_scan(bk_cum[:, :, :].rearrange("p b c -> p (b c)"), ones_row[:, :],
                                     bk_eq[:, :, :].rearrange("p b c -> p (b c)"), before[:, one],
                                     ALU.mult, ALU.add).then_inc(buck2_link, 1)
                dve.wait_ge(buck2_link, 6 * k + 2)
                v.tensor_tensor(bk_cum[:, :, :], bk_cum[:, :, :], bc_in(base[:, four], EK), ALU.add).then_inc(buck2_link, 1)
                dve.wait_ge(buck2_link, 6 * k + 3)
                v.tensor_tensor(bk_cum[:, :, :], bk_cum[:, :, :], bk_eq[:, :, :], ALU.mult).then_inc(buck2_link, 1)
                dve.wait_ge(buck2_link, 6 * k + 4)
                v.tensor_reduce(bk_sum[:, :], bk_cum[:, :, :].rearrange("p b c -> p c b"), AX.X, ALU.add).then_inc(buck2_link, 1)
                dve.wait_ge(buck2_link, 6 * k + 5)
                v.tensor_tensor(c_pos, c_pos, bk_sum[:, :], ALU.add).then_inc(buck2_link, 1)
                dve.wait_ge(buck2_link, 6 * k + 6)
            link(v.tensor_scalar(c_pos, c_pos, -1.0, 0.0, ALU.add, ALU.max))
            link(v.tensor_copy(c_i[:, 0, :], c_pos))
            v.tensor_scalar(c_i[:, 1, :], c_i[:, 0, :], 7, None, ALU.arith_shift_right)
            link(v.tensor_scalar(c_i[:, 2, :], c_i[:, 0, :], P - 1, None, ALU.bitwise_and))
            v.tensor_copy(c_ph, c_i[:, 1, :])
            link(v.tensor_copy(c_pl, c_i[:, 2, :]))
            link(v.scalar_tensor_tensor(c_put, c_pl, float(CH), c_ph, ALU.mult, ALU.add))
            link(v.scalar_tensor_tensor(c_put, c_put, -float(FAR), c_ok, ALU.add, ALU.mult))
            v.tensor_scalar(put_i[:, :], c_put, float(FAR), None, ALU.add)
            v.tensor_copy(put_r[:, :, 0].bitcast(I32), ctab[:, :, 0])
            v.tensor_copy(put_r[:, :, 1], c_lo)
            v.tensor_copy(put_r[:, :, 2], ctab[:, :, 3])
            v.memset(put_r[:, :, 3], 0.0).then_inc(edge_placed, 1)
            link(v.tensor_copy(unit_i[0:1, 0, :], ucum[0:1, :]))
            link(v.tensor_scalar(unit_i[0:1, 1, :], units[0:1, :], -1.0, 0.0, ALU.add, ALU.max))
            link(v.tensor_tensor(tot[0:1, :], ucum[0:1, :], iota[0:1, 0:NT], ALU.subtract))
            link(v.tensor_scalar(tot[0:1, :], tot[0:1, :], nsm[0:1, 9:10], 0.0, ALU.add, ALU.max))
            link(v.tensor_copy(unit_i[0:1, 2, :], tot[0:1, :]))
            link(v.tensor_tensor(nsm[0:1, 10:11], tot[0:1, NT - 1:NT], units[0:1, NT - 1:NT], ALU.add))
            link(v.tensor_scalar(nsm[0:1, 10:11], nsm[0:1, 10:11], -1.0, None, ALU.add))
            v.tensor_copy(scal_i[0:1, 2:3], nsm[0:1, 10:11]).then_inc(tables_ready, 1)
            dve.wait_ge(tables_ready, 1)
            qh, nh = first_heavy(dve)
            dve.sem_inc(xlo_ready, 2)
            dve.sem_inc(hb_ready, HB_CREDIT)
            dve.sem_inc(glo_ready, G_CREDIT)
            dve.sem_inc(residual_added, RES_CREDIT)
            for late in (rstd_ready, h_scaled, h_shifted, x1_ready, y_summed, y_stats, y_rstd, y_norm):
                dve.sem_inc(late, LAG)

            def split(l, q, j):
                n = (l * NQ + q) * QUAD + j
                dve.wait_ge(xhi_ready, n + 1)
                v.tensor_tensor(xlo[:, j % 2, :, :].rearrange("p c k -> p (c k)"), psT[j % 2][:, :],
                                xhi[:, j % 2, :, :].bitcast(F32).rearrange("p c k -> p (c k)"),
                                ALU.subtract).then_inc(xlo_ready, 1)

            def reciprocal_std(l, q, j):
                dve.wait_ge(std_ready, (l * NQ + q) * QUAD + j + 1)
                v.reciprocal(stat[:, j % 2, 2:3], stat[:, j % 2, 1:2]).then_inc(rstd_ready, 1)

            def scale(l, q, j):
                dve.wait_ge(rstd_ready, (l * NQ + q) * QUAD + j + 1 + LAG)
                v.scalar_tensor_tensor(T1, HB[:, j % 2, :], stat[:, j % 2, 2:3], gain[:, l, :],
                                       ALU.mult, ALU.mult).then_inc(h_scaled, 1)

            def shift_up(l, q, j):
                dve.wait_ge(h_scaled, (l * NQ + q) * QUAD + j + 1 + LAG)
                v.tensor_tensor(T2, T1, shift[:, l, :], ALU.add).then_inc(h_shifted, 1)

            def residual(l, q, j):
                n = (l * NQ + q) * QUAD + j
                dve.wait_ge(h_shifted, n + 1 + LAG)
                dve.wait_ge(xr_ready, n + 1 + XR_CREDIT)
                if l < LA - 1:
                    dve.wait_ge(out_stored[j], 16 * (l * NQ + q) + 16)
                    v.scalar_tensor_tensor(OUT[:, j, :], T2, 0.0, XR[:, j, :], ALU.max, ALU.add).then_inc(out_ready, 1)
                else:
                    v.scalar_tensor_tensor(T1, T2, 0.0, XR[:, j, :], ALU.max, ALU.add).then_inc(residual_added, 1)

            def add_x(l, q, j):
                dve.wait_ge(residual_added, QUAD * q + j + 1 + RES_CREDIT)
                wait_alone(dve, y_loaded[j], 16 * q + 16)
                v.tensor_tensor(Y[:, j, :], Y[:, j, :], T1, ALU.add).then_inc(x1_ready, 1)

            def x1_sums(l, q, j):
                dve.wait_ge(x1_ready, QUAD * q + j + 1 + LAG)
                v.bn_stats(ymvb[:, :], Y[:, j, :]).then_inc(y_summed, 1)

            def x1_stats(l, q, j):
                wait_alone(dve, y_summed, QUAD * q + j + 1 + LAG)
                v.bn_aggr(ymv[:, j % 2, :], ymvb[:, :]).then_inc(y_stats, 1)

            def x1_reciprocal_std(l, q, j):
                dve.wait_ge(y_std, QUAD * q + j + 1 + LAG)
                v.reciprocal(ystat[:, j % 2, 1:2], ystat[:, j % 2, 0:1]).then_inc(y_rstd, 1)

            def x1_scale(l, q, j):
                dve.wait_ge(y_rstd, QUAD * q + j + 1 + LAG)
                v.scalar_tensor_tensor(ystat[:, j % 2, 2:3], ymv[:, j % 2, 0:1], -1.0, ystat[:, j % 2, 1:2],
                                       ALU.mult, ALU.mult).then_inc(y_norm, 1)

            def add_bias(l, q, j):
                n = (l * NQ + q) * QUAD + j
                dve.wait_ge(h_ready, n + 1 + H_CREDIT)
                if LA <= l < L - 1:
                    dve.wait_ge(out_ready, n + 1 + OUT_CREDIT - 2)
                v.tensor_tensor(HB[:, j % 2, :], psH[j % 2][:, :], bias[:, l, :], ALU.add).then_inc(hb_ready, 1)

            def add_x1(l, q, j):
                dve.wait_ge(hb_ready, (l * NQ + q) * QUAD + j + 1 + HB_CREDIT)
                wait_alone(dve, x1_loaded[j], 16 * q + 16)
                with dve.If(q > 0):
                    wait_alone(dve, fin_stored[j], 16 * q)
                v.tensor_tensor(OUT[:, j, :], HB[:, j % 2, :], XR[:, j, :], ALU.add).then_inc(out_ready, 1)

            def split_next(l, q, j):
                if j < QUAD - 1:
                    split(l, q, j + 1)
                else:
                    with dve.If(q < NQ - 1):
                        split(l, within(q + 1, 1, NQ - 1), 0)

            def weigh(l, h, j):
                for c in range(2):
                    dve.wait_ge(ghi_ready, 2 * (QUAD * (l * nh + h) + j) + c + 1)
                    last = v.scalar_tensor_tensor(glo[:, c, :], G[:, j, c, :], stage_f[:, j, 2 * c + 1:2 * c + 2],
                                                  ghi[:, c, :].bitcast(F32), ALU.mult, ALU.subtract)
                last.then_inc(glo_ready, 1)

            def complete(l, q, h, j):
                dve.wait_ge(g_summed, QUAD * (l * nh + h) + j + 1 + S_CREDIT)
                dve.wait_ge(x_loaded[j], 16 * (l * NQ + q) + 16)
                v.scalar_tensor_tensor(V[:, :], X[:, j, :, :].rearrange("p c k -> p (c k)"), own[:, ds(QUAD * q + j, 1)],
                                       psV[:, :], ALU.mult, ALU.add).then_inc(v_ready, 1)


            def lagged(lag, l, q, j, *steps):
                if j >= lag:
                    for do in steps:
                        do(l, q, j - lag)
                else:
                    with dve.If(q > 0):
                        for do in steps:
                            do(l, quad_before(q), QUAD + j - lag)

            def split_v(l, h, j):
                dve.wait_ge(vhi_ready, QUAD * (l * nh + h) + j + 1)
                v.tensor_tensor(vlo[:, :, :].rearrange("p c k -> p (c k)"), psVT[:, :],
                                vhi[:, :, :].bitcast(F32).rearrange("p c k -> p (c k)"),
                                ALU.subtract).then_inc(vlo_ready, 1)

            def tile(l, q, j, h=None):
                if l < L - 1:
                    lagged(1, l, q, j, add_bias)
                if h is not None:
                    split_v(l, h, j)
                    if j < QUAD - 1:
                        weigh(l, h, j + 1)
                    else:
                        with dve.If(q < NQ - 1):
                            weigh(l, h + 1, 0)
                if l < LA:
                    lagged(2, l, q, j, scale)
                if l == LA - 1:
                    lagged(3, l, q, j, x1_stats)
                split_next(l, q, j)
                if l < LA:
                    lagged(1, l, q, j, reciprocal_std)
                    lagged(2, l, q, j, shift_up, residual)
                if l == LA - 1:
                    lagged(3, l, q, j, x1_reciprocal_std)
                    lagged(2, l, q, j, add_x)
                    lagged(3, l, q, j, x1_scale)
                if h is not None:
                    if j < QUAD - 1:
                        complete(l, q, h, j + 1)
                    else:
                        with dve.If(q < NQ - 1):
                            complete(l, within(q + 1, 1, NQ - 1), h + 1, 0)
                if l == LA - 1:
                    lagged(2, l, q, j, x1_sums)
                if l == L - 1:
                    add_bias(l, q, j)
                    add_x1(l, q, j)

            def last_tiles(l):
                q, j = NQ - 1, QUAD - 1
                if l < L - 1:
                    add_bias(l, q, j)
                if l < LA:
                    for k in (j - 1, j):
                        scale(l, q, k)
                        if l == LA - 1:
                            x1_stats(l, q, k - 1)
                        if k == j - 1:
                            reciprocal_std(l, q, j)
                        shift_up(l, q, k)
                        residual(l, q, k)
                        if l == LA - 1:
                            x1_reciprocal_std(l, q, k - 1)
                            add_x(l, q, k)
                            x1_scale(l, q, k - 1)
                            x1_sums(l, q, k)
                if l == LA - 1:
                    x1_stats(l, q, j)
                    x1_reciprocal_std(l, q, j)
                    x1_scale(l, q, j)

            for l in range(L):
                if l == L - 1:
                    for j in range(QUAD):
                        dve.wait_ge(out_stored[j], 16 * (l * NQ + 1))
                split(l, 0, 0)
                with dve.If(qh > 0):
                    with dve.Fori(0, qh) as q:
                        for j in range(QUAD):
                            tile(l, q, j)
                weigh(l, 0, 0)
                complete(l, qh, 0, 0)
                for q, h in heavy_quads(dve, qh, nh):
                    for j in range(QUAD):
                        tile(l, q, j, h)
                last_tiles(l)


_INS = ["x", "src", "dst", "L0_gnn_W_l", "L0_gnn_W_r", "L0_gnn_b", "L0_gnn_ln_g", "L0_gnn_ln_b",
        "L1_gnn_Ws_self", "L1_gnn_Ws_neigh", "L1_gnn_bs"]


def kernel(**inputs):
    import numpy as _np
    import concourse.bacc as _bacc
    from concourse import mybir as _mybir
    from concourse.bass_utils import run_bass_kernel_spmd as _run

    nc = _bacc.Bacc("TRN2", target_bir_lowering=False, num_devices=1)
    arrays, args = {}, []
    for name in _INS:
        a = _np.ascontiguousarray(inputs[name])
        arrays[f"in_{name}"] = a
        args.append(nc.dram_tensor(f"in_{name}", a.shape, _mybir.dt.from_np(a.dtype), kind="ExternalInput").ap())
    shape = inputs["x"].shape
    args.append(nc.dram_tensor("out_0", shape, _mybir.dt.float32, kind="ExternalOutput").ap())
    build_gnn(nc, *args)
    r = _run(nc, [arrays], core_ids=[0])
    return r.results[0]["out_0"]
```
